# Optimizing a Trainium2 kernel written in Bass

```python
import numpy as np
import jax
import jax.numpy as jnp

def _softmax(x, axis=-1):
    return jax.nn.softmax(x, axis=axis)

def _gelu(x):
    return jax.nn.gelu(x, approximate=True)

def _silu(x):
    return jax.nn.silu(x)

def _sigmoid(x):
    return jax.nn.sigmoid(x)

def _layernorm(x, axis=-1, eps=1e-05):
    m = jnp.mean(x, axis=axis, keepdims=True)
    v = jnp.var(x, axis=axis, keepdims=True)
    return (x - m) / jnp.sqrt(v + eps)

def _scatter_add(tgt, idx, src, axis=0):
    return tgt.at[idx].add(src)

def _segment_sum(src, seg, n):
    return jax.ops.segment_sum(src, seg, n)
kernel_name = 'mk_flamingo_gated_d4_seqx_r8_15da02'

def setup_inputs(seed: int=0):
    np.random.seed(seed)
    _w = jnp.asarray

    def _rec_inputs():
        import jax
        import jax.numpy as jnp
        _rk = jax.random.key(seed)
        x = -7.109e-05 + 0.9999 * jax.random.normal(jax.random.fold_in(_rk, 1), (4, 256, 256), jnp.float32)
        _lenS = 256 - jax.random.randint(jax.random.fold_in(_rk, 7), (4,), 0, max(1, 256 // 4) + 1, jnp.int32)
        _lenS2 = 256 - jax.random.randint(jax.random.fold_in(_rk, 8), (4,), 0, max(1, 256 // 4) + 1, jnp.int32)
        _ctx_512P = jax.random.normal(jax.random.fold_in(_rk, 11), (4, 16, 64), jnp.float32)
        _ctx_512c = jax.random.dirichlet(jax.random.fold_in(_rk, 511), 0.3 * jnp.ones((16,), jnp.float32), (4, 256))
        _ctx_512t = jnp.einsum('bsk,bkd->bsd', _ctx_512c, _ctx_512P)
        _ctx_512t = _ctx_512t * jax.lax.rsqrt(jnp.mean(jnp.square(_ctx_512t)) + 1e-12) * 0.953939
        ctx_512 = 2.81802e-05 + 1.00001 * (_ctx_512t + 0.3 * jax.random.normal(jax.random.fold_in(_rk, 611), (4, 256, 64), jnp.float32))
        _g = jax.random.normal(jax.random.fold_in(_rk, 9001), (2, 4), jnp.float32)
        _g = jnp.sign(_g) * jnp.maximum(jnp.abs(_g), 1.0) + (_g == 0) * 1.0
        g_xattn = _g[0]
        g_ffn = _g[1]
        return (x, ctx_512, g_xattn, g_ffn)
    x, ctx_512, g_xattn, g_ffn = _rec_inputs()

    def _L0_xattn_setup():
        import jax, jax.numpy as jnp
        import numpy as np
        EPS = 1e-06
        IMAGE_DIMS = 256
        key = jax.random.key(seed)
        k1, k2, k3 = jax.random.split(key, 3)
        B, I, J, D = (16, 256, 256, 64)
        p = jax.random.normal(k1, (B, I, J), dtype=jnp.float32)
        k_v = jax.random.normal(k2, (B, J, D), dtype=jnp.float32)
        W_k = jax.random.normal(k3, (D, D), dtype=jnp.float32) * (1.0 / np.sqrt(D))
        b_k = jnp.zeros((D,), dtype=jnp.float32)
        ln_gamma = jnp.ones((J,), dtype=jnp.float32)
        ln_beta = jnp.zeros((J,), dtype=jnp.float32)
        return {'p': p, 'k_v': k_v, 'W_k': W_k, 'b_k': b_k, 'ln_gamma': ln_gamma, 'ln_beta': ln_beta}
    _L0_xattn_all = _L0_xattn_setup()
    _L0_xattn_in = {k: v for k, v in _L0_xattn_all.items() if k in ('W_k', 'b_k', 'ln_gamma', 'ln_beta')}
    del _L0_xattn_all

    def _L0_ffn_setup():
        import jax, jax.numpy as jnp
        import numpy as np
        B, T, D = (2, 128, 256)
        E, F, K = (64, 64, 4)
        S, HS = (2, 64 * 4)
        key = jax.random.key(seed)
        ks = jax.random.split(key, 9)
        s = 0.02
        f32 = jnp.float32
        return {'x': jax.random.normal(ks[0], (B, T, D), f32), 'router_w': jax.random.normal(ks[1], (D, E), f32) * s, 'router_bias': jnp.zeros((E,), f32), 'wg': jax.random.normal(ks[2], (E, D, F), f32) * s, 'wu': jax.random.normal(ks[3], (E, D, F), f32) * s, 'wd': jax.random.normal(ks[4], (E, F, D), f32) * s, 'swg': jax.random.normal(ks[5], (S, D, HS), f32) * s, 'swu': jax.random.normal(ks[6], (S, D, HS), f32) * s, 'swd': jax.random.normal(ks[7], (S, HS, D), f32) * s}
    _L0_ffn_all = _L0_ffn_setup()
    _L0_ffn_in = {k: v for k, v in _L0_ffn_all.items() if k in ('router_w', 'router_bias', 'wg', 'wu', 'wd', 'swg', 'swu', 'swd')}
    del _L0_ffn_all

    def _L1_xattn_setup():
        import jax, jax.numpy as jnp
        import numpy as np
        import math
        NUM_Q_HEADS = 32
        NUM_KV_HEADS = 8
        key = jax.random.key(seed)
        k1, k2, k3 = jax.random.split(key, 3)
        B, S, E = (2, 256, 256)
        kv_E = NUM_KV_HEADS * (E // NUM_Q_HEADS)
        q = jax.random.normal(k1, (B, S, E), dtype=jnp.float32)
        k = jax.random.normal(k2, (B, S, kv_E), dtype=jnp.float32)
        v = jax.random.normal(k3, (B, S, kv_E), dtype=jnp.float32)
        return {'q': q, 'k': k, 'v': v}
    _L1_xattn_all = _L1_xattn_setup()
    _L1_xattn_in = {k: v for k, v in _L1_xattn_all.items() if k in ()}
    del _L1_xattn_all

    def _L1_ffn_setup():
        import jax, jax.numpy as jnp
        import numpy as np
        B_, S, D = (2, 256, 256)
        F_ = 1024
        R = 16
        H = 16
        HD = D // H
        MOD_SCALE = 0.1
        EPS = 1e-06

        def _rmsnorm(x, w):
            v = jnp.mean(x * x, axis=-1, keepdims=True)
            return x * jax.lax.rsqrt(v + EPS) * w

        def _attention(x, Wq, Wk, Wv, Wo):
            b, s, d = x.shape
            q = (x @ Wq.T).reshape(b, s, H, HD)
            k = (x @ Wk.T).reshape(b, s, H, HD)
            v = (x @ Wv.T).reshape(b, s, H, HD)
            scores = jnp.einsum('bqhd,bkhd->bhqk', q, k) / np.sqrt(HD).astype(np.float32)
            causal = jnp.tril(jnp.ones((s, s), bool))
            scores = jnp.where(causal, scores, jnp.finfo(scores.dtype).min)
            probs = jax.nn.softmax(scores, axis=-1)
            out = jnp.einsum('bhqk,bkhd->bqhd', probs, v).reshape(b, s, d)
            return out @ Wo.T
        key = jax.random.key(seed)
        ks = jax.random.split(key, 12)
        sd = 0.02
        return {'hidden_states': jax.random.normal(ks[0], (B_, S, D), jnp.float32), 'ln1_w': jnp.ones((D,), jnp.float32), 'ln2_w': jnp.ones((D,), jnp.float32), 'Wq': jax.random.normal(ks[1], (D, D), jnp.float32) * sd, 'Wk': jax.random.normal(ks[2], (D, D), jnp.float32) * sd, 'Wv': jax.random.normal(ks[3], (D, D), jnp.float32) * sd, 'Wo': jax.random.normal(ks[4], (D, D), jnp.float32) * sd, 'A': jax.random.normal(ks[5], (D, R), jnp.float32) * (0.01 / np.sqrt(D)), 'B': jax.random.normal(ks[6], (R, F_), jnp.float32) * (0.01 / np.sqrt(R)), 'W_in_base': jax.random.normal(ks[7], (F_, D), jnp.float32) * sd, 'W_up_base': jax.random.normal(ks[8], (F_, D), jnp.float32) * sd, 'W_down': jax.random.normal(ks[9], (D, F_), jnp.float32) * sd}
    _L1_ffn_all = _L1_ffn_setup()
    _L1_ffn_in = {k: v for k, v in _L1_ffn_all.items() if k in ('ln1_w', 'ln2_w', 'Wq', 'Wk', 'Wv', 'Wo', 'A', 'B', 'W_in_base', 'W_up_base', 'W_down')}
    del _L1_ffn_all

    def _L2_xattn_setup():
        import jax, jax.numpy as jnp
        import numpy as np
        P_ASEM = 0.6
        key = jax.random.key(seed)
        k1, k2, k3 = jax.random.split(key, 3)
        B, N, D = (8, 256, 64)
        x = jax.random.normal(k1, (B, N, D), dtype=jnp.float32)
        adj = jax.random.uniform(k2, (B, N, N), dtype=jnp.float32)
        bound = 1.0 / np.sqrt(2 * D)
        W = jax.random.uniform(k3, (1, 2 * D), dtype=jnp.float32, minval=-bound, maxval=bound)
        b = jnp.zeros((1,), dtype=jnp.float32)
        return {'x': x, 'adj': adj, 'W': W, 'b': b}
    _L2_xattn_all = _L2_xattn_setup()
    _L2_xattn_in = {k: v for k, v in _L2_xattn_all.items() if k in ('W', 'b')}
    del _L2_xattn_all

    def _L2_ffn_setup():
        import jax, jax.numpy as jnp
        import numpy as np
        EPS = 1e-05

        def rms_norm(x):
            return x * jax.lax.rsqrt(jnp.mean(x * x, axis=-1, keepdims=True) + EPS)

        def act_quant(x):
            scale = 127.0 / jnp.clip(jnp.max(jnp.abs(x), axis=-1, keepdims=True), 1e-05)
            q = jnp.clip(jnp.round(x * scale), -128.0, 127.0) / scale
            return x + jax.lax.stop_gradient(q - x)

        def weight_quant(w):
            scale = 1.0 / jnp.clip(jnp.mean(jnp.abs(w)), 1e-05)
            q = jnp.clip(jnp.round(w * scale), -1.0, 1.0) / scale
            return w + jax.lax.stop_gradient(q - w)

        def bitlinear158(x, w, b):
            xq = act_quant(rms_norm(x))
            wq = weight_quant(w)
            return jnp.einsum('bsd,od->bso', xq, wq) + b

        def layer_norm(x, g, b):
            mu = jnp.mean(x, axis=-1, keepdims=True)
            var = jnp.mean((x - mu) ** 2, axis=-1, keepdims=True)
            return (x - mu) * jax.lax.rsqrt(var + EPS) * g + b
        key = jax.random.key(seed)
        ks = jax.random.split(key, 3)
        d, inner = (256, 1024)
        x = jax.random.normal(ks[0], (4, 256, d), dtype=jnp.float32)
        w1 = jax.random.normal(ks[1], (inner, d), dtype=jnp.float32) * 0.02
        b1 = jnp.zeros((inner,), jnp.float32)
        ln_g = jnp.ones((inner,), jnp.float32)
        ln_b = jnp.zeros((inner,), jnp.float32)
        w2 = jax.random.normal(ks[2], (d, inner), dtype=jnp.float32) * 0.02
        b2 = jnp.zeros((d,), jnp.float32)
        return {'x': x, 'w1': w1, 'b1': b1, 'ln_g': ln_g, 'ln_b': ln_b, 'w2': w2, 'b2': b2}
    _L2_ffn_all = _L2_ffn_setup()
    _L2_ffn_in = {k: v for k, v in _L2_ffn_all.items() if k in ('w1', 'b1', 'ln_g', 'ln_b', 'w2', 'b2')}
    del _L2_ffn_all

    def _L3_xattn_setup():
        import jax, jax.numpy as jnp
        import numpy as np
        import math
        D_MODEL = 256
        N_HEADS = 16
        N_GROUPS = 4
        HEADS_PER_GROUP = N_HEADS // N_GROUPS
        HEAD_DIM = D_MODEL // N_HEADS
        B, S = (2, 256)
        key = jax.random.key(seed)
        k1, k2, k3, k4, k5 = jax.random.split(key, 5)
        q = jax.random.normal(k1, (B, S, D_MODEL), dtype=jnp.float32)
        k = jax.random.normal(k2, (B, S, N_GROUPS * HEAD_DIM), dtype=jnp.float32)
        v = jax.random.normal(k3, (B, S, N_GROUPS * HEAD_DIM), dtype=jnp.float32)
        lim = 1.0 / math.sqrt(D_MODEL)
        Wc = jax.random.uniform(k4, (D_MODEL, D_MODEL), minval=-lim, maxval=lim, dtype=jnp.float32)
        bc = jax.random.uniform(k5, (D_MODEL,), minval=-lim, maxval=lim, dtype=jnp.float32)
        return {'q': q, 'k': k, 'v': v, 'Wc': Wc, 'bc': bc}
    _L3_xattn_all = _L3_xattn_setup()
    _L3_xattn_in = {k: v for k, v in _L3_xattn_all.items() if k in ('Wc', 'bc')}
    del _L3_xattn_all

    def _L3_ffn_setup():
        import jax, jax.numpy as jnp
        import numpy as np
        LN_EPS = 1e-05
        L2_EPS = 1e-12

        def _l2norm(v, axis):
            n = jnp.sqrt(jnp.sum(v * v, axis=axis, keepdims=True))
            return v / jnp.maximum(n, L2_EPS)
        key = jax.random.key(seed)
        ks = jax.random.split(key, 4)
        B, N, D, E, S, H = (8, 256, 256, 16, 128, 64)
        x = jax.random.normal(ks[0], (B, N, D), dtype=jnp.float32)
        mu = jax.random.normal(ks[1], (D, E, S), dtype=jnp.float32) / np.sqrt(D)
        W1 = jax.random.normal(ks[2], (E, D, H), dtype=jnp.float32) * np.sqrt(2.0 / D)
        W2 = jax.random.normal(ks[3], (E, H, D), dtype=jnp.float32) * np.sqrt(2.0 / (H + D))
        return {'x': x, 'gamma': jnp.ones((D,), jnp.float32), 'beta': jnp.zeros((D,), jnp.float32), 'mu': mu, 'scale': jnp.ones((1,), jnp.float32), 'W1': W1, 'b1': jnp.zeros((E, H), jnp.float32), 'W2': W2, 'b2': jnp.zeros((E, D), jnp.float32)}
    _L3_ffn_all = _L3_ffn_setup()
    _L3_ffn_in = {k: v for k, v in _L3_ffn_all.items() if k in ('gamma', 'beta', 'mu', 'scale', 'W1', 'b1', 'W2', 'b2')}
    del _L3_ffn_all
    return {'x': x, 'ctx_512': ctx_512, 'g_xattn': g_xattn, 'g_ffn': g_ffn, 'L0_xattn_W_k': _L0_xattn_in['W_k'], 'L0_xattn_b_k': _L0_xattn_in['b_k'], 'L0_xattn_ln_gamma': _L0_xattn_in['ln_gamma'], 'L0_xattn_ln_beta': _L0_xattn_in['ln_beta'], 'L0_ffn_router_w': _L0_ffn_in['router_w'], 'L0_ffn_router_bias': _L0_ffn_in['router_bias'], 'L0_ffn_wg': _L0_ffn_in['wg'], 'L0_ffn_wu': _L0_ffn_in['wu'], 'L0_ffn_wd': _L0_ffn_in['wd'], 'L0_ffn_swg': _L0_ffn_in['swg'], 'L0_ffn_swu': _L0_ffn_in['swu'], 'L0_ffn_swd': _L0_ffn_in['swd'], 'L1_ffn_ln1_w': _L1_ffn_in['ln1_w'], 'L1_ffn_ln2_w': _L1_ffn_in['ln2_w'], 'L1_ffn_Wq': _L1_ffn_in['Wq'], 'L1_ffn_Wk': _L1_ffn_in['Wk'], 'L1_ffn_Wv': _L1_ffn_in['Wv'], 'L1_ffn_Wo': _L1_ffn_in['Wo'], 'L1_ffn_A': _L1_ffn_in['A'], 'L1_ffn_B': _L1_ffn_in['B'], 'L1_ffn_W_in_base': _L1_ffn_in['W_in_base'], 'L1_ffn_W_up_base': _L1_ffn_in['W_up_base'], 'L1_ffn_W_down': _L1_ffn_in['W_down'], 'L2_xattn_W': _L2_xattn_in['W'], 'L2_xattn_b': _L2_xattn_in['b'], 'L2_ffn_w1': _L2_ffn_in['w1'], 'L2_ffn_b1': _L2_ffn_in['b1'], 'L2_ffn_ln_g': _L2_ffn_in['ln_g'], 'L2_ffn_ln_b': _L2_ffn_in['ln_b'], 'L2_ffn_w2': _L2_ffn_in['w2'], 'L2_ffn_b2': _L2_ffn_in['b2'], 'L3_xattn_Wc': _L3_xattn_in['Wc'], 'L3_xattn_bc': _L3_xattn_in['bc'], 'L3_ffn_gamma': _L3_ffn_in['gamma'], 'L3_ffn_beta': _L3_ffn_in['beta'], 'L3_ffn_mu': _L3_ffn_in['mu'], 'L3_ffn_scale': _L3_ffn_in['scale'], 'L3_ffn_W1': _L3_ffn_in['W1'], 'L3_ffn_b1': _L3_ffn_in['b1'], 'L3_ffn_W2': _L3_ffn_in['W2'], 'L3_ffn_b2': _L3_ffn_in['b2']}

def reference(x, ctx_512, g_xattn, g_ffn, L0_xattn_W_k, L0_xattn_b_k, L0_xattn_ln_gamma, L0_xattn_ln_beta, L0_ffn_router_w, L0_ffn_router_bias, L0_ffn_wg, L0_ffn_wu, L0_ffn_wd, L0_ffn_swg, L0_ffn_swu, L0_ffn_swd, L1_ffn_ln1_w, L1_ffn_ln2_w, L1_ffn_Wq, L1_ffn_Wk, L1_ffn_Wv, L1_ffn_Wo, L1_ffn_A, L1_ffn_B, L1_ffn_W_in_base, L1_ffn_W_up_base, L1_ffn_W_down, L2_xattn_W, L2_xattn_b, L2_ffn_w1, L2_ffn_b1, L2_ffn_ln_g, L2_ffn_ln_b, L2_ffn_w2, L2_ffn_b2, L3_xattn_Wc, L3_xattn_bc, L3_ffn_gamma, L3_ffn_beta, L3_ffn_mu, L3_ffn_scale, L3_ffn_W1, L3_ffn_b1, L3_ffn_W2, L3_ffn_b2):
    import jax
    import jax.numpy as jnp

    def _L0_xattn_ref(p, k_v, W_k, b_k, ln_gamma, ln_beta):
        import jax, jax.numpy as jnp
        import numpy as np
        EPS = 1e-06
        IMAGE_DIMS = 256
        kv = k_v @ W_k.T + b_k
        out = jnp.einsum('bij,bjd->bid', p, kv)
        scale = IMAGE_DIMS ** (-0.5)
        sim = jnp.einsum('bid,bjd->bij', out, kv) * scale
        mu = jnp.mean(sim, axis=-1, keepdims=True)
        var = jnp.var(sim, axis=-1, keepdims=True)
        sim = (sim - mu) * jax.lax.rsqrt(var + EPS) * ln_gamma + ln_beta
        attn = jax.nn.softmax(sim, axis=-1)
        return attn

    def _L0_ffn_ref(x, router_w, router_bias, wg, wu, wd, swg, swu, swd):
        import jax, jax.numpy as jnp
        import numpy as np
        B, T, D = (2, 128, 256)
        E, F, K = (64, 64, 4)
        S, HS = (2, 64 * 4)
        b, t, d = x.shape
        flat = x.reshape(b * t, d)
        n = flat.shape[0]
        logits = flat @ router_w
        scores = jax.nn.softmax(logits, axis=-1)
        _, topk_idx = jax.lax.top_k(logits + router_bias, K)
        topk_scores = jnp.take_along_axis(scores, topk_idx, axis=-1)
        topk_scores = topk_scores / topk_scores.sum(axis=-1, keepdims=True)
        comb = jnp.zeros((n, E), dtype=flat.dtype).at[jnp.arange(n)[:, None], topk_idx].set(topk_scores)
        g = jax.nn.silu(jnp.einsum('nd,edf->nef', flat, wg))
        u = jnp.einsum('nd,edf->nef', flat, wu)
        routed = jnp.einsum('ne,nef,efd->nd', comb, g * u, wd)
        sg = jax.nn.silu(jnp.einsum('nd,sdh->nsh', flat, swg))
        su = jnp.einsum('nd,sdh->nsh', flat, swu)
        shared = jnp.einsum('nsh,shd->nd', sg * su, swd)
        return (routed + shared).reshape(b, t, d)

    def _L1_xattn_ref(q, k, v):
        import jax, jax.numpy as jnp
        import numpy as np
        import math
        NUM_Q_HEADS = 32
        NUM_KV_HEADS = 8
        B, S, E = q.shape
        H, KV = (NUM_Q_HEADS, NUM_KV_HEADS)
        D = E // H
        G = H // KV
        scale = math.sqrt(D)
        qh = q.reshape(B, S, KV, G, D).transpose(0, 2, 3, 1, 4)
        kh = k.reshape(B, S, KV, D).transpose(0, 2, 1, 3)
        vh = v.reshape(B, S, KV, D).transpose(0, 2, 1, 3)
        scores = jnp.einsum('bkgsd,bktd->bkgst', qh, kh) / scale
        weights = jax.nn.softmax(scores, axis=-1)
        out = jnp.einsum('bkgst,bktd->bkgsd', weights, vh)
        return out.transpose(0, 3, 1, 2, 4).reshape(B, S, E)

    def _L1_ffn_ref(hidden_states, ln1_w, ln2_w, Wq, Wk, Wv, Wo, A, B, W_in_base, W_up_base, W_down):
        import jax, jax.numpy as jnp
        import numpy as np
        B_, S, D = (2, 256, 256)
        F_ = 1024
        R = 16
        H = 16
        HD = D // H
        MOD_SCALE = 0.1
        EPS = 1e-06

        def _rmsnorm(x, w):
            v = jnp.mean(x * x, axis=-1, keepdims=True)
            return x * jax.lax.rsqrt(v + EPS) * w

        def _attention(x, Wq, Wk, Wv, Wo):
            b, s, d = x.shape
            q = (x @ Wq.T).reshape(b, s, H, HD)
            k = (x @ Wk.T).reshape(b, s, H, HD)
            v = (x @ Wv.T).reshape(b, s, H, HD)
            scores = jnp.einsum('bqhd,bkhd->bhqk', q, k) / np.sqrt(HD).astype(np.float32)
            causal = jnp.tril(jnp.ones((s, s), bool))
            scores = jnp.where(causal, scores, jnp.finfo(scores.dtype).min)
            probs = jax.nn.softmax(scores, axis=-1)
            out = jnp.einsum('bhqk,bkhd->bqhd', probs, v).reshape(b, s, d)
            return out @ Wo.T
        residual = hidden_states
        x = _rmsnorm(hidden_states, ln1_w)
        attn = _attention(x, Wq, Wk, Wv, Wo)
        mod = MOD_SCALE * jnp.tanh(attn @ A)
        h = _rmsnorm(residual, ln2_w)
        gate_pre = h @ W_in_base.T + mod * (h @ A) @ B
        gate = jax.nn.silu(gate_pre)
        up = h @ W_up_base.T
        mlp_out = gate * up @ W_down.T
        return residual + mlp_out

    def _L2_xattn_ref(x, adj, W, b):
        import jax, jax.numpy as jnp
        import numpy as np
        P_ASEM = 0.6
        D = x.shape[-1]
        Wi = W[:, :D]
        Wj = W[:, D:]
        si = jnp.einsum('bnd,d->bn', x, Wi[0])
        sj = jnp.einsum('bnd,d->bn', x, Wj[0])
        xij = jax.nn.sigmoid(si[:, :, None] + sj[:, None, :] + b[0])
        return P_ASEM * xij + (1.0 - P_ASEM) * adj

    def _L2_ffn_ref(x, w1, b1, ln_g, ln_b, w2, b2):
        import jax, jax.numpy as jnp
        import numpy as np
        EPS = 1e-05

        def rms_norm(x):
            return x * jax.lax.rsqrt(jnp.mean(x * x, axis=-1, keepdims=True) + EPS)

        def act_quant(x):
            scale = 127.0 / jnp.clip(jnp.max(jnp.abs(x), axis=-1, keepdims=True), 1e-05)
            q = jnp.clip(jnp.round(x * scale), -128.0, 127.0) / scale
            return x + jax.lax.stop_gradient(q - x)

        def weight_quant(w):
            scale = 1.0 / jnp.clip(jnp.mean(jnp.abs(w)), 1e-05)
            q = jnp.clip(jnp.round(w * scale), -1.0, 1.0) / scale
            return w + jax.lax.stop_gradient(q - w)

        def bitlinear158(x, w, b):
            xq = act_quant(rms_norm(x))
            wq = weight_quant(w)
            return jnp.einsum('bsd,od->bso', xq, wq) + b

        def layer_norm(x, g, b):
            mu = jnp.mean(x, axis=-1, keepdims=True)
            var = jnp.mean((x - mu) ** 2, axis=-1, keepdims=True)
            return (x - mu) * jax.lax.rsqrt(var + EPS) * g + b
        h = jax.nn.silu(bitlinear158(x, w1, b1))
        h = jax.nn.gelu(h, approximate=False)
        h = layer_norm(h, ln_g, ln_b)
        return bitlinear158(h, w2, b2)

    def _L3_xattn_ref(q, k, v, Wc, bc):
        import jax, jax.numpy as jnp
        import numpy as np
        import math
        D_MODEL = 256
        N_HEADS = 16
        N_GROUPS = 4
        HEADS_PER_GROUP = N_HEADS // N_GROUPS
        HEAD_DIM = D_MODEL // N_HEADS
        B, S = (2, 256)
        b, s, _ = q.shape
        qh = q.reshape(b, s, N_GROUPS, HEADS_PER_GROUP, HEAD_DIM).transpose(0, 2, 3, 1, 4)
        kh = k.reshape(b, s, N_GROUPS, HEAD_DIM).transpose(0, 2, 1, 3)
        vh = v.reshape(b, s, N_GROUPS, HEAD_DIM).transpose(0, 2, 1, 3)
        scale = 1.0 / math.sqrt(HEAD_DIM)
        scores = jnp.einsum('bghsd,bgtd->bghst', qh, kh) * scale
        probs = jax.nn.softmax(scores, axis=-1)
        out = jnp.einsum('bghst,bgtd->bghsd', probs, vh)
        out = out.transpose(0, 3, 1, 2, 4).reshape(b, s, D_MODEL)
        return out @ Wc.T + bc

    def _L3_ffn_ref(x, gamma, beta, mu, scale, W1, b1, W2, b2):
        import jax, jax.numpy as jnp
        import numpy as np
        LN_EPS = 1e-05
        L2_EPS = 1e-12

        def _l2norm(v, axis):
            n = jnp.sqrt(jnp.sum(v * v, axis=axis, keepdims=True))
            return v / jnp.maximum(n, L2_EPS)
        B, N, D = x.shape
        _, E, S = mu.shape
        mean = jnp.mean(x, axis=-1, keepdims=True)
        var = jnp.mean(jnp.square(x - mean), axis=-1, keepdims=True)
        x_ln = (x - mean) / jnp.sqrt(var + LN_EPS) * gamma + beta
        x_n = _l2norm(x_ln, -1) * scale
        mu_n = _l2norm(mu, 0)
        logits = jnp.einsum('bnd,des->bnes', x_n, mu_n)
        dispatch = jax.nn.softmax(logits, axis=1)
        combine = jax.nn.softmax(logits.reshape(B, N, E * S), axis=-1)
        slot_in = jnp.einsum('bnd,bnes->besd', x_ln, dispatch)
        h = jax.nn.gelu(jnp.einsum('besd,edh->besh', slot_in, W1) + b1[None, :, None, :], approximate=False)
        slot_out = jnp.einsum('besh,ehd->besd', h, W2) + b2[None, :, None, :]
        out = jnp.einsum('bsd,bns->bnd', slot_out.reshape(B, E * S, D), combine)
        return out
    x = x + jnp.tanh(g_xattn[0]) * _L0_xattn_ref(_layernorm(x, axis=-1), ctx_512, L0_xattn_W_k, L0_xattn_b_k, L0_xattn_ln_gamma, L0_xattn_ln_beta)
    x = x + jnp.tanh(g_ffn[0]) * _L0_ffn_ref(_layernorm(x, axis=-1), L0_ffn_router_w, L0_ffn_router_bias, L0_ffn_wg, L0_ffn_wu, L0_ffn_wd, L0_ffn_swg, L0_ffn_swu, L0_ffn_swd)
    x = x + jnp.tanh(g_xattn[1]) * _L1_xattn_ref(_layernorm(x, axis=-1), ctx_512, ctx_512)
    x = x + jnp.tanh(g_ffn[1]) * _L1_ffn_ref(_layernorm(x, axis=-1), L1_ffn_ln1_w, L1_ffn_ln2_w, L1_ffn_Wq, L1_ffn_Wk, L1_ffn_Wv, L1_ffn_Wo, L1_ffn_A, L1_ffn_B, L1_ffn_W_in_base, L1_ffn_W_up_base, L1_ffn_W_down)
    x = x + jnp.tanh(g_xattn[2]) * _L2_xattn_ref(ctx_512, _layernorm(x, axis=-1), L2_xattn_W, L2_xattn_b)
    x = x + jnp.tanh(g_ffn[2]) * _L2_ffn_ref(_layernorm(x, axis=-1), L2_ffn_w1, L2_ffn_b1, L2_ffn_ln_g, L2_ffn_ln_b, L2_ffn_w2, L2_ffn_b2)
    x = x + jnp.tanh(g_xattn[3]) * _L3_xattn_ref(_layernorm(x, axis=-1), ctx_512, ctx_512, L3_xattn_Wc, L3_xattn_bc)
    x = x + jnp.tanh(g_ffn[3]) * _L3_ffn_ref(_layernorm(x, axis=-1), L3_ffn_gamma, L3_ffn_beta, L3_ffn_mu, L3_ffn_scale, L3_ffn_W1, L3_ffn_b1, L3_ffn_W2, L3_ffn_b2)
    return x

_drawn_inputs = setup_inputs


def setup_inputs(seed=0):
    import zlib

    import numpy as np

    out = dict(_drawn_inputs(seed))
    spreads = {'L0_xattn_b_k': (0.0, 2.0),
     'L0_xattn_ln_gamma': (1.0, 0.6),
     'L0_xattn_ln_beta': (0.0, 0.8),
     'L0_ffn_router_bias': (0.0, 0.8),
     'L1_ffn_ln1_w': (1.0, 0.6),
     'L1_ffn_ln2_w': (1.0, 0.6),
     'L2_ffn_b1': (0.0, 0.297),
     'L2_ffn_ln_g': (1.0, 0.6),
     'L2_ffn_ln_b': (0.0, 1.101),
     'L2_ffn_b2': (0.0, 0.467),
     'L3_ffn_gamma': (1.0, 0.6),
     'L3_ffn_beta': (0.0, 2.0),
     'L3_ffn_b1': (0.0, 2.0),
     'L3_ffn_b2': (0.0, 1.658)}
    factors = {'L0_xattn_W_k': 8.0,
     'L0_ffn_router_w': 8.0,
     'L0_ffn_wg': 8.0,
     'L0_ffn_wu': 8.0,
     'L0_ffn_wd': 8.0,
     'L0_ffn_swg': 3.534,
     'L0_ffn_swu': 3.476,
     'L0_ffn_swd': 3.491,
     'L1_ffn_Wq': 175.683,
     'L1_ffn_Wk': 178.521,
     'L1_ffn_Wv': 175.74,
     'L1_ffn_Wo': 177.177,
     'L1_ffn_A': 177.024,
     'L1_ffn_B': 174.537,
     'L1_ffn_W_in_base': 3.094,
     'L1_ffn_W_up_base': 3.079,
     'L1_ffn_W_down': 3.078,
     'L3_xattn_bc': 8.876,
     'L3_ffn_mu': 200.0,
     'L2_xattn_W': 3.972}
    for name, (base, spread) in spreads.items():
        noise = np.random.default_rng([zlib.crc32(name.encode()), seed]).standard_normal(out[name].shape)
        drawn = base * np.exp(spread * noise) if base else spread * noise
        out[name] = jnp.asarray(drawn.astype(out[name].dtype))
    for name, factor in factors.items():
        out[name] = (out[name] * factor).astype(out[name].dtype)
    return out
```

```python
from contextlib import ExitStack

import numpy as np

import concourse.bass as bass
from concourse import mybir

P = 128
ALU = mybir.AluOpType
ACT = mybir.ActivationFunctionType
F32 = mybir.dt.float32
BF16 = mybir.dt.bfloat16
I32 = mybir.dt.int32
AX = mybir.AxisListType.X

B, N, D = 4, 256, 256
NT = N // P
DC = D // P
CD = 64
E, F = 64, 64
TOPK = 4
PAIRS = E // 2 + 4
F1 = 1024
R = 16
SE, SS, SH = 16, 128, 64
SLOTS = SE * SS
MASKED = -1e30
BIG = 3e38
ROUND = 1.5 * 2.0 ** 23
TOKENS = B * N
HALVES = TOKENS // 512
ATTENTIONS = {"l1x": (32, 4, 8, False), "l1f": (16, 1, 16, True), "l3x": (16, 4, 16, False)}


ATT_COUNTS = {}
for _L, (_H, _G, _HD, _) in ATTENTIONS.items():
    _groups = _H // _G // 4 + _H // 4
    for _name, _n in (("parts", 2), ("parts_copied", 4), ("partsT", _groups), ("parts_outa", (_groups + 1) // 2),
                      ("parts_outb", _groups // 2), ("q_scores", _H), ("max", _H), ("max_parts", 1), ("mT_ps", 1),
                      ("mT", 1), ("v", 2 if _G > 1 else 3), ("probs", _H), ("scores", _H), ("pv", _H),
                      ("oT", _H // 8), ("o", _H // 8), ("attn", NT)):
        ATT_COUNTS.setdefault(_name, {})[_L] = _n


def before(L, name):
    order = list(ATTENTIONS)
    return sum(ATT_COUNTS[name][k] for k in order[:order.index(L)])


class Steps:

    def __init__(self, eng, sem):
        self.eng, self.sem, self.n = eng, sem, 0

    def __call__(self, ins):
        ins.then_inc(self.sem, 1)
        self.n += 1
        self.eng.wait_ge(self.sem, self.n)


def flamingo(nc, I, out):
    with ExitStack() as ctx:
        sems, batch_sems = {}, []

        def once(name):
            if name not in sems:
                sems[name] = ctx.enter_context(nc.semaphore(name))
            return sems[name]

        def S(name):
            if name not in sems:
                sems[name] = ctx.enter_context(nc.semaphore(name))
                batch_sems.append(sems[name])
            return sems[name]

        top = [(nc.sbuf_base + 63) // 64 * 64]
        high = [0]

        def sb(name, shape, dt=F32):
            size = int(np.prod(shape[1:])) * (2 if dt == BF16 else 4)
            t = nc.alloc_sbuf_tensor_at(name, list(shape), dt, offset=top[0])
            top[0] += (size + 31) // 32 * 32
            high[0] = max(high[0], top[0])
            return t

        bank = [ctx.enter_context(nc.psum_tensor(f"bank{k}", [P, 512], F32)) for k in range(8)]
        bankb = [k[:, :].bitcast(BF16) for k in bank]

        xs = sb("xs", [P, B * NT, D])
        ctxs = sb("ctxs", [P, B * NT, CD])
        ident = sb("ident", [P, P])
        identb = sb("identb", [P, P], BF16)
        ones = sb("ones", [P, P])
        sel = sb("sel", [96, 32, P], BF16)
        mask_q = sb("mask_q", [P, NT, N], BF16)
        mask_t = sb("mask_t", [P, NT, N], BF16)
        gates = sb("gates", [P, 8])
        mst = sb("mst", [P, NT, 3, 32], BF16)
        vst = sb("vst", [P, NT, 16, 32])
        wkT = sb("wkT", [CD, CD])
        bk_col = sb("bk_col", [CD, 1])
        bk_row = sb("bk_row", [P, CD])
        sc_scale = sb("sc_scale", [P, 1])
        l2b = sb("l2b", [P, 1])
        l2wi = sb("l2wi", [P, CD])
        l2wj = sb("l2wj", [CD, P])
        wqkvT = sb("wqkvT", [P, DC, 3 * D])
        wcT = sb("wcT", [P, DC, D])
        winT = sb("winT", [P, DC, F1])
        wupT = sb("wupT", [P, DC, F1])
        wdT = sb("wdT", [P, F1 // P, D])
        w1qT = sb("w1qT", [P, DC, F1], BF16)
        w2qT = sb("w2qT", [P, F1 // P, D], BF16)
        mun = sb("mun", [P, DC, SLOTS])
        w1s = sb("w1s", [P, DC, SE, SH])
        w2a = sb("w2a", [SH + 1, SE, D])
        rowsD = {n: sb("row_" + n, [P, D]) for n in
                 ("L0_xattn_ln_gamma", "L0_xattn_ln_beta", "L1_ffn_ln1_w", "L1_ffn_ln2_w", "L2_ffn_b2",
                  "L3_xattn_bc", "L3_ffn_gamma", "L3_ffn_beta")}
        rowsF = {n: sb("row_" + n, [P, F1]) for n in ("L2_ffn_b1", "L2_ffn_ln_g", "L2_ffn_ln_b")}
        wa = sb("wa", [P, DC, R])
        am = sb("am", [P, DC, R])
        bm = sb("bm", [R, F1])
        b1T = sb("b1T", [SH, SE])
        wdq = sb("wdq", [P, 2])
        x = sb("x", [P, NT, D])
        c = sb("c", [P, NT, CD])
        xn = sb("xn", [P, NT, D])
        xT = sb("xT", [P, DC, N])
        cT = sb("cT", [CD, N])
        tmp = sb("tmp", [P, NT, D])
        bn = sb("bn", [P, 4, 6])
        mv = sb("mv", [P, NT, 2])
        ve = sb("ve", [P, 4])
        rs = sb("rs", [P, 4])
        nw = sb("nw", [P, 4])
        st = sb("st", [P, 16])
        rbc = sb("rbc", [P, N])
        cmx = sb("cmx", [P, SE])
        cmr = sb("cmr", [P, SE])
        cmT = sb("cmT", [96, P], BF16)
        region = top[0]

        xnT = sb("xnT", [P, DC, TOKENS])
        comb_hm = sb("comb_hm", [P, TOKENS], BF16)
        comb_l = sb("comb_l", [E + 1, TOKENS], BF16)
        pick_hm = sb("pick_hm", [P, PAIRS, P], BF16)
        pick_l = sb("pick_l", [E + 1, PAIRS, P], BF16)
        SLOTN = 4
        wg = [sb(f"wg{k}", [P, DC, 2 * F]) for k in range(SLOTN)]
        wu = [sb(f"wu{k}", [P, DC, 2 * F]) for k in range(SLOTN)]
        wd = [sb(f"wd{k}", [P, D]) for k in range(SLOTN)]
        sg = [sb(f"sg{k}", [P, 512]) for k in range(2)]
        hu = [sb(f"hu{k}", [P, 512]) for k in range(2)]
        hh = [sb(f"hh{k}", [P, 512]) for k in range(2)]
        kvT = sb("kvT", [CD, N])
        kv = sb("kv", [P, NT, CD])
        oT = sb("oT", [CD, N])
        rw = sb("rw", [P, DC, E])
        rb = sb("rb", [P, E])
        lg0 = sb("lg0", [P, NT, E])
        lb0 = sb("lb0", [P, NT, E + TOPK])
        lr0 = sb("lr0", [P, NT, E + TOPK])
        cb0 = sb("cb0", [P, NT, E])
        ct0 = sb("ct0", [P, NT, E])
        cst = sb("cst", [P, NT, 3, E], BF16)
        m8 = sb("m8", [P, NT, 8])
        zero_w = sb("zero_w", [P, P], BF16)
        yT = xnT

        top[0] = region + DC * TOKENS * 4
        stage = [sb(f"stage{k}", [P, 2048]) for k in range(4)]
        tern = [sb(f"tern{k}", [P, 2048], BF16) for k in range(2)]
        mu2 = sb("mu2", [P, DC, SLOTS])
        top[0] = region
        qst = sb("qst", [P, NT, 6 * D], BF16)
        kst = sb("kst", [P, NT, 6 * D], BF16)
        qT = sb("qT", [96, 32, N], BF16)
        kT = sb("kT", [96, 16, N], BF16)
        prob = [sb(f"prob{k}", [P, 512]) for k in range(4)]
        mx = sb("mx", [P, NT, 32])
        mr = sb("mr", [P, NT, 32])
        qr = sb("qr", [P, NT, D])
        mT = sb("mT", [96, N], BF16)
        otr = sb("otr", [P, 4, 512])
        after_otr = top[0]
        top[0] -= 4 * 512 * 4
        qf = sb("qf", [P, NT, D])
        kf = sb("kf", [P, NT, D])
        top[0] = after_otr
        rc = sb("rc", [P, 4, 16])
        at = sb("at", [P, NT, D])
        atT = sb("atT", [P, DC, N])
        hT = sb("hT", [P, DC, N])
        modT = sb("modT", [R, N])
        mh = sb("mh", [R, N])
        top[0] = region
        sgf = [sb(f"sgf{k}", [P, N]) for k in range(2)]
        gu = sb("gu", [P, F1 // P, N])
        top[0] = region
        h2 = sb("h2", [P, NT, F1])
        h2s = sb("h2s", [P, NT, F1])
        q1 = sb("q1", [P, NT, D], BF16)
        q1T = sb("q1T", [P, DC, N], BF16)
        q2 = sb("q2", [P, NT, F1], BF16)
        q2T = sb("q2T", [P, F1 // P, N], BF16)
        top[0] = region
        so = sb("so", [P, SE, D + 1])
        top[0] = region
        lg = sb("lg", [P, NT, SLOTS])
        top[0] = region + (SE * (D + 1) * 4 + 31) // 32 * 32
        lT = sb("lT", [P, SE, N])
        siT = sb("siT", [P, DC, SLOTS])
        hsT = sb("hsT", [SH + 1, SLOTS])
        xl = sb("xl", [P, NT, D])
        rsum = [sb(f"rsum{k}", [P, 512]) for k in range(2)]
        rmx = sb("rmx", [P, NT, 4])
        mT3 = sb("mT3", [96, N], BF16)
        assert high[0] <= nc.sbuf_usable_end

        block = ctx.enter_context(nc.Block())

        def blocks_of(w, rows, cols, dst):
            groups = []
            for ic in range(cols // P):
                for oc0 in range(0, rows // P, 4):
                    n = min(4, rows // P - oc0)
                    groups.append(([w[:, (oc0 + j) * cols + ic * P:(oc0 + j) * cols + ic * P + P] for j in range(n)],
                                   dst(ic, oc0 * P, n * P)))
            return groups

        PREP = []
        for k in range(3):
            PREP += blocks_of(stage[0][:, k * 512:(k + 1) * 512], D, D,
                              lambda ic, o, n, k=k: wqkvT[:, ic, k * D + o:k * D + o + n])
        PREP += blocks_of(stage[0][:, 1536:2048], D, D, lambda ic, o, n: wcT[:, ic, o:o + n])
        PREP += blocks_of(stage[1], F1, D, lambda ic, o, n: winT[:, ic, o:o + n])
        STAGE_GROUPS = [None, len(PREP)]
        PREP += blocks_of(stage[2], F1, D, lambda ic, o, n: wupT[:, ic, o:o + n])
        PREP += blocks_of(stage[3], D, F1, lambda ic, o, n: wdT[:, ic, o:o + n])
        PREPB = blocks_of(tern[0], F1, D, lambda ic, o, n: w1qT[:, ic, o:o + n])
        PREPB += blocks_of(tern[1], D, F1, lambda ic, o, n: w2qT[:, ic, o:o + n])

        REST = len(rowsD) - 2 + len(rowsF) + 12

        def clear(eng):
            nums = sorted(s.num for s in batch_sems)
            first = nums[0]
            for a, b in zip(nums, nums[1:] + [None]):
                if b != a + 1:
                    eng.sem_clear(range(first, a + 1))
                    first = b

        def end_of_batch(eng):
            eng.sem_inc(once("batch_arrived"), 1)

        @block.sync
        def _(sp):
            W = sp.dma_start
            ld = once("first_loads")
            W(xs[:, :, :], I["x"].rearrange("b (i p) d -> p (b i) d", p=P)).then_inc(once("x_loaded"), 16)
            W(ctxs[:, :, :], I["ctx_512"].rearrange("b (i p) d -> p (b i) d", p=P)).then_inc(once("x_loaded"), 16)
            W(wkT[:, :], I["L0_xattn_W_k"]).then_inc(ld, 16)
            W(bk_col[:, :], I["L0_xattn_b_k"].rearrange("(p a) -> p a", a=1)).then_inc(ld, 16)
            W(bk_row[:, :], I["L0_xattn_b_k"].partition_broadcast(P)).then_inc(ld, 16)
            for n in ("L0_xattn_ln_gamma", "L0_xattn_ln_beta"):
                W(rowsD[n][:, :], I[n].partition_broadcast(P)).then_inc(ld, 16)
            W(gates[:, 0:4], I["g_xattn"].partition_broadcast(P)).then_inc(ld, 16)
            W(gates[:, 4:8], I["g_ffn"].partition_broadcast(P)).then_inc(ld, 16)
            W(rw[:, :, :], I["L0_ffn_router_w"].rearrange("(p c) e -> p c e", c=DC)).then_inc(ld, 16)
            W(rb[:, :], I["L0_ffn_router_bias"].partition_broadcast(P)).then_inc(ld, 16)

            def load_experts(k, pair, shared):
                sem = once(f"experts_loaded{k}")
                for w, name in ((wg[k], "g"), (wu[k], "u")):
                    for e in range(2):
                        if shared is None:
                            src = I["L0_ffn_w" + name].rearrange("(q e) (p c) f -> e q p c f", e=2, c=DC)[e, pair]
                        else:
                            src = I["L0_ffn_sw" + name].rearrange("s (p c) (q e f) -> s q e p c f", c=DC, e=2, f=F)[
                                shared // 2, shared % 2, e]
                        W(w[:, :, e * F:(e + 1) * F], src).then_inc(sem, 16)
                if shared is None:
                    W(wd[k][:, :], I["L0_ffn_wd"].rearrange("(q e) f d -> q (e f) d", e=2)[pair]).then_inc(sem, 16)
                else:
                    W(wd[k][:, :], I["L0_ffn_swd"].rearrange("s (q p) d -> (s q) p d", p=P)[shared]).then_inc(sem, 16)

            for k in range(SLOTN):
                load_experts(k, k, None)
            rest = once("rest_loads")
            for n in list(rowsD)[2:]:
                W(rowsD[n][:, :], I[n].partition_broadcast(P)).then_inc(rest, 16)
            for n in rowsF:
                W(rowsF[n][:, :], I[n].partition_broadcast(P)).then_inc(rest, 16)
            W(sc_scale[:, :], I["L3_ffn_scale"].partition_broadcast(P)).then_inc(rest, 16)
            W(l2b[:, :], I["L2_xattn_b"].partition_broadcast(P)).then_inc(rest, 16)
            W(l2wi[:, :], I["L2_xattn_W"][0, 0:CD].partition_broadcast(P)).then_inc(rest, 16)
            W(l2wj[:, 0:1], I["L2_xattn_W"].rearrange("a (t p) -> t p a", p=CD)[1]).then_inc(rest, 16)
            W(mun[:, :, :], I["L3_ffn_mu"].rearrange("(c p) e s -> p c (e s)", p=P)).then_inc(rest, 16)
            for cc in range(DC):
                W(w1s[:, cc, :, :], I["L3_ffn_W1"].rearrange("e (c p) h -> c p e h", p=P)[cc]).then_inc(rest, 16)
            W(w2a[0:SH, :, :], I["L3_ffn_W2"].rearrange("e h d -> h e d")).then_inc(rest, 16)
            W(w2a[SH:SH + 1, :, :], I["L3_ffn_b2"].rearrange("(a e) d -> a e d", a=1)).then_inc(rest, 16)
            W(am[:, :, :], I["L1_ffn_A"].rearrange("(c p) r -> p c r", p=P)).then_inc(rest, 16)
            W(bm[:, :], I["L1_ffn_B"]).then_inc(rest, 16)
            W(b1T[:, :], I["L3_ffn_b1"].rearrange("e h -> h e"),
              allow_slow_non_contiguous=True).then_inc(rest, 16)
            with sp.Fori(0, E // 2 // SLOTN - 1) as t:
                for k in range(SLOTN):
                    sp.wait_ge(once("hidden_used"), t * (2 * SLOTN) + (2 * k + 4))
                    sp.sem_inc(once("slot_free"), 1)
                    load_experts(k, t * SLOTN + (SLOTN + k), None)
            for k in range(SLOTN):
                sp.wait_ge(once("hidden_used"), 2 * (E // 2 - SLOTN + k + 1) + 2)
                load_experts(k, None, k)
            sp.wait_ge(once("hidden_used"), 2 * PAIRS + 2)
            sp.wait_ge(once("experts_out"), 2 * HALVES)
            stg = once("stage_loaded")
            for k, n in enumerate(("Wq", "Wk", "Wv")):
                W(stage[0][:, k * 512:(k + 1) * 512].rearrange("p (o i) -> p o i", i=D),
                  I["L1_ffn_" + n].rearrange("(o p) i -> p o i", p=P)).then_inc(stg, 16)
            W(stage[0][:, 1536:2048].rearrange("p (o i) -> p o i", i=D),
              I["L3_xattn_Wc"].rearrange("(o p) i -> p o i", p=P)).then_inc(stg, 16)
            for k, n, cols in ((1, "L1_ffn_W_in_base", D), (2, "L1_ffn_W_up_base", D), (3, "L1_ffn_W_down", F1),
                               (0, "L2_ffn_w1", D), (1, "L2_ffn_w2", F1)):
                if n == "L2_ffn_w1":
                    sp.wait_ge(once("prep_done"), STAGE_GROUPS[1])
                W(stage[k][:, :].rearrange("p (o i) -> p o i", i=cols),
                  I[n].rearrange("(o p) i -> p o i", p=P)).then_inc(stg, 16)
            sp.wait_ge(once("prep_done"), len(PREP) + len(PREPB))
            W(stage[2][:, 0:512].rearrange("p (o i) -> p o i", i=D),
              I["L1_ffn_Wo"].rearrange("(o p) i -> p o i", p=P)).then_inc(once("wo_loaded"), 16)
            with sp.Fori(0, B) as b:
                sp.wait_ge(S("x_final"), NT)
                W(out.rearrange("b (i p) d -> b p i d", p=P)[b], x[:, :, :]).then_inc(once("x_out"), 16)
                sp.wait_ge(once("x_out"), b * 16 + 16)
                end_of_batch(sp)
                sp.wait_ge(once("batch_cleared"), b + (B + 1))
                sp.sem_inc(once("next_batch"), 1)

        def four_transposes(pe, dst, src, ident_, strided=False):
            for cc in range(DC):
                for i in range(NT):
                    s = src[:, i, cc:D:DC] if strided else src[:, i, cc * P:(cc + 1) * P]
                    last = pe.transpose(dst[:, cc * N + i * P:cc * N + i * P + P], s, ident_)
            return last

        @block.tensor
        def _(pe):
            mm = pe.matmul
            pe.wait_ge(once("first_loads"), 9 * 16)
            pe.wait_ge(once("consts"), 5)
            pe.transpose(bank[0][0:CD, 0:CD], wkT[:, :], ident[0:CD, 0:CD]).then_inc(once("wk_turned"), 1)
            pe.wait_ge(once("wkT_ready"), 1)

            with pe.Fori(0, B) as b:
                pe.wait_ge(S("c_ready"), 1)
                for i in range(NT):
                    last = pe.transpose(bank[0][0:CD, i * P:(i + 1) * P], c[:, i, :], ident[:, :])
                last.then_inc(S("p0"), 1)
                pe.wait_ge(S("cT"), 1)
                mm(bank[1][0:CD, 0:N], wkT[:, :], cT[:, :], start=True, stop=True).then_inc(S("kvT_ps"), 1)
                for i in range(NT):
                    last = mm(bank[2][:, i * CD:(i + 1) * CD], cT[:, i * P:(i + 1) * P], wkT[:, :], start=True, stop=True)
                last.then_inc(S("kv_ps"), 1)
                pe.wait_ge(S("xn"), NT)
                four_transposes(pe, bank[3], xn, ident[:, :]).then_inc(S("xT_ps"), 1)
                pe.wait_ge(S("kv"), 1)
                pe.wait_ge(S("xT"), 1)
                for j in range(DC):
                    last = mm(bank[4][0:CD, 0:N], kv[:, j, :], xT[:, j, :], start=j == 0, stop=j == DC - 1)
                last.then_inc(S("oT_ps"), 1)
                pe.wait_ge(S("oT"), 1)
                pe.wait_ge(S("kvT"), 1)
                for i in range(NT):
                    mm(bank[5][:, i * N:(i + 1) * N], oT[:, i * P:(i + 1) * P], kvT[:, :],
                       start=True, stop=True).then_inc(S("sim_ps"), 1)
                pe.wait_ge(S("xn"), 2 * NT)
                four_transposes(pe, bank[6], xn, ident[:, :], True).then_inc(S("xT_ps"), 1)
                pe.wait_ge(S("xT"), 2)
                for i in range(NT):
                    for cc in range(DC):
                        last = mm(bank[7][:, i * E:(i + 1) * E], xT[:, cc, i * P:(i + 1) * P], rw[:, cc, :],
                                  start=cc == 0, stop=cc == DC - 1)
                last.then_inc(S("router_ps"), 1)
                pe.wait_ge(S("comb"), 1)
                for i in range(NT):
                    pe.transpose(bankb[0][:, i * P:(i + 1) * P], cst[:, i, 0:2, :], identb[:, :])
                    last = pe.transpose(bankb[1][0:E, i * P:(i + 1) * P], cst[:, i, 2, :], identb[:, :])
                last.then_inc(S("comb_ps"), 1)
                end_of_batch(pe)
                pe.wait_ge(once("batch_cleared"), b + 1)

            def up(k, h, u, pair):
                n = 3 * (2 * k + h)
                tok = slice(h * 512, (h + 1) * 512)
                if h == 0:
                    pe.wait_ge(once(f"experts_loaded{k}"), pair[1])
                if not (isinstance(u, int) and u == 0):
                    pe.wait_ge(once("gate_used"), u)
                    pe.wait_ge(once("hidden_made"), u)
                for cc in range(DC):
                    last = mm(bank[4 + n % 4][:, :], wg[k][:, cc, :], xnT[:, cc, tok], start=cc == 0, stop=cc == 1)
                last.then_inc(once("gate_made"), 1)
                for cc in range(DC):
                    last = mm(bank[4 + (n + 1) % 4][:, :], wu[k][:, cc, :], xnT[:, cc, tok], start=cc == 0, stop=cc == 1)
                last.then_inc(once("up_made"), 1)
                pe.wait_ge(once("up_used"), u + 2)
                mm(bank[4 + (n + 2) % 4][:, :], pick_hm[:, pair[0], :], comb_hm[:, tok], start=True, stop=False)
                mm(bank[4 + (n + 2) % 4][:, :], pick_l[:, pair[0], :], comb_l[:, tok], start=False, stop=True)\
                    .then_inc(once("weight_made"), 1)

            def down(k, h, u, first=False, last_pair=False):
                pe.wait_ge(once("hidden_made"), u + 2)
                for m in range(DC):
                    last = mm(bank[2 * m + h][:, :], wd[k][:, m * P:(m + 1) * P], hh[h][:, :],
                              start=first, stop=last_pair, skip_group_check=True)
                last.then_inc(once("hidden_used"), 1)

            pe.wait_ge(once("picks"), 2)
            for h in range(HALVES):
                for m in range(DC):
                    mm(bank[2 * m + h][:, :], zero_w[:, :], comb_hm[:, h * 512:(h + 1) * 512], start=True, stop=False,
                       skip_group_check=True)
            LOADS = 5 * 16
            pe.sem_inc(once("hidden_used"), 2)
            up(0, 0, 0, (0, LOADS))
            with pe.Fori(0, E // 2 // SLOTN) as t:
                for k in range(SLOTN):
                    for h in range(HALVES):
                        u = 2 * k + h
                        if u + 1 < 2 * SLOTN:
                            up((u + 1) // 2, (u + 1) % 2, t * 8 + (u + 1),
                               (t * SLOTN + (u + 1) // 2, t * LOADS + LOADS))
                        else:
                            up(0, 0, t * 8 + 8, (t * SLOTN + SLOTN, t * LOADS + 2 * LOADS))
                        down(k, h, t * 8 + u)
            T = E // 2 // SLOTN
            for u in range(2 * SLOTN):
                if u + 1 < 2 * SLOTN:
                    up((u + 1) // 2, (u + 1) % 2, T * 8 + u + 1, (T * SLOTN + (u + 1) // 2, (T + 1) * LOADS))
                down(u // 2, u % 2, T * 8 + u, last_pair=u // 2 == SLOTN - 1)
            pe.wait_ge(once("experts_out"), 2 * HALVES)
            for k in range(4):
                for i in range(2):
                    for m in range(DC):
                        last = pe.transpose(bank[4 + k][:, i * D + m * P:i * D + (m + 1) * P],
                                            yT[:, m, (2 * k + i) * P:(2 * k + i + 1) * P], ident[:, :])
                last.then_inc(once("y_rows"), 1)

            pe.wait_ge(once("stage_loaded"), 7 * 16)
            for g, (srcs, dst) in enumerate(PREP + PREPB):
                if g >= 4:
                    pe.wait_ge(once("prep_done"), g - 3)
                if g == len(PREP):
                    pe.wait_ge(once("abs_sums"), 2)
                    pe.wait_ge(once("xs_updated"), 4)
                    mm(bank[4][:, 0:2], ones[:, :], st[:, 0:2], start=True, stop=True).then_inc(once("abs_total"), 1)
                    pe.wait_ge(once("ternary"), 2)
                for j, src in enumerate(srcs):
                    if g < len(PREP):
                        last = pe.transpose(bank[g % 4][:, j * P:(j + 1) * P], src, ident[:, :])
                    else:
                        last = pe.transpose(bankb[g % 4][:, j * P:(j + 1) * P], src, identb[:, :])
                last.then_inc(once("prep_made"), 1)
            pe.wait_ge(once("mu_squared"), 1)
            for e in range(SE):
                for cc in range(DC):
                    last = mm(bank[5][:, e:e + 1], mu2[:, cc, e * SS:(e + 1) * SS], ones[:, 0:1], start=cc == 0, stop=cc == 1)
            last.then_inc(once("mu_sums"), 1)
            pe.wait_ge(once("mu_parts"), 1)
            pe.transpose(bankb[6][0:96, 0:P], mst[:, 0, :, :], identb[:, :]).then_inc(once("mu_partsT_ps"), 1)
            pe.wait_ge(once("mu_partsT"), 1)
            for e in range(SE):
                last = mm(bank[e // 4][:, e % 4 * SS:(e % 4 + 1) * SS], sel[:, e, :], cmT[:, :], start=True, stop=True)
            last.then_inc(once("mu_scales"), 1)
            pe.wait_ge(once("wo_loaded"), 16)
            for m in range(DC):
                for cc in range(DC):
                    last = mm(bank[7][:, m * R:(m + 1) * R], stage[2][:, cc * D + m * P:cc * D + (m + 1) * P], am[:, cc, :],
                              start=cc == 0, stop=cc == DC - 1)
            last.then_inc(once("wa_made"), 1)
            pe.wait_ge(once("prepared"), 2)

            def attention(L):
                H, G, HD, causal = ATTENTIONS[L]
                KV, K6 = H // G, 6 * HD
                pe.wait_ge(S("att_parts"), before(L, "parts") + 2)
                pe.wait_ge(S("att_parts_copied"), before(L, "parts_copied") + 4)
                groups = [(kst, g) for g in range(KV // 4)] + [(qst, g) for g in range(H // 4)]
                for g, (src, h4) in enumerate(groups):
                    if g >= 2:
                        pe.wait_ge(S("att_parts_out" + "ab"[g % 2]), before(L, "parts_out" + "ab"[g % 2]) + g // 2)
                    for j in range(4):
                        h = 4 * h4 + j
                        for i in range(NT):
                            last = pe.transpose(bankb[4 + g % 2][0:K6, j * N + i * P:j * N + (i + 1) * P],
                                                src[:, i, h * K6:(h + 1) * K6], identb[:, :])
                    last.then_inc(S("att_partsT"), 1)
                pe.wait_ge(S("att_parts_outa"), before(L, "parts_outa") + (len(groups) + 1) // 2)
                if len(groups) > 1:
                    pe.wait_ge(S("att_parts_outb"), before(L, "parts_outb") + len(groups) // 2)
                for i in range(NT):
                    for u in range(H // 2):
                        n = i * (H // 2) + u
                        if n >= 4:
                            pe.wait_ge(S("att_max"), before(L, "max") + n - 3)
                        if causal:
                            mm(bank[n % 4][:, :], identb[:, :], mask_q[:, i:i + 1, :].broadcast_to([P, 2, N]),
                               start=True, stop=False, skip_group_check=True)
                        for e in range(2):
                            h = 2 * u + e
                            last = mm(bank[n % 4][:, e * N:(e + 1) * N], qT[0:K6, h, i * P:(i + 1) * P], kT[0:K6, h // G, :],
                                      start=not causal, stop=True, skip_group_check=True)
                        last.then_inc(S("att_q_scores"), 1)
                pe.wait_ge(S("att_max_parts"), before(L, "max_parts") + 1)
                for i in range(NT):
                    last = pe.transpose(bankb[4][0:96, i * P:(i + 1) * P], mst[:, i, :, :], identb[:, :])
                last.then_inc(S("att_mT_ps"), 1)
                pe.wait_ge(S("att_mT"), before(L, "mT") + 1)
                pe.wait_ge(S("att_v"), before(L, "v") + ATT_COUNTS["v"][L])

                def weighted(n):
                    u, ti = n // 2, n % 2
                    pe.wait_ge(S("att_probs"), before(L, "probs") + n + 1)
                    strip = slice(32 * (u % 4), 32 * (u % 4) + 32)
                    if G > 1:
                        last = mm(bank[4 + u // 4][strip, :], vst[:, ti, 2 * u // G, :], prob[n % 4][:, :],
                                  start=ti == 0, stop=ti == 1, skip_group_check=True)
                    else:
                        for e in range(2):
                            last = mm(bank[4 + u // 4][strip, e * N:(e + 1) * N], vst[:, ti, 2 * u + e, :],
                                      prob[n % 4][:, e * N:(e + 1) * N], start=ti == 0 and e == 0, stop=ti == 1,
                                      skip_group_check=True)
                    last.then_inc(S("att_pv"), 1)

                for n in range(H):
                    u, ti = n // 2, n % 2
                    if n >= 4:
                        pe.wait_ge(S("att_probs"), before(L, "probs") + n - 3)
                    if causal:
                        mm(bank[n % 4][:, :], identb[:, :], mask_t[:, ti:ti + 1, :].broadcast_to([P, 2, N]),
                           start=True, stop=False, skip_group_check=True)
                    for e in range(2):
                        h = 2 * u + e
                        mm(bank[n % 4][:, e * N:(e + 1) * N], sel[:, h, :], mT[:, :], start=not causal, stop=False,
                           skip_group_check=True)
                        last = mm(bank[n % 4][:, e * N:(e + 1) * N], kT[0:K6, h // G, ti * P:(ti + 1) * P], qT[0:K6, h, :],
                                  start=False, stop=True, skip_group_check=True)
                    last.then_inc(S("att_scores"), 1)
                    if n >= 2:
                        weighted(n - 2)
                weighted(H - 2)
                weighted(H - 1)
                for ob in range(H // 8):
                    pe.wait_ge(S("att_oT"), before(L, "oT") + ob + 1)
                    for e in range(2):
                        for i in range(NT):
                            last = pe.transpose(bank[ob][:, (2 * e + i) * P:(2 * e + i + 1) * P],
                                                otr[:, ob, e * N + i * P:e * N + (i + 1) * P], ident[:, :])
                    last.then_inc(S("att_o"), 1)

            with pe.Fori(0, B) as b:
                attention("l1x")

                pe.wait_ge(S("l1f_in"), 1)
                four_transposes(pe, bank[0], tmp, ident[:, :]).then_inc(S("l1f_in_ps"), 1)
                pe.wait_ge(S("l1f_in"), 2)
                four_transposes(pe, bank[1], qr, ident[:, :]).then_inc(S("l1f_in_ps"), 1)
                pe.wait_ge(S("l1f_inT"), 1)
                for i in range(NT):
                    for cc in range(DC):
                        mm(bank[2 + i][:, :], xT[:, cc, i * P:(i + 1) * P], wqkvT[:, cc, 0:512], start=cc == 0, stop=cc == 1)
                    for cc in range(DC):
                        last = mm(bank[4][:, i * D:(i + 1) * D], xT[:, cc, i * P:(i + 1) * P], wqkvT[:, cc, 512:768],
                                  start=cc == 0, stop=cc == 1)
                    last.then_inc(S("qkv_ps"), 1)
                attention("l1f")
                pe.wait_ge(S("att_attn"), before("l1f", "attn") + NT)
                four_transposes(pe, bank[4], at, ident[:, :]).then_inc(S("l1f_atT_ps"), 1)
                pe.wait_ge(S("l1f_inT"), 2)
                for cc in range(DC):
                    mm(bank[5][0:R, N:2 * N], am[:, cc, :], hT[:, cc, :], start=cc == 0, stop=cc == 1)
                pe.wait_ge(S("l1f_atT"), 1)
                for cc in range(DC):
                    last = mm(bank[5][0:R, 0:N], wa[:, cc, :], atT[:, cc, :], start=cc == 0, stop=cc == 1)
                last.then_inc(S("mod_ps"), 1)
                pe.wait_ge(S("mh"), 1)
                for f in range(F1 // P):
                    if f >= 4:
                        pe.wait_ge(S("l1f_gu"), f - 3)
                    fs = slice(f * P, (f + 1) * P)
                    mm(bank[f % 4][:, 0:N], winT[:, 0, fs], hT[:, 0, :], start=True, stop=False)
                    mm(bank[f % 4][:, 0:N], winT[:, 1, fs], hT[:, 1, :], start=False, stop=False)
                    mm(bank[f % 4][:, 0:N], bm[:, fs], mh[:, :], start=False, stop=True)
                    mm(bank[f % 4][:, N:2 * N], wupT[:, 0, fs], hT[:, 0, :], start=True, stop=False)
                    mm(bank[f % 4][:, N:2 * N], wupT[:, 1, fs], hT[:, 1, :], start=False, stop=True)\
                        .then_inc(S("l1f_up"), 1)
                for i in range(NT):
                    for f in range(F1 // P):
                        pe.wait_ge(S("l1f_gu"), f + 1)
                        last = mm(bank[6 + i][:, 0:D], gu[:, f, i * P:(i + 1) * P], wdT[:, f, :],
                                  start=f == 0, stop=f == F1 // P - 1)
                    last.then_inc(S("l1f_down"), 1)

                pe.wait_ge(S("c_ready"), 1)
                for i in range(NT):
                    last = pe.transpose(bank[0][0:CD, i * P:(i + 1) * P], c[:, i, :], ident[:, :])
                last.then_inc(S("cT_ps"), 1)
                pe.wait_ge(S("cT"), 1)
                mm(bank[1][:, 0:N], l2wj[:, :], cT[:, :], start=True, stop=True).then_inc(S("sj_ps"), 1)

                pe.wait_ge(S("l2f_q1"), NT)
                for i in range(NT):
                    for cc in range(DC):
                        last = pe.transpose(bankb[0][:, cc * N + i * P:cc * N + i * P + P], q1[:, i, cc * P:(cc + 1) * P], identb[:, :])
                last.then_inc(S("q1T_ps"), 1)
                pe.wait_ge(S("q1T"), 1)
                for i in range(NT):
                    for hf in range(2):
                        for cc in range(DC):
                            last = mm(bank[1 + 2 * i + hf][:, :], q1T[:, cc, i * P:(i + 1) * P],
                                      w1qT[:, cc, hf * 512:(hf + 1) * 512], start=cc == 0, stop=cc == 1)
                    last.then_inc(S("l2f_up"), 1)
                for i in range(NT):
                    pe.wait_ge(S("l2f_q2"), i + 1)
                    for f in range(F1 // P):
                        last = pe.transpose(bankb[5 + i][:, f * P:(f + 1) * P], q2[:, i, f * P:(f + 1) * P], identb[:, :])
                    last.then_inc(S("q2T_ps"), 1)
                for i in range(NT):
                    pe.wait_ge(S("q2T"), i + 1)
                    for f in range(F1 // P):
                        last = mm(bank[7 * i][:, 0:D], q2T[:, f, i * P:(i + 1) * P], w2qT[:, f, :],
                                  start=f == 0, stop=f == F1 // P - 1)
                    last.then_inc(S("l2f_down"), 1)

                attention("l3x")
                pe.wait_ge(S("att_attn"), before("l3x", "attn") + NT)
                four_transposes(pe, bank[4], at, ident[:, :]).then_inc(S("l3x_atT_ps"), 1)
                pe.wait_ge(S("l3x_atT"), 1)
                for i in range(NT):
                    for cc in range(DC):
                        last = mm(bank[5][:, i * D:(i + 1) * D], atT[:, cc, i * P:(i + 1) * P], wcT[:, cc, :],
                                  start=cc == 0, stop=cc == 1)
                    last.then_inc(S("l3x_proj"), 1)

                pe.wait_ge(S("l3f_xn"), NT)
                four_transposes(pe, bank[0], tmp, ident[:, :]).then_inc(S("l3f_xT_ps"), 1)
                pe.wait_ge(S("l3f_xT"), 1)
                for i in range(NT):
                    for ch in range(4):
                        for cc in range(DC):
                            last = mm(bank[4 * i + ch][:, :], xT[:, cc, i * P:(i + 1) * P], mun[:, cc, ch * 512:(ch + 1) * 512],
                                      start=cc == 0, stop=cc == 1)
                        last.then_inc(S("logits_ps"), 1)
                for g in range(8):
                    pe.wait_ge(S("logits_out"), 8)
                    for j in range(2):
                        for i in range(NT):
                            last = pe.transpose(bank[g][:, j * N + i * P:j * N + (i + 1) * P],
                                                lg[:, i, (2 * g + j) * P:(2 * g + j + 1) * P], ident[:, :])
                    last.then_inc(S("logitsT_ps"), 1)
                pe.wait_ge(S("row_parts"), 1)
                pe.wait_ge(S("lT_raw"), 8)
                for i in range(NT):
                    last = pe.transpose(bankb[0][0:96, i * P:(i + 1) * P], mst[:, i, :, :], identb[:, :])
                last.then_inc(S("row_partsT_ps"), 1)
                pe.wait_ge(S("row_partsT"), 1)
                mm(bank[1][:, 0:N], sel[:, 0, :], mT3[:, :], start=True, stop=True).then_inc(S("row_max_all"), 1)
                pe.wait_ge(S("slot_parts"), 1)
                pe.transpose(bankb[2][0:96, 0:P], mst[:, 0, :, :], identb[:, :]).then_inc(S("slot_partsT_ps"), 1)
                pe.wait_ge(S("slot_partsT"), 1)
                for e in range(SE):
                    last = mm(bank[4 + e // 4][:, e % 4 * SS:(e % 4 + 1) * SS], sel[:, e, :], cmT[:, :], start=True, stop=True)
                    if e % 4 == 3:
                        last.then_inc(S("slot_max_all"), 1)
                pe.wait_ge(S("dispatch"), NT)
                for ch in range(4):
                    cs = slice(ch * 512, (ch + 1) * 512)
                    if ch >= 2:
                        pe.wait_ge(S("slot_sums_used"), ch - 1)
                    for i in range(NT):
                        last = mm(bank[ch % 2][:, :], ones[:, :], lg[:, i, cs], start=i == 0, stop=i == 1)
                    last.then_inc(S("slot_sums"), 1)
                    for m in range(DC):
                        n = 2 * ch + m
                        if n >= 4:
                            pe.wait_ge(S("slot_in"), n - 3)
                        for i in range(NT):
                            last = mm(bank[2 + n % 4][:, :], xl[:, i, m * P:(m + 1) * P], lg[:, i, cs], start=i == 0, stop=i == 1)
                        last.then_inc(S("slot_in_ps"), 1)
                pe.wait_ge(S("slot_in"), 8)
                for g in range(4):
                    if g >= 2:
                        pe.wait_ge(S("soft_hidden"), 4 * (g - 1))
                    for e in range(4 * g, 4 * g + 4):
                        for cc in range(DC):
                            last = mm(bank[6 + g % 2][0:SH, e % 4 * SS:(e % 4 + 1) * SS], w1s[:, cc, e, :],
                                      siT[:, cc, e * SS:(e + 1) * SS], start=cc == 0, stop=cc == 1)
                    last.then_inc(S("soft_up"), 1)
                pe.wait_ge(S("ones_rows"), 2)
                for g in range(8):
                    if g >= 4:
                        pe.wait_ge(S("slot_out"), g - 3)
                    pe.wait_ge(S("soft_hidden"), 2 * g + 2)
                    for j in range(2):
                        e = 2 * g + j
                        last = mm(bank[g % 4][:, j * D:(j + 1) * D], hsT[:, e * SS:(e + 1) * SS], w2a[:, e, :],
                                  start=True, stop=True)
                    last.then_inc(S("slot_out_ps"), 1)
                pe.wait_ge(S("slot_out"), 8)
                pe.wait_ge(S("combine"), 2)
                for i in range(NT):
                    for e in range(SE):
                        last = mm(bank[4 + i][:, 0:D + 1], lT[:, e, i * P:(i + 1) * P], so[:, e, :], start=e == 0, stop=e == SE - 1)
                    last.then_inc(S("soft_out"), 1)
                end_of_batch(pe)
                pe.wait_ge(once("batch_cleared"), b + (B + 1))

        @block.scalar
        def _(act):
            def copy(dst, src, scale=1.0):
                return act.activation(dst, src, ACT.Copy, scale=scale)

            act.wait_ge(once("first_loads"), 9 * 16)
            act.activation(gates[:, :], gates[:, :], ACT.Tanh).then_inc(once("gates_ready"), 1)
            act.wait_ge(once("wk_turned"), 1)
            copy(wkT[:, :], bank[0][0:CD, 0:CD]).then_inc(once("wkT_ready"), 1)
            with act.Fori(0, B) as b:
                act.wait_ge(S("p0"), 1)
                copy(cT[:, :], bank[0][0:CD, 0:N]).then_inc(S("cT"), 1)
                act.wait_ge(S("kvT_ps"), 1)
                act.activation(kvT[:, :], bank[1][0:CD, 0:N], ACT.Identity, bias=bk_col[:, 0:1]).then_inc(S("kvT"), 1)
                act.wait_ge(S("xT_ps"), 1)
                copy(xT[:, :, :], bank[3][:, :]).then_inc(S("xT"), 1)
                act.wait_ge(S("oT_ps"), 1)
                copy(oT[:, :], bank[4][0:CD, 0:N], scale=float(D) ** -0.5).then_inc(S("oT"), 1)
                for i in range(NT):
                    act.wait_ge(S("l0_ln_done"), i + 1)
                    act.activation(tmp[:, i, :], tmp[:, i, :], ACT.Exp, bias=nw[:, i:i + 1],
                                   accum_out=st[:, i:i + 1]).then_inc(S("l0_exp"), 1)
                act.wait_ge(S("xT_ps"), 2)
                copy(xT[:, :, :], bank[6][:, :]).then_inc(S("xT"), 1)
                for i in range(NT):
                    act.wait_ge(S("router_max"), i + 1)
                    act.activation(cb0[:, i, :], lg0[:, i, :], ACT.Exp, bias=nw[:, 2 + i:3 + i]).then_inc(S("router_exp"), 1)
                act.wait_ge(S("comb_ps"), 1)
                copy(comb_hm[:, bass.ts(b, N)], bankb[0][:, 0:N]).then_inc(S("act_last"), 1)
                copy(comb_l[0:E, bass.ts(b, N)], bankb[1][0:E, 0:N]).then_inc(S("act_last"), 1)
                act.wait_ge(S("act_last"), 2)
                end_of_batch(act)
                act.wait_ge(once("batch_cleared"), b + 1)

            def gate(k, u):
                n = 3 * k
                act.wait_ge(once("gate_made"), u + 1)
                act.wait_ge(once("up_used"), u + 1)
                act.activation(sg[k % 2][:, :], bank[4 + n % 4][:, :], ACT.Silu).then_inc(once("gate_used"), 1)

            act.wait_ge(once("picks"), 2)
            with act.Fori(0, PAIRS // SLOTN) as t:
                for k in range(2 * SLOTN):
                    gate(k, t * 8 + k)
            act.wait_ge(once("hidden_used"), 2 * PAIRS + 2)
            for h in range(HALVES):
                for m in range(DC):
                    copy(yT[:, m, h * 512:(h + 1) * 512], bank[2 * m + h][:, :]).then_inc(once("experts_out"), 1)
            act.wait_ge(once("prep_waits_experts"), 1)
            for g, (srcs, dst) in enumerate(PREP + PREPB):
                if g == len(PREP):
                    act.wait_ge(once("stage_loaded"), 9 * 16)
                    for k in range(2):
                        act.activation(tern[k][:, :], stage[k][:, :], ACT.Abs, accum_out=st[:, k:k + 1]).then_inc(once("abs_sums"), 1)
                act.wait_ge(once("prep_made"), g + 1)
                src = (bank if g < len(PREP) else bankb)[g % 4]
                copy(dst, src[:, 0:len(srcs) * P]).then_inc(once("prep_done"), 1)
            act.wait_ge(once("mu_partsT_ps"), 1)
            copy(cmT[:, :], bankb[6][0:96, 0:P]).then_inc(once("mu_partsT"), 1)

            def attention(L):
                H, G, HD, causal = ATTENTIONS[L]
                KV, K6 = H // G, 6 * HD
                dsts = [kT[0:K6, 4 * g:4 * g + 4, :] for g in range(KV // 4)] + [qT[0:K6, 4 * g:4 * g + 4, :] for g in range(H // 4)]
                for g in range(0, len(dsts), 2):
                    act.wait_ge(S("att_partsT"), before(L, "partsT") + g + 1)
                    copy(dsts[g], bankb[4][0:K6, :]).then_inc(S("att_parts_outa"), 1)
                act.wait_ge(S("att_mT_ps"), before(L, "mT_ps") + 1)
                copy(mT[:, :], bankb[4][0:96, 0:N]).then_inc(S("att_mT"), 1)
                for n in range(H):
                    act.wait_ge(S("att_scores"), before(L, "scores") + n + 1)
                    if n >= 4:
                        act.wait_ge(S("att_pv"), before(L, "pv") + n - 3)
                    act.activation(prob[n % 4][:, :], bank[n % 4][:, :], ACT.Exp).then_inc(S("att_probs"), 1)
                for ob in range(H // 8):
                    act.wait_ge(S("att_pv"), before(L, "pv") + 8 * ob + 8)
                    copy(otr[:, ob, :], bank[4 + ob][:, :]).then_inc(S("att_oT"), 1)

            with act.Fori(0, B) as b:
                attention("l1x")
                act.wait_ge(S("l1f_in_ps"), 1)
                copy(xT[:, :, :], bank[0][:, :]).then_inc(S("l1f_inT"), 1)
                act.wait_ge(S("l1f_in_ps"), 2)
                copy(hT[:, :, :], bank[1][:, :]).then_inc(S("l1f_inT"), 1)
                for i in range(NT):
                    act.wait_ge(S("qkv_ps"), i + 1)
                    copy(qf[:, i, :], bank[2 + i][:, 0:D], scale=0.25).then_inc(S("qk"), 1)
                    copy(kf[:, i, :], bank[2 + i][:, D:2 * D]).then_inc(S("qk"), 1)
                attention("l1f")
                act.wait_ge(S("l1f_atT_ps"), 1)
                copy(atT[:, :, :], bank[4][:, :]).then_inc(S("l1f_atT"), 1)
                act.wait_ge(S("mod_ps"), 1)
                act.activation(modT[:, :], bank[5][0:R, 0:N], ACT.Tanh).then_inc(S("modT"), 1)
                for f in range(F1 // P):
                    act.wait_ge(S("l1f_up"), f + 1)
                    if f >= 2:
                        act.wait_ge(S("l1f_gu"), f - 1)
                    act.activation(sgf[f % 2][:, :], bank[f % 4][:, 0:N], ACT.Silu).then_inc(S("l1f_silu"), 1)
                act.wait_ge(S("cT_ps"), 1)
                copy(cT[:, :], bank[0][0:CD, 0:N]).then_inc(S("cT"), 1)
                act.wait_ge(S("sj_ps"), 1)
                act.wait_ge(S("si"), 1)
                for i in range(NT):
                    act.activation(tmp[:, i, :], bank[1][:, 0:N], ACT.Sigmoid, bias=st[:, 8 + i:9 + i]).then_inc(S("l2x_sig"), 1)
                act.wait_ge(S("q1T_ps"), 1)
                copy(q1T[:, :, :], bankb[0][:, 0:512]).then_inc(S("q1T"), 1)
                for i in range(NT):
                    act.wait_ge(S("l2f_pre"), i + 1)
                    act.activation(h2[:, i, :], h2[:, i, :], ACT.Silu).then_inc(S("l2f_silu"), 1)
                for i in range(NT):
                    act.wait_ge(S("l2f_silu"), i + 1)
                    act.activation(h2[:, i, :], h2[:, i, :], ACT.Gelu).then_inc(S("l2f_gelu"), 1)
                for i in range(NT):
                    act.wait_ge(S("l2f_ln"), i + 1)
                    act.activation(h2s[:, i, :], h2[:, i, :], ACT.Square, accum_out=st[:, 4 + i:5 + i]).then_inc(S("l2f_sq"), 1)
                for i in range(NT):
                    act.wait_ge(S("q2T_ps"), i + 1)
                    copy(q2T[:, :, i * P:(i + 1) * P], bankb[5 + i][:, :].rearrange("p (f t) -> p f t", t=P)).then_inc(S("q2T"), 1)
                attention("l3x")
                act.wait_ge(S("l3x_atT_ps"), 1)
                copy(atT[:, :, :], bank[4][:, :]).then_inc(S("l3x_atT"), 1)
                act.wait_ge(S("l3f_xT_ps"), 1)
                copy(xT[:, :, :], bank[0][:, :]).then_inc(S("l3f_xT"), 1)
                for g in range(8):
                    act.wait_ge(S("logits_ps"), g + 1)
                    copy(lg[:, g // 4, g % 4 * 512:(g % 4 + 1) * 512], bank[g][:, :]).then_inc(S("logits_out"), 1)
                for g in range(8):
                    act.wait_ge(S("logitsT_ps"), g + 1)
                    copy(lT[:, 2 * g:2 * g + 2, :], bank[g][:, :]).then_inc(S("lT_raw"), 1)
                act.wait_ge(S("row_partsT_ps"), 1)
                copy(mT3[:, :], bankb[0][0:96, 0:N]).then_inc(S("row_partsT"), 1)
                act.wait_ge(S("slot_partsT_ps"), 1)
                copy(cmT[:, :], bankb[2][0:96, 0:P]).then_inc(S("slot_partsT"), 1)
                for i in range(NT):
                    act.wait_ge(S("logits_less_max"), 4 * (i + 1))
                    act.activation(lg[:, i, :], lg[:, i, :], ACT.Exp).then_inc(S("dispatch"), 1)
                for j in range(2):
                    act.wait_ge(S("lT_less_max"), j + 1)
                    act.activation(lT[:, 8 * j:8 * j + 8, :], lT[:, 8 * j:8 * j + 8, :], ACT.Exp).then_inc(S("combine"), 1)
                for e in range(SE):
                    act.wait_ge(S("soft_up"), e // 4 + 1)
                    act.activation(hsT[0:SH, e * SS:(e + 1) * SS], bank[6 + e // 4 % 2][0:SH, e % 4 * SS:(e % 4 + 1) * SS],
                                   ACT.Gelu, bias=b1T[:, e:e + 1]).then_inc(S("soft_hidden"), 1)
                for g in range(8):
                    act.wait_ge(S("slot_out_ps"), g + 1)
                    copy(so[:, 2 * g:2 * g + 2, 0:D], bank[g % 4][:, :].rearrange("p (j d) -> p j d", j=2)).then_inc(S("slot_out"), 1)
                act.wait_ge(S("slot_out"), 8)
                end_of_batch(act)
                act.wait_ge(once("batch_cleared"), b + (B + 1))

        @block.vector
        def _(dve):
            V = nc.vector
            ts, tt, stt = V.tensor_scalar, V.tensor_tensor, V.scalar_tensor_tensor

            def rsqrt(step, out_, v):
                k = v.shape[1]
                w = nw[:, 0:k] if k <= 4 else cmr[:, 0:k]
                step(ts(w.bitcast(I32), v.bitcast(I32), 1, None, ALU.arith_shift_right))
                step(ts(out_.bitcast(I32), w.bitcast(I32), -1, 0x5F3759DF, ALU.mult, ALU.add))
                for _ in range(3):
                    step(tt(w, out_, v, ALU.mult))
                    step(stt(out=w, in0=w, scalar=-0.5, in1=out_, op0=ALU.mult, op1=ALU.mult))
                    step(stt(out=out_, in0=w, scalar=1.5, in1=out_, op0=ALU.add, op1=ALU.mult))

            def stats(step, src, eps):
                for i in range(NT):
                    step(V.bn_stats(bn[:, i, :], src(i)))
                    step(V.bn_aggr(mv[:, i, :], bn[:, i, :]))
                step(ts(ve[:, 0:NT], mv[:, :, 1], eps, None, ALU.add))
                rsqrt(step, rs[:, 0:NT], ve[:, 0:NT])

            def layernorm(step, out_, scale=1.0):
                stats(step, lambda i: x[:, i, :], 1e-5)
                if scale != 1.0:
                    step(ts(rs[:, 0:NT], rs[:, 0:NT], scale, None, ALU.mult))
                for i in range(NT):
                    step(ts(out_[:, i, :], x[:, i, :], mv[:, i, 0:1], rs[:, i:i + 1], ALU.subtract, ALU.mult))

            def three_parts(step, parts, v, left):
                step(V.tensor_copy(parts[0], v))
                step(tt(left, v, parts[0], ALU.subtract))
                step(V.tensor_copy(parts[1], left))
                step(tt(parts[2], left, parts[1], ALU.subtract))

            dve.wait_ge(once("x_loaded"), 32)
            dve.wait_ge(once("first_loads"), 9 * 16)
            dve.wait_ge(once("gates_ready"), 1)
            with dve.Fori(0, B) as b:
                step = Steps(dve, S("dve_step"))
                dve.wait_ge(S("x_ready"), 1)
                layernorm(step, xn)
                dve.sem_inc(S("xn"), NT)
                dve.wait_ge(S("kv_ps"), 1)
                tt(kv[:, :, :], bank[2][:, 0:P].rearrange("p (i d) -> p i d", i=NT),
                   bk_row[:, :].unsqueeze(1).broadcast_to([P, NT, CD]), ALU.add).then_inc(S("kv"), 1)
                dve.wait_ge(S("sim_ps"), 2)
                stats(step, lambda i: bank[5][:, i * N:(i + 1) * N], 1e-6)
                for i in range(NT):
                    step(ts(tmp[:, i, :], bank[5][:, i * N:(i + 1) * N], mv[:, i, 0:1], rs[:, i:i + 1], ALU.subtract, ALU.mult))
                    step(tt(tmp[:, i, :], tmp[:, i, :], rowsD["L0_xattn_ln_gamma"][:, :], ALU.mult))
                    step(tt(tmp[:, i, :], tmp[:, i, :], rowsD["L0_xattn_ln_beta"][:, :], ALU.add))
                    step(V.reduce_max(ve[:, i:i + 1], tmp[:, i, :], AX))
                    ts(nw[:, i:i + 1], ve[:, i:i + 1], -1.0, None, ALU.mult).then_inc(S("l0_ln_done"), 1)
                dve.wait_ge(S("l0_exp"), 2)
                step(V.reciprocal(st[:, 2:4], st[:, 0:2]))
                step(ts(st[:, 2:4], st[:, 2:4], gates[:, 0:1], None, ALU.mult))
                for i in range(NT):
                    step(stt(out=x[:, i, :], in0=tmp[:, i, :], scalar=st[:, 2 + i:3 + i], in1=x[:, i, :], op0=ALU.mult, op1=ALU.add))
                dve.sem_inc(S("x_done"), 1)
                layernorm(step, xn)
                dve.sem_inc(S("xn"), NT)
                dve.wait_ge(S("router_ps"), 1)
                step(V.tensor_copy(lg0[:, :, :], bank[7][:, 0:NT * E].rearrange("p (i e) -> p i e", i=NT)))
                step(V.memset(lb0[:, :, E:E + TOPK], -BIG))
                step(tt(lb0[:, :, 0:E], lg0[:, :, :], rb[:, :].unsqueeze(1).broadcast_to([P, NT, E]), ALU.add))
                for i in range(NT):
                    step(V.reduce_max(ve[:, i:i + 1], lg0[:, i, :], AX))
                    ts(nw[:, 2 + i:3 + i], ve[:, i:i + 1], -1.0, None, ALU.mult).then_inc(S("router_max"), 1)
                    step(V.max(m8[:, i, :], lb0[:, i, 0:E]))
                    step(V.memset(m8[:, i, TOPK:8], -BIG))
                    step(V.match_replace(lr0[:, i, :], m8[:, i, :], lb0[:, i, :], BIG))
                dve.wait_ge(S("router_exp"), 2)
                step(tt(ct0[:, :, :], lr0[:, :, 0:E], lb0[:, :, 0:E], ALU.not_equal))
                step(tt(ct0[:, :, :], ct0[:, :, :], cb0[:, :, :], ALU.mult))
                step(V.reduce_sum(st[:, 4:6], ct0[:, :, :], AX))
                step(V.reciprocal(st[:, 6:8], st[:, 4:6]))
                for i in range(NT):
                    step(ts(ct0[:, i, :], ct0[:, i, :], st[:, 6 + i:7 + i], None, ALU.mult))
                three_parts(step, [cst[:, :, k, :] for k in range(3)], ct0[:, :, :], cb0[:, :, :])
                dve.sem_inc(S("comb"), 1)
                end_of_batch(dve)
                dve.wait_ge(once("batch_cleared"), b + 1)

            step = Steps(dve, once("dve_step_prep"))
            dve.wait_ge(once("picks"), 2)
            dve.sem_inc(once("hidden_made"), 1)
            dve.sem_inc(once("up_used"), 2)
            with dve.Fori(0, PAIRS // SLOTN) as t:
                for k in range(2 * SLOTN):
                    n, u = 3 * k, t * 8 + k
                    dve.wait_ge(once("gate_used"), u + 1)
                    dve.wait_ge(once("up_made"), u + 1)
                    tt(hu[k % 2][:, :], bank[4 + (n + 1) % 4][:, :], sg[k % 2][:, :], ALU.mult).then_inc(once("up_used"), 1)
                    dve.wait_ge(once("up_used"), u + 3)
                    dve.wait_ge(once("weight_made"), u + 1)
                    dve.wait_ge(once("hidden_used"), u + 1)
                    tt(hh[k % 2][:, :], bank[4 + (n + 2) % 4][:, :], hu[k % 2][:, :], ALU.mult).then_inc(once("hidden_made"), 1)
            for k in range(4):
                dve.wait_ge(once("y_rows"), k + 1)
                rows = xs[:, 2 * k:2 * k + 2, :]
                stt(out=rows, in0=bank[4 + k][:, :].rearrange("p (i d) -> p i d", i=2), scalar=gates[:, 4:5], in1=rows,
                    op0=ALU.mult, op1=ALU.add).then_inc(once("xs_updated"), 1)
            dve.wait_ge(once("rest_loads"), REST * 16)
            dve.wait_ge(once("prep_waits_experts"), 1)
            step(tt(mu2[:, :, :], mun[:, :, :], mun[:, :, :], ALU.mult))
            dve.sem_inc(once("mu_squared"), 1)
            dve.wait_ge(once("abs_total"), 1)
            step(ts(wdq[:, :], bank[4][:, 0:2], 1.0 / (F1 * D), 1e-5, ALU.mult, ALU.max))
            step(V.reciprocal(st[:, 2:4], wdq[:, :]))
            for k in range(2):
                w = stage[k][:, :]
                step(ts(w, w, st[:, 2 + k:3 + k], -1.0, ALU.mult, ALU.max))
                step(ts(w, w, 1.0, ROUND, ALU.min, ALU.add))
                ts(tern[k][:, :], w, ROUND, None, ALU.subtract).then_inc(once("ternary"), 1)
            dve.wait_ge(once("mu_sums"), 1)
            step(V.tensor_copy(cmx[:, :], bank[5][:, 0:SE]))
            rsqrt(step, rbc[:, 0:SE], cmx[:, :])
            step(tt(cmx[:, :], cmx[:, :], rbc[:, 0:SE], ALU.mult))
            step(ts(cmx[:, :], cmx[:, :], 1e-12, None, ALU.max))
            step(V.reciprocal(rbc[:, 0:SE], cmx[:, :]))
            three_parts(step, [mst[:, 0, k, 0:SE] for k in range(3)], rbc[:, 0:SE], cmr[:, 0:SE])
            dve.sem_inc(once("mu_parts"), 1)
            dve.wait_ge(once("mu_scales"), 1)
            for ch in range(4):
                for cc in range(DC):
                    m = mun[:, cc, ch * 512:(ch + 1) * 512]
                    step(tt(m, m, bank[ch][:, :], ALU.mult))
            dve.sem_inc(once("prepared"), 1)
            dve.wait_ge(once("wa_made"), 1)
            step(V.tensor_copy(wa[:, :, :], bank[7][:, 0:DC * R].rearrange("p (m r) -> p m r", m=DC)))
            step(V.tensor_copy(l2wj[:, 1:P], l2wj[:, 0:1].broadcast_to([CD, P - 1])))
            dve.sem_inc(once("prepared"), 1)
            dve.wait_ge(once("xs_updated"), 4)

            def attention(step, L, q, k):
                H, G, HD, causal = ATTENTIONS[L]
                KV, K6 = H // G, 6 * HD

                def slot(t, heads, s):
                    v = t[:, :, 0:heads * K6].rearrange("p i (h s d) -> p s i h d", h=heads, s=6)
                    return v[:, s]
                for t, heads, src, slots in ((kst, KV, k, (0, 1, 4)), (qst, H, q, (0, 2, 5))):
                    src = src.rearrange("p i (h d) -> p i h d", h=heads)
                    left = qr[:, :, 0:heads * HD].rearrange("p i (h d) -> p i h d", h=heads)
                    three_parts(step, [slot(t, heads, s) for s in slots], src, left)
                    dve.sem_inc(S("att_parts"), 1)
                ng = KV // 4 + H // 4
                dsts = [kT[0:K6, 4 * g:4 * g + 4, :] for g in range(KV // 4)] + [qT[0:K6, 4 * g:4 * g + 4, :] for g in range(H // 4)]
                for g in range(1, ng, 2):
                    dve.wait_ge(S("att_partsT"), before(L, "partsT") + g + 1)
                    V.tensor_copy(dsts[g], bankb[5][0:K6, :].rearrange("p (h n) -> p h n", h=4)).then_inc(S("att_parts_outb"), 1)
                for i in range(NT):
                    for u in range(H // 2):
                        n = i * (H // 2) + u
                        dve.wait_ge(S("att_q_scores"), before(L, "q_scores") + n + 1)
                        V.reduce_max(mx[:, i, 2 * u:2 * u + 2], bank[n % 4][:, :].rearrange("p (e t) -> p e t", e=2), AX)\
                            .then_inc(S("att_max"), 1)
                dve.wait_ge(S("att_max"), before(L, "max") + H)
                step(ts(mx[:, :, 0:H], mx[:, :, 0:H], -1.0, None, ALU.mult))
                three_parts(step, [mst[:, :, s, 0:H] for s in range(3)], mx[:, :, 0:H], mr[:, :, 0:H])
                dve.sem_inc(S("att_max_parts"), 1)
                for ob in range(H // 8):
                    dve.wait_ge(S("att_o"), before(L, "o") + ob + 1)
                    o = bank[ob][:, :].rearrange("p (e i j d) -> p e i j d", e=2, i=NT, j=4)
                    step(V.reciprocal(rc[:, ob, :], bank[ob][:, :].rearrange("p (k d) -> p k d", d=32)[:, :, HD]))
                    r = rc[:, ob, :].rearrange("p (e i j) -> p e i j", e=2, i=NT)
                    for i in range(NT):
                        for e in range(2):
                            dst = at[:, i, ob * 8 * HD:(ob + 1) * 8 * HD].rearrange("p (j e d) -> p e j d", e=2, d=HD)
                            step(tt(dst[:, e], o[:, e, i, :, 0:HD], r[:, e, i, :].unsqueeze(2).broadcast_to([P, 4, HD]), ALU.mult))
                dve.sem_inc(S("att_attn"), NT)

            def residual(step, y, g, done=None):
                for i in range(NT):
                    step(stt(out=x[:, i, :], in0=y(i), scalar=gates[:, g:g + 1], in1=x[:, i, :], op0=ALU.mult, op1=ALU.add))

            def quantised(step, k, src, n, out_, ssum, big, out_sem):
                pass

            with dve.Fori(0, B) as b:
                step = Steps(dve, S("dve_step"))
                dve.wait_ge(S("x_ready"), 1)
                dve.wait_ge(S("c_ready"), 1)
                layernorm(step, xn, 8 ** -0.5)
                dve.sem_inc(S("l1x_begun"), 1)
                attention(step, "l1x", xn[:, :, :], c[:, :, :])
                residual(step, lambda i: at[:, i, :], 1)

                layernorm(step, xn)
                for i in range(NT):
                    step(V.tensor_tensor_reduce(out=tmp[:, i, :], in0=xn[:, i, :], in1=xn[:, i, :], scale=1.0, scalar=0.0,
                                                op0=ALU.mult, op1=ALU.add, accum_out=st[:, i:i + 1]))
                step(ts(ve[:, 0:NT], st[:, 0:NT], 1.0 / D, 1e-6, ALU.mult, ALU.add))
                rsqrt(step, rs[:, 0:NT], ve[:, 0:NT])
                for w, dst in (("L1_ffn_ln1_w", tmp), ("L1_ffn_ln2_w", qr)):
                    for i in range(NT):
                        step(stt(out=dst[:, i, :], in0=xn[:, i, :], scalar=rs[:, i:i + 1], in1=rowsD[w][:, :],
                                 op0=ALU.mult, op1=ALU.mult))
                    dve.sem_inc(S("l1f_in"), 1)
                dve.wait_ge(S("l1f_in_ps"), 2)
                dve.wait_ge(S("qkv_ps"), 2)
                V.tensor_copy(vst[:, :, :, 0:16], bank[4][:, :].rearrange("p (i h d) -> p i h d", i=NT, d=16)).then_inc(S("att_v"), 1)
                dve.wait_ge(S("qk"), 4)
                attention(step, "l1f", qf[:, :, :], kf[:, :, :])
                dve.wait_ge(S("modT"), 1)
                stt(out=mh[:, :], in0=modT[:, :], scalar=0.1, in1=bank[5][0:R, N:2 * N], op0=ALU.mult, op1=ALU.mult)\
                    .then_inc(S("mh"), 1)
                for f in range(F1 // P):
                    dve.wait_ge(S("l1f_silu"), f + 1)
                    tt(gu[:, f, :], bank[f % 4][:, N:2 * N], sgf[f % 2][:, :], ALU.mult).then_inc(S("l1f_gu"), 1)
                dve.wait_ge(S("l1f_down"), 2)
                for i in range(NT):
                    step(tt(xn[:, i, :], xn[:, i, :], bank[6 + i][:, 0:D], ALU.add))
                residual(step, lambda i: xn[:, i, :], 5)

                for i in range(NT):
                    step(V.tensor_tensor_reduce(out=qr[:, i, 0:CD], in0=c[:, i, :], in1=l2wi[:, :], scale=1.0, scalar=0.0,
                                                op0=ALU.mult, op1=ALU.add, accum_out=st[:, 8 + i:9 + i]))
                step(ts(st[:, 8:10], st[:, 8:10], l2b[:, 0:1], None, ALU.add))
                dve.sem_inc(S("si"), 1)
                layernorm(step, xn)
                dve.wait_ge(S("l2x_sig"), 2)
                for i in range(NT):
                    step(ts(tmp[:, i, :], tmp[:, i, :], 0.6, None, ALU.mult))
                    step(stt(out=tmp[:, i, :], in0=xn[:, i, :], scalar=1.0 - 0.6, in1=tmp[:, i, :], op0=ALU.mult, op1=ALU.add))
                residual(step, lambda i: tmp[:, i, :], 2)

                def factors(i, k):
                    pass

                layernorm(step, xn)
                for i in range(NT):
                    step(V.tensor_tensor_reduce(out=tmp[:, i, :], in0=xn[:, i, :], in1=xn[:, i, :], scale=1.0, scalar=0.0,
                                                op0=ALU.mult, op1=ALU.add, accum_out=st[:, 4 + i:5 + i]))

                def quantise(src, n, k, dst, work, name):
                    step(ts(ve[:, 0:NT], st[:, 4:6], 1.0 / n, 1e-5, ALU.mult, ALU.add))
                    rsqrt(step, rs[:, 0:NT], ve[:, 0:NT])
                    for i in range(NT):
                        step(V.reduce_max(st[:, 6 + i:7 + i], src(i), AX, apply_absolute_value=True))
                    step(tt(st[:, 6:8], st[:, 6:8], rs[:, 0:NT], ALU.mult))
                    step(ts(st[:, 6:8], st[:, 6:8], 1e-5, None, ALU.max))
                    step(ts(st[:, 10:12], st[:, 6:8], 1.0 / 127.0, wdq[:, k:k + 1], ALU.mult, ALU.mult))
                    step(V.reciprocal(st[:, 6:8], st[:, 6:8]))
                    step(stt(out=rs[:, 0:NT], in0=st[:, 6:8], scalar=127.0, in1=rs[:, 0:NT], op0=ALU.mult, op1=ALU.mult))
                    for i in range(NT):
                        step(ts(work(i), src(i), rs[:, i:i + 1], -128.0, ALU.mult, ALU.max))
                        step(ts(work(i), work(i), 127.0, ROUND, ALU.min, ALU.add))
                        ts(dst(i), work(i), ROUND, None, ALU.subtract).then_inc(S(name), 1)

                quantise(lambda i: xn[:, i, :], D, 0, lambda i: q1[:, i, :], lambda i: tmp[:, i, :], "l2f_q1")
                for i in range(NT):
                    dve.wait_ge(S("l2f_up"), i + 1)
                    for hf in range(2):
                        cs = slice(hf * 512, (hf + 1) * 512)
                        step(stt(out=h2[:, i, cs], in0=bank[1 + 2 * i + hf][:, :], scalar=st[:, 10 + i:11 + i],
                                 in1=rowsF["L2_ffn_b1"][:, cs], op0=ALU.mult, op1=ALU.add))
                    dve.sem_inc(S("l2f_pre"), 1)
                for i in range(NT):
                    dve.wait_ge(S("l2f_gelu"), i + 1)
                    for hf in range(2):
                        step(V.bn_stats(bn[:, 2 * i + hf, :], h2[:, i, hf * 512:(hf + 1) * 512]))
                    step(V.bn_aggr(mv[:, i, :], bn[:, 2 * i:2 * i + 2, :].rearrange("p a s -> p (a s)")))
                step(ts(ve[:, 0:NT], mv[:, :, 1], 1e-5, None, ALU.add))
                rsqrt(step, rs[:, 0:NT], ve[:, 0:NT])
                for i in range(NT):
                    step(ts(h2[:, i, :], h2[:, i, :], mv[:, i, 0:1], rs[:, i:i + 1], ALU.subtract, ALU.mult))
                    step(tt(h2[:, i, :], h2[:, i, :], rowsF["L2_ffn_ln_g"][:, :], ALU.mult))
                    step(tt(h2[:, i, :], h2[:, i, :], rowsF["L2_ffn_ln_b"][:, :], ALU.add))
                    dve.sem_inc(S("l2f_ln"), 1)
                dve.wait_ge(S("l2f_sq"), 2)
                quantise(lambda i: h2[:, i, :], F1, 1, lambda i: q2[:, i, :], lambda i: h2s[:, i, :], "l2f_q2")
                for i in range(NT):
                    dve.wait_ge(S("l2f_down"), i + 1)
                    step(stt(out=tmp[:, i, :], in0=bank[7 * i][:, 0:D], scalar=st[:, 10 + i:11 + i],
                             in1=rowsD["L2_ffn_b2"][:, :], op0=ALU.mult, op1=ALU.add))
                residual(step, lambda i: tmp[:, i, :], 6)

                layernorm(step, xn, 0.25)
                dve.sem_inc(S("l3x_begun"), 1)
                attention(step, "l3x", xn[:, :, :], c[:, :, :])
                dve.wait_ge(S("l3x_proj"), 2)
                for i in range(NT):
                    step(tt(tmp[:, i, :], bank[5][:, i * D:(i + 1) * D], rowsD["L3_xattn_bc"][:, :], ALU.add))
                residual(step, lambda i: tmp[:, i, :], 3)

                layernorm(step, xn)
                dve.sem_inc(S("l3f_begun"), 1)
                for i in range(NT):
                    step(tt(xl[:, i, :], xn[:, i, :], rowsD["L3_ffn_gamma"][:, :], ALU.mult))
                    step(tt(xl[:, i, :], xl[:, i, :], rowsD["L3_ffn_beta"][:, :], ALU.add))
                    step(V.tensor_tensor_reduce(out=tmp[:, i, :], in0=xl[:, i, :], in1=xl[:, i, :], scale=1.0, scalar=0.0,
                                                op0=ALU.mult, op1=ALU.add, accum_out=st[:, i:i + 1]))
                rsqrt(step, rs[:, 0:NT], st[:, 0:NT])
                step(tt(st[:, 0:NT], st[:, 0:NT], rs[:, 0:NT], ALU.mult))
                step(ts(st[:, 0:NT], st[:, 0:NT], 1e-12, None, ALU.max))
                step(V.reciprocal(rs[:, 0:NT], st[:, 0:NT]))
                step(ts(rs[:, 0:NT], rs[:, 0:NT], sc_scale[:, 0:1], None, ALU.mult))
                for i in range(NT):
                    ts(tmp[:, i, :], xl[:, i, :], rs[:, i:i + 1], None, ALU.mult).then_inc(S("l3f_xn"), 1)
                for g in range(8):
                    dve.wait_ge(S("logits_out"), g + 1)
                    V.reduce_max(rmx[:, g // 4, g % 4:g % 4 + 1], lg[:, g // 4, g % 4 * 512:(g % 4 + 1) * 512], AX).then_inc(S("logits_max"), 1)
                dve.wait_ge(S("logits_max"), 8)
                step(V.reduce_max(ve[:, 0:NT], rmx[:, :, :], AX))
                step(ts(ve[:, 0:NT], ve[:, 0:NT], -1.0, None, ALU.mult))
                three_parts(step, [mst[:, :, s, 0] for s in range(3)], ve[:, 0:NT], nw[:, 0:NT])
                dve.sem_inc(S("row_parts"), 1)
                for g in range(8):
                    dve.wait_ge(S("lT_raw"), g + 1)
                    V.reduce_max(cmx[:, 2 * g:2 * g + 2], lT[:, 2 * g:2 * g + 2, :], AX).then_inc(S("slots_max"), 1)
                dve.wait_ge(S("row_partsT_ps"), 1)
                dve.wait_ge(S("slots_max"), 8)
                step(ts(cmx[:, :], cmx[:, :], -1.0, None, ALU.mult))
                three_parts(step, [mst[:, 0, s, 0:SE] for s in range(3)], cmx[:, :], cmr[:, :])
                dve.sem_inc(S("slot_parts"), 1)
                dve.wait_ge(S("row_max_all"), 1)
                step(V.tensor_copy(rbc[:, :], bank[1][:, 0:N]))
                for i in range(NT):
                    for ch in range(4):
                        dve.wait_ge(S("slot_max_all"), ch + 1)
                        lc = lg[:, i, ch * 512:(ch + 1) * 512]
                        tt(lc, lc, bank[4 + ch][:, :], ALU.add).then_inc(S("logits_less_max"), 1)
                for j in range(2):
                    lc = lT[:, 8 * j:8 * j + 8, :]
                    dve.wait_ge(S("lT_raw"), 8)
                    tt(lc, lc, rbc[:, :].unsqueeze(1).broadcast_to([P, 8, N]), ALU.add).then_inc(S("lT_less_max"), 1)
                for ch in range(4):
                    dve.wait_ge(S("slot_sums"), ch + 1)
                    step(V.reciprocal(rsum[ch % 2][:, :], bank[ch % 2][:, :]))
                    dve.sem_inc(S("slot_sums_used"), 1)
                    for m in range(DC):
                        n = 2 * ch + m
                        dve.wait_ge(S("slot_in_ps"), n + 1)
                        tt(siT[:, m, ch * 512:(ch + 1) * 512], bank[2 + n % 4][:, :], rsum[ch % 2][:, :], ALU.mult)\
                            .then_inc(S("slot_in"), 1)
                for i in range(NT):
                    dve.wait_ge(S("soft_out"), i + 1)
                    step(V.reciprocal(st[:, i:i + 1], bank[4 + i][:, D:D + 1]))
                    step(ts(st[:, i:i + 1], st[:, i:i + 1], gates[:, 7:8], None, ALU.mult))
                    stt(out=x[:, i, :], in0=bank[4 + i][:, 0:D], scalar=st[:, i:i + 1], in1=x[:, i, :],
                        op0=ALU.mult, op1=ALU.add).then_inc(S("x_final"), 1)
                dve.wait_ge(S("x_final"), 2)
                end_of_batch(dve)
                dve.wait_ge(once("batch_cleared"), b + (B + 1))

        @block.gpsimd
        def _(pool):
            G = nc.gpsimd
            step = Steps(pool, once("pool_step"))

            def select(t, compare, fill, base, pattern, m=1):
                step(G.affine_select(out=t, in_=t, compare_op=compare, fill=fill, base=base, pattern=pattern, channel_multiplier=m))

            step(G.memset(ident[:, :], 0.0))
            select(ident[:, :], ALU.not_equal, 1.0, 0, [[-1, P]])
            pool.sem_inc(once("consts"), 1)
            step(G.tensor_copy(identb[:, :], ident[:, :]))
            pool.sem_inc(once("consts"), 1)
            step(G.memset(ones[:, :], 1.0))
            pool.sem_inc(once("consts"), 1)
            step(G.memset(sel[:, :, :], 0.0))
            for k in range(3):
                select(sel[:, :, :], ALU.not_equal, 1.0, -32 * k, [[-1, 32], [0, P]])
            pool.sem_inc(once("consts"), 1)
            step(G.memset(mask_q[:, :, :], 0.0))
            select(mask_q[:, :, :], ALU.is_ge, MASKED, 0, [[P, NT], [-1, N]])
            step(G.memset(mask_t[:, :, :], 0.0))
            select(mask_t[:, :, :], ALU.is_ge, MASKED, 0, [[-P, NT], [1, N]], -1)
            step(G.memset(mst[:, :, :, :], 0.0))
            step(G.memset(vst[:, :, :, :], 0.0))
            pool.sem_inc(once("consts"), 1)
            step(G.memset(zero_w[:, :], 0.0))
            step(G.memset(pick_hm[:, :, :], 0.0))
            step(G.memset(pick_l[:, :, :], 0.0))
            for k in range(2):
                t = pick_hm[:, 0:E // 2, :].rearrange("p q (e f) -> p q e f", e=2)
                select(t, ALU.not_equal, 1.0, -E * k, [[-2, E // 2], [-1, 2], [0, F]])
            t = pick_l[:, 0:E // 2, :].rearrange("p q (e f) -> p q e f", e=2)
            select(t, ALU.not_equal, 1.0, 0, [[-2, E // 2], [-1, 2], [0, F]])
            step(G.memset(pick_l[E:E + 1, E // 2:PAIRS, :], 1.0))
            step(G.memset(comb_l[E:E + 1, :], 1.0))
            pool.wait_ge(once("x_loaded"), 32)
            with pool.Fori(0, B) as b:
                step = Steps(pool, S("pool_step_b"))
                G.tensor_copy(c[:, :, :], ctxs[:, bass.ts(b, NT), :]).then_inc(S("c_ready"), 1)
                G.tensor_copy(x[:, :, :], xs[:, bass.ts(b, NT), :]).then_inc(S("x_ready"), 1)
                pool.wait_ge(S("x_done"), 1)
                step(G.tensor_copy(xs[:, bass.ts(b, NT), :], x[:, :, :]))
                pool.wait_ge(S("xT"), 2)
                step(G.tensor_copy(xnT[:, :, bass.ts(b, N)], xT[:, :, :]))
                pool.wait_ge(once("batch_arrived"), b * 3 + 3)
                pool.sem_inc(once("all_arrived"), 1)
                clear(pool)
                pool.sem_inc(once("batch_cleared"), 1)
            pool.sem_inc(once("picks"), 2)
            pool.wait_ge(once("hidden_used"), 2 * PAIRS + 2)
            pool.sem_inc(once("prep_waits_experts"), 1)
            pool.wait_ge(once("prepared"), 2)
            pool.wait_ge(once("xs_updated"), 4)

            def attention(step, L, v):
                H, GG, HD, causal = ATTENTIONS[L]
                KV, K6 = H // GG, 6 * HD

                def slot(t, heads, s, i):
                    v = t[:, i, 0:heads * K6].rearrange("p (h s d) -> p s h d", h=heads, s=6)
                    return v[:, s]
                G.memset(vst[:, :, 0:KV, HD:HD + 1], 1.0).then_inc(S("att_v"), 1)
                if v is not None:
                    G.tensor_copy(vst[:, :, 0:KV, 0:HD], v.rearrange("p i (h d) -> p i h d", h=KV)).then_inc(S("att_v"), 1)
                else:
                    pool.sem_inc(S("att_v"), 1)
                for n, (t, heads, copies) in enumerate(((kst, KV, ((2, 0), (5, 0), (3, 1))), (qst, H, ((1, 0), (4, 0), (3, 2))))):
                    pool.wait_ge(S("att_parts"), before(L, "parts") + n + 1)
                    for i in range(NT):
                        for to, fro in copies:
                            last = step(G.tensor_copy(slot(t, heads, to, i), slot(t, heads, fro, i)))
                        pool.sem_inc(S("att_parts_copied"), 1)

            with pool.Fori(0, B) as b:
                step = Steps(pool, S("pool_step_b"))
                G.tensor_copy(c[:, :, :], ctxs[:, bass.ts(b, NT), :]).then_inc(S("c_ready"), 1)
                G.tensor_copy(x[:, :, :], xs[:, bass.ts(b, NT), :]).then_inc(S("x_ready"), 1)
                pool.wait_ge(S("c_ready"), 1)
                pool.wait_ge(S("l1x_begun"), 1)
                attention(step, "l1x", c[:, :, :])
                pool.wait_ge(S("l1f_in"), 2)
                attention(step, "l1f", None)
                pool.wait_ge(S("l3x_begun"), 1)
                attention(step, "l3x", c[:, :, :])
                pool.wait_ge(S("l3f_begun"), 1)
                G.memset(hsT[SH:SH + 1, :], 1.0).then_inc(S("ones_rows"), 1)
                pool.wait_ge(S("ones_rows"), 1)
                pool.wait_ge(S("slot_in_ps"), 8)
                G.memset(so[:, :, D:D + 1], 1.0).then_inc(S("ones_rows"), 1)
                pool.wait_ge(once("batch_arrived"), b * 4 + (3 * B + 4))
                pool.sem_inc(once("all_arrived"), 1)
                clear(pool)
                pool.sem_inc(once("batch_cleared"), 1)


_INS = ['x', 'ctx_512', 'g_xattn', 'g_ffn', 'L0_xattn_W_k', 'L0_xattn_b_k', 'L0_xattn_ln_gamma', 'L0_xattn_ln_beta',
        'L0_ffn_router_w', 'L0_ffn_router_bias', 'L0_ffn_wg', 'L0_ffn_wu', 'L0_ffn_wd', 'L0_ffn_swg', 'L0_ffn_swu',
        'L0_ffn_swd', 'L1_ffn_ln1_w', 'L1_ffn_ln2_w', 'L1_ffn_Wq', 'L1_ffn_Wk', 'L1_ffn_Wv', 'L1_ffn_Wo', 'L1_ffn_A',
        'L1_ffn_B', 'L1_ffn_W_in_base', 'L1_ffn_W_up_base', 'L1_ffn_W_down', 'L2_xattn_W', 'L2_xattn_b', 'L2_ffn_w1',
        'L2_ffn_b1', 'L2_ffn_ln_g', 'L2_ffn_ln_b', 'L2_ffn_w2', 'L2_ffn_b2', 'L3_xattn_Wc', 'L3_xattn_bc',
        'L3_ffn_gamma', 'L3_ffn_beta', 'L3_ffn_mu', 'L3_ffn_scale', 'L3_ffn_W1', 'L3_ffn_b1', 'L3_ffn_W2', 'L3_ffn_b2']


def kernel(**inputs):
    import numpy as _np
    import concourse.bacc as _bacc
    from concourse import mybir as _mybir
    from concourse.bass_utils import run_bass_kernel_spmd as _run

    nc = _bacc.Bacc("TRN2", target_bir_lowering=False, num_devices=1)
    arrays, args = {}, {}
    for name in _INS:
        a = _np.ascontiguousarray(inputs[name])
        arrays[f"in_{name}_dram"] = a
        args[name] = nc.dram_tensor(f"in_{name}_dram", a.shape, _mybir.dt.from_np(a.dtype), kind="ExternalInput").ap()
    out = nc.dram_tensor("out_0_dram", (B, N, D), _mybir.dt.float32, kind="ExternalOutput").ap()
    flamingo(nc, args, out)
    r = _run(nc, [arrays], core_ids=[0])
    return r.results[0]["out_0_dram"]
```

```python
from contextlib import ExitStack

import numpy as np

import concourse.bass as bass
from concourse import mybir

P = 128
ALU = mybir.AluOpType
ACT = mybir.ActivationFunctionType
F32 = mybir.dt.float32
FR = mybir.dt.float32r
BF16 = mybir.dt.bfloat16
I32 = mybir.dt.int32
AX = mybir.AxisListType.X

B, N, D = 4, 256, 256
NT = N // P
DC = D // P
CD = 64
E, F = 64, 64
TOPK = 4
PAIRS = E // 2 + 4
F1 = 1024
R = 16
SE, SS, SH = 16, 128, 64
SLOTS = SE * SS
MASKED = -1e30
BIG = 3e38
ROUND = 1.5 * 2.0 ** 23
TOKENS = B * N
HALVES = TOKENS // 512
ATTENTIONS = {"l1x": (32, 4, 8, False), "l1f": (16, 1, 16, True), "l3x": (16, 4, 16, False)}


ATT_COUNTS = {}
for _L, (_H, _G, _HD, _) in ATTENTIONS.items():
    _K, _GR = _H // _G // 4, _H // 8
    for _name, _n in (("parts", 2), ("partsT", _K + 2 * _GR), ("left0", (_K + 11 * _GR + 1) // 2),
                      ("left1", (_K + 11 * _GR) // 2), ("q_scores", _H), ("max_parts", _GR), ("mT_ps", _GR),
                      ("v", 2 if _G > 1 else 3), ("probs", _H), ("scores", _H), ("pv", _H),
                      ("oT", _GR), ("o", _GR), ("attn", NT)):
        ATT_COUNTS.setdefault(_name, {})[_L] = _n


def before(L, name):
    order = list(ATTENTIONS)
    return sum(ATT_COUNTS[name][k] for k in order[:order.index(L)])


class Steps:

    def __init__(self, eng, sem):
        self.eng, self.sem, self.n = eng, sem, 0

    def __call__(self, *instructions):
        for ins in instructions:
            ins.then_inc(self.sem, 1)
        self.n += len(instructions)
        self.eng.wait_ge(self.sem, self.n)


def flamingo(nc, I, out):
    with ExitStack() as ctx:
        sems, batch_sems = {}, []

        def once(name):
            if name not in sems:
                sems[name] = ctx.enter_context(nc.semaphore(name))
            return sems[name]

        def S(name):
            if name not in sems:
                sems[name] = ctx.enter_context(nc.semaphore(name))
                batch_sems.append(sems[name])
            return sems[name]

        top = [(nc.sbuf_base + 63) // 64 * 64]
        high = [0]

        def sb(name, shape, dt=F32):
            size = int(np.prod(shape[1:])) * (2 if dt == BF16 else 4)
            t = nc.alloc_sbuf_tensor_at(name, list(shape), dt, offset=top[0])
            top[0] += (size + 31) // 32 * 32
            high[0] = max(high[0], top[0])
            return t

        bank = [ctx.enter_context(nc.psum_tensor(f"bank{k}", [P, 512], F32)) for k in range(8)]
        bankb = [k[:, :].bitcast(BF16) for k in bank]

        xs = sb("xs", [P, B * NT, D])
        ctxs = sb("ctxs", [P, B * NT, CD])
        ident = sb("ident", [P, P])
        identb = sb("identb", [P, P], BF16)
        ones = sb("ones", [P, P])
        sel = sb("sel", [96, 32, P], BF16)
        mask_q = sb("mask_q", [P, NT, N], BF16)
        mask_t = sb("mask_t", [P, NT, N], BF16)
        gates = sb("gates", [P, 8])
        mst = sb("mst", [P, NT, 3, 32], BF16)
        vst = sb("vst", [P, NT, 16, 32])
        wkT = sb("wkT", [CD, CD])
        bk_col = sb("bk_col", [CD, 1])
        bk_row = sb("bk_row", [P, CD])
        sc_scale = sb("sc_scale", [P, 1])
        l2b = sb("l2b", [P, 1])
        l2wi = sb("l2wi", [P, CD])
        l2wj = sb("l2wj", [CD, P])
        at_wqkvT = top[0]
        wqkvT = sb("wqkvT", [P, DC, 3 * D])
        wcT = sb("wcT", [P, DC, D])
        early = top[0]
        winT = sb("winT", [P, DC, F1])
        wupT = sb("wupT", [P, DC, F1])
        wdT = sb("wdT", [P, F1 // P, D])
        w1qT = sb("w1qT", [P, DC, F1], BF16)
        w2qT = sb("w2qT", [P, F1 // P, D], BF16)
        mun = sb("mun", [P, DC, SLOTS])
        w1s = sb("w1s", [P, DC, SE, SH])
        w2a = sb("w2a", [SH + 1, SE, D + 1])
        rowsD = {n: sb("row_" + n, [P, D]) for n in
                 ("L0_xattn_ln_gamma", "L0_xattn_ln_beta", "L1_ffn_ln1_w", "L1_ffn_ln2_w", "L2_ffn_b2",
                  "L3_xattn_bc", "L3_ffn_gamma", "L3_ffn_beta")}
        rowsF = {n: sb("row_" + n, [P, F1]) for n in ("L2_ffn_b1", "L2_ffn_ln_g", "L2_ffn_ln_b")}
        wa = sb("wa", [P, DC, R])
        am = sb("am", [P, DC, R])
        bm = sb("bm", [R, F1])
        b1 = sb("b1", [P, SE, SH])
        wdq = sb("wdq", [P, 2])
        at_x = top[0]
        x = sb("x", [P, NT, D])
        c = sb("c", [P, NT, CD])
        xn = sb("xn", [P, NT, D])
        xT = sb("xT", [P, DC, N])
        cT = sb("cT", [CD, N])
        tmp = sb("tmp", [P, NT, D])
        bn = sb("bn", [P, 4, 6])
        mv = sb("mv", [P, NT, 2])
        ve = sb("ve", [P, 4])
        rs = sb("rs", [P, 4])
        nw = sb("nw", [P, 4])
        st = sb("st", [P, 16])
        rbc = sb("rbc", [P, N])
        cmx = sb("cmx", [P, SE])
        cmr = sb("cmr", [P, SE])
        cmT = sb("cmT", [96, P], BF16)
        region = top[0]

        xh = sb("xh", [P, DC, TOKENS], FR)
        comb_hm = sb("comb_hm", [P, TOKENS], BF16)
        comb_l = sb("comb_l", [E + 1, TOKENS], BF16)
        pick_hm = sb("pick_hm", [P, PAIRS, P], BF16)
        pick_l = sb("pick_l", [E + 1, PAIRS, P], BF16)
        SLOTN = 4
        wraw = [sb(f"wraw{k}", [P, 3, D]) for k in range(SLOTN)]
        wg = [w[:, 0, :].rearrange("p (c f) -> p c f", c=DC) for w in wraw]
        wu = [w[:, 1, :].rearrange("p (c f) -> p c f", c=DC) for w in wraw]
        wd = [w[:, 2, :] for w in wraw]
        sg = [sb(f"sg{k}", [P, 512]) for k in range(2)]
        hu = [sb(f"hu{k}", [P, 512]) for k in range(2)]
        hh = [sb(f"hh{k}", [P, 512]) for k in range(2)]
        kvT = sb("kvT", [CD, N])
        kv = sb("kv", [P, NT, CD])
        oT = sb("oT", [CD, N])
        rw = sb("rw", [P, DC, E])
        rb = sb("rb", [P, E])
        lg0 = sb("lg0", [P, NT, E])
        lb0 = sb("lb0", [P, NT, E + TOPK])
        lr0 = sb("lr0", [P, NT, E + TOPK])
        cb0 = sb("cb0", [P, NT, E])
        ct0 = sb("ct0", [P, NT, E])
        cst = sb("cst", [P, NT, 3, E], BF16)
        m8 = sb("m8", [P, NT, 8])
        zero_w = sb("zero_w", [P, P], BF16)
        after_experts = top[0]
        top[0] = region
        yT = sb("yT", [P, DC, TOKENS])
        top[0] = early
        xlo = sb("xlo", [P, DC, TOKENS], FR)
        wh = [sb(f"wh{k}", [P, 3, D], FR) for k in range(2)]
        wl = [sb(f"wl{k}", [P, 3, D], FR) for k in range(2)]
        hhi = [sb(f"hhi{k}", [P, 512], FR) for k in range(2)]
        hlo = [sb(f"hlo{k}", [P, 512], FR) for k in range(2)]
        assert top[0] <= early + 32 * 1024
        l2_raw = []
        for k, place in enumerate((at_wqkvT, at_x)):
            top[0] = place
            l2_raw.append(sb(f"l2_raw{k}", [P, 2048]))
        top[0] = after_experts

        top[0] = region
        top[0] += DC * TOKENS * 4
        stage = [sb(f"stage{k}", [P, 2048]) for k in range(4)]
        wo = sb("wo", [P, DC, D])
        mu2 = sb("mu2", [P, DC, SLOTS])
        top[0] = region
        tern = [sb(f"tern{k}", [P, 2048], BF16) for k in range(2)]
        top[0] = region
        qst = sb("qst", [P, NT, 6 * D], BF16)
        kst = sb("kst", [P, NT, 6 * D], BF16)
        qT = sb("qT", [96, 32, N], BF16)
        kT = sb("kT", [96, 16, N], BF16)
        prob = [sb(f"prob{k}", [P, 512]) for k in range(4)]
        mx = sb("mx", [P, NT, 32])
        mr = sb("mr", [P, NT, 32])
        qr = sb("qr", [P, NT, D])
        mT = sb("mT", [96, N], BF16)
        otr = sb("otr", [P, 4, 512])
        after_otr = top[0]
        top[0] -= 4 * 512 * 4
        qf = sb("qf", [P, NT, D])
        kf = sb("kf", [P, NT, D])
        top[0] = after_otr
        rc = sb("rc", [P, 4, 16])
        at = sb("at", [P, NT, D])
        atT = sb("atT", [P, DC, N])
        hT = sb("hT", [P, DC, N])
        modT, mh = rbc[0:R, :], cT[0:R, :]
        top[0] = region
        sgf = [sb(f"sgf{k}", [P, N]) for k in range(2)]
        gu = sb("gu", [P, F1 // P, N])
        top[0] = region
        h2 = sb("h2", [P, NT, F1])
        h2s = sb("h2s", [P, NT, F1])
        q1 = sb("q1", [P, NT, D], BF16)
        q1T = sb("q1T", [P, DC, N], BF16)
        q2 = sb("q2", [P, NT, F1], BF16)
        q2T = sb("q2T", [P, F1 // P, N], BF16)
        top[0] = region
        aT = sb("aT", [SH + 1, SE, N])
        top[0] = region
        lg = sb("lg", [P, NT, SLOTS])
        lT = sb("lT", [P, SE, N])
        xw = sb("xw", [P, NT, SE, SH + 1])
        hs = sb("hs", [P, SE, SH + 1])
        xl = sb("xl", [P, NT, D])
        rmx = sb("rmx", [P, NT, 4])
        mT3 = sb("mT3", [96, N], BF16)
        assert high[0] <= nc.sbuf_usable_end

        block = ctx.enter_context(nc.Block())

        def blocks_of(w, rows, cols, dst):
            groups = []
            for ic in range(cols // P):
                for oc0 in range(0, rows // P, 4):
                    n = min(4, rows // P - oc0)
                    groups.append(([w[:, (oc0 + j) * cols + ic * P:(oc0 + j) * cols + ic * P + P] for j in range(n)],
                                   dst(ic, oc0 * P, n * P)))
            return groups

        PREP = []
        for k in range(3):
            PREP += blocks_of(stage[0][:, k * 512:(k + 1) * 512], D, D,
                              lambda ic, o, n, k=k: wqkvT[:, ic, k * D + o:k * D + o + n])
        PREP += blocks_of(stage[0][:, 1536:2048], D, D, lambda ic, o, n: wcT[:, ic, o:o + n])
        PREP += blocks_of(stage[1], F1, D, lambda ic, o, n: winT[:, ic, o:o + n])
        FIRST_STAGES = len(PREP)
        PREP += blocks_of(stage[2], F1, D, lambda ic, o, n: wupT[:, ic, o:o + n])
        PREP += blocks_of(stage[3], D, F1, lambda ic, o, n: wdT[:, ic, o:o + n])
        PREPB = blocks_of(tern[0], F1, D, lambda ic, o, n: w1qT[:, ic, o:o + n])
        PREPB += blocks_of(tern[1], D, F1, lambda ic, o, n: w2qT[:, ic, o:o + n])

        REST = len(rowsD) - 2 + len(rowsF) + 12

        def clear(eng):
            nums = sorted(s.num for s in batch_sems)
            first = nums[0]
            for a, b in zip(nums, nums[1:] + [None]):
                if b != a + 1:
                    eng.sem_clear(range(first, a + 1))
                    first = b

        def end_of_batch(eng):
            eng.sem_inc(once("batch_arrived"), 1)

        @block.sync
        def _(sp):
            W = sp.dma_start
            ld = once("first_loads")
            W(xs[:, :, :], I["x"].rearrange("b (i p) d -> p (b i) d", p=P)).then_inc(once("x_loaded"), 16)
            W(ctxs[:, :, :], I["ctx_512"].rearrange("b (i p) d -> p (b i) d", p=P)).then_inc(once("x_loaded"), 16)
            W(wkT[:, :], I["L0_xattn_W_k"]).then_inc(ld, 16)
            W(bk_col[:, :], I["L0_xattn_b_k"].rearrange("(p a) -> p a", a=1)).then_inc(ld, 16)
            W(bk_row[:, :], I["L0_xattn_b_k"].partition_broadcast(P)).then_inc(ld, 16)
            for n in ("L0_xattn_ln_gamma", "L0_xattn_ln_beta"):
                W(rowsD[n][:, :], I[n].partition_broadcast(P)).then_inc(ld, 16)
            W(gates[:, 0:4], I["g_xattn"].partition_broadcast(P)).then_inc(ld, 16)
            W(gates[:, 4:8], I["g_ffn"].partition_broadcast(P)).then_inc(ld, 16)
            W(rw[:, :, :], I["L0_ffn_router_w"].rearrange("(p c) e -> p c e", c=DC)).then_inc(ld, 16)
            W(rb[:, :], I["L0_ffn_router_bias"].partition_broadcast(P)).then_inc(ld, 16)

            def load_experts(k, pair, shared):
                sem = once(f"experts_loaded{k}")
                for w, name in ((wg[k], "g"), (wu[k], "u")):
                    for e in range(2):
                        if shared is None:
                            src = I["L0_ffn_w" + name].rearrange("(q e) (p c) f -> e q p c f", e=2, c=DC)[e, pair]
                        else:
                            src = I["L0_ffn_sw" + name].rearrange("s (p c) (q e f) -> s q e p c f", c=DC, e=2, f=F)[
                                shared // 2, shared % 2, e]
                        W(w[:, :, e * F:(e + 1) * F], src).then_inc(sem, 16)
                if shared is None:
                    W(wd[k][:, :], I["L0_ffn_wd"].rearrange("(q e) f d -> q (e f) d", e=2)[pair]).then_inc(sem, 16)
                else:
                    W(wd[k][:, :], I["L0_ffn_swd"].rearrange("s (q p) d -> (s q) p d", p=P)[shared]).then_inc(sem, 16)

            for k in range(SLOTN):
                load_experts(k, k, None)
            rest = once("rest_loads")
            for n in list(rowsD)[2:]:
                W(rowsD[n][:, :], I[n].partition_broadcast(P)).then_inc(rest, 16)
            for n in rowsF:
                W(rowsF[n][:, :], I[n].partition_broadcast(P)).then_inc(rest, 16)
            W(sc_scale[:, :], I["L3_ffn_scale"].partition_broadcast(P)).then_inc(rest, 16)
            W(l2b[:, :], I["L2_xattn_b"].partition_broadcast(P)).then_inc(rest, 16)
            W(l2wi[:, :], I["L2_xattn_W"][0, 0:CD].partition_broadcast(P)).then_inc(rest, 16)
            W(l2wj[:, 0:1], I["L2_xattn_W"].rearrange("a (t p) -> t p a", p=CD)[1]).then_inc(rest, 16)
            W(mun[:, :, :], I["L3_ffn_mu"].rearrange("(c p) e s -> p c (e s)", p=P)).then_inc(rest, 16)
            for cc in range(DC):
                W(w1s[:, cc, :, :], I["L3_ffn_W1"].rearrange("e (c p) h -> c p e h", p=P)[cc]).then_inc(rest, 16)
            W(w2a[0:SH, :, 0:D], I["L3_ffn_W2"].rearrange("e h d -> h e d")).then_inc(rest, 16)
            W(w2a[SH:SH + 1, :, 0:D], I["L3_ffn_b2"].rearrange("(a e) d -> a e d", a=1)).then_inc(rest, 16)
            W(am[:, :, :], I["L1_ffn_A"].rearrange("(c p) r -> p c r", p=P)).then_inc(rest, 16)
            W(bm[:, :], I["L1_ffn_B"]).then_inc(rest, 16)
            W(b1[:, :, :], I["L3_ffn_b1"].partition_broadcast(P)).then_inc(rest, 16)
            def stage_load(to, n, cols, sem):
                W(to[:, :].rearrange("p (o i) -> p o i", i=cols),
                  I[n].rearrange("(o p) i -> p o i", p=P)).then_inc(sem, 16)

            with sp.Fori(0, E // 2 // SLOTN - 1) as t:
                for k in range(SLOTN):
                    sp.wait_ge(once("weights_split"), t * SLOTN + (k + 1))
                    sp.sem_inc(once("slot_free"), 1)
                    load_experts(k, t * SLOTN + (SLOTN + k), None)
            sp.wait_ge(once("picks"), 2)
            stage_load(l2_raw[0], "L2_ffn_w1", D, once("l2_loaded"))
            stage_load(l2_raw[1], "L2_ffn_w2", F1, once("l2_loaded"))
            for k in range(SLOTN):
                sp.wait_ge(once("weights_split"), E // 2 - SLOTN + k + 1)
                load_experts(k, None, k)
            sp.wait_ge(once("hidden_used"), 2 * PAIRS + 4)
            sp.wait_ge(once("experts_out"), 2 * HALVES)
            stg = once("stage_loaded")
            for k, n in enumerate(("Wq", "Wk", "Wv")):
                W(stage[0][:, k * 512:(k + 1) * 512].rearrange("p (o i) -> p o i", i=D),
                  I["L1_ffn_" + n].rearrange("(o p) i -> p o i", p=P)).then_inc(stg, 16)
            W(stage[0][:, 1536:2048].rearrange("p (o i) -> p o i", i=D),
              I["L3_xattn_Wc"].rearrange("(o p) i -> p o i", p=P)).then_inc(stg, 16)
            stage_load(stage[1], "L1_ffn_W_in_base", D, stg)
            stg = once("stage_rest_loaded")
            stage_load(stage[2], "L1_ffn_W_up_base", D, stg)
            stage_load(stage[3], "L1_ffn_W_down", F1, stg)
            W(wo[:, :, :], I["L1_ffn_Wo"].rearrange("(o p) i -> p o i", p=P)).then_inc(stg, 16)
            with sp.Fori(0, B) as b:
                sp.wait_ge(once("x_final"), b * NT + NT)
                sp.sem_inc(once("next_batch"), 1)
                W(out.rearrange("b (i p) d -> b p i d", p=P)[b], xs[:, bass.ts(b, NT), :]).then_inc(once("x_out"), 16)
            sp.wait_ge(once("x_out"), B * 16)

        def four_transposes(pe, dst, src, ident_, strided=False):
            for cc in range(DC):
                for i in range(NT):
                    s = src[:, i, cc:D:DC] if strided else src[:, i, cc * P:(cc + 1) * P]
                    last = pe.transpose(dst[:, cc * N + i * P:cc * N + i * P + P], s, ident_)
            return last

        @block.tensor
        def _(pe):
            mm = pe.matmul
            pe.wait_ge(once("first_loads"), 9 * 16)
            pe.wait_ge(once("consts"), 2)
            pe.transpose(bank[0][0:CD, 0:CD], wkT[:, :], ident[0:CD, 0:CD]).then_inc(once("wk_turned"), 1)
            pe.wait_ge(once("wkT_ready"), 1)

            with pe.Fori(0, B) as b:
                pe.wait_ge(S("c_ready"), 1)
                for i in range(NT):
                    last = pe.transpose(bank[0][0:CD, i * P:(i + 1) * P], c[:, i, :], ident[:, :])
                last.then_inc(S("p0"), 1)
                pe.wait_ge(S("cT"), 1)
                mm(bank[1][0:CD, 0:N], wkT[:, :], cT[:, :], start=True, stop=True).then_inc(S("kvT_ps"), 1)
                for i in range(NT):
                    last = mm(bank[2][:, i * CD:(i + 1) * CD], cT[:, i * P:(i + 1) * P], wkT[:, :], start=True, stop=True)
                last.then_inc(S("kv_ps"), 1)
                pe.wait_ge(S("xn"), NT)
                four_transposes(pe, bank[3], xn, ident[:, :]).then_inc(S("xT_ps"), 1)
                pe.wait_ge(S("kv"), 1)
                pe.wait_ge(S("xT"), 1)
                for j in range(DC):
                    last = mm(bank[4][0:CD, 0:N], kv[:, j, :], xT[:, j, :], start=j == 0, stop=j == DC - 1)
                last.then_inc(S("oT_ps"), 1)
                pe.wait_ge(S("oT"), 1)
                pe.wait_ge(S("kvT"), 1)
                for i in range(NT):
                    mm(bank[5][:, i * N:(i + 1) * N], oT[:, i * P:(i + 1) * P], kvT[:, :],
                       start=True, stop=True).then_inc(S("sim_ps"), 1)
                pe.wait_ge(S("xn"), 2 * NT)
                four_transposes(pe, bank[6], xn, ident[:, :], True).then_inc(S("xT_ps"), 1)
                pe.wait_ge(S("xT"), 2)
                for i in range(NT):
                    for cc in range(DC):
                        last = mm(bank[7][:, i * E:(i + 1) * E], xT[:, cc, i * P:(i + 1) * P], rw[:, cc, :],
                                  start=cc == 0, stop=cc == DC - 1)
                last.then_inc(S("router_ps"), 1)
                pe.wait_ge(S("comb"), 1)
                for i in range(NT):
                    pe.transpose(bankb[0][:, i * P:(i + 1) * P], cst[:, i, 0:2, :], identb[:, :])
                    last = pe.transpose(bankb[1][0:E, i * P:(i + 1) * P], cst[:, i, 2, :], identb[:, :])
                last.then_inc(S("comb_ps"), 1)
                end_of_batch(pe)
                pe.wait_ge(once("batch_cleared"), b + 1)

            def up(k, h, u, pair):
                n = 3 * (2 * k + h)
                tok = slice(h * 512, (h + 1) * 512)
                if h == 0:
                    pe.wait_ge(once("weights_split"), pair + 1)
                if not (isinstance(u, int) and u == 0):
                    pe.wait_ge(once("gate_used"), u)
                    pe.wait_ge(once("hidden_made"), u)
                for m, made in ((0, "gate_made"), (1, "up_made")):
                    for j, (w, v) in enumerate(((wh, xh), (wh, xlo), (wl, xh))):
                        for cc in range(DC):
                            last = mm(bank[4 + (n + m) % 4][:, :], w[k % 2][:, m, cc * P:(cc + 1) * P], v[:, cc, tok],
                                      start=j == 0 and cc == 0, stop=j == 2 and cc == 1)
                    last.then_inc(once(made), 1)
                pe.wait_ge(once("up_used"), u + 2)
                mm(bank[4 + (n + 2) % 4][:, :], pick_hm[:, pair, :], comb_hm[:, tok], start=True, stop=False)
                mm(bank[4 + (n + 2) % 4][:, :], pick_l[:, pair, :], comb_l[:, tok], start=False, stop=True)\
                    .then_inc(once("weight_made"), 1)

            def down(k, h, u, last_pair=False):
                pe.wait_ge(once("hidden_made"), u + 2)
                for m in range(DC):
                    for j, (w, v) in enumerate(((wh, hhi), (wl, hhi), (wh, hlo))):
                        last = mm(bank[2 * m + h][:, :], w[k % 2][:, 2, m * P:(m + 1) * P], v[h][:, :],
                                  start=False, stop=last_pair and j == 2, skip_group_check=True)
                last.then_inc(once("hidden_used"), 1)

            pe.wait_ge(once("consts"), 5)
            pe.wait_ge(once("picks"), 2)
            for h in range(HALVES):
                for m in range(DC):
                    mm(bank[2 * m + h][:, :], zero_w[:, :], comb_hm[:, h * 512:(h + 1) * 512], start=True, stop=False,
                       skip_group_check=True)
            up(0, 0, 0, 0)
            with pe.Fori(0, E // 2 // SLOTN) as t:
                for k in range(SLOTN):
                    for h in range(HALVES):
                        u = 2 * k + h
                        if u + 1 < 2 * SLOTN:
                            up((u + 1) // 2, (u + 1) % 2, t * 8 + (u + 1), t * SLOTN + (u + 1) // 2)
                        else:
                            up(0, 0, t * 8 + 8, t * SLOTN + SLOTN)
                        down(k, h, t * 8 + u)
            T = E // 2 // SLOTN
            for u in range(2 * SLOTN):
                if u + 1 < 2 * SLOTN:
                    up((u + 1) // 2, (u + 1) % 2, T * 8 + u + 1, T * SLOTN + (u + 1) // 2)
                down(u // 2, u % 2, T * 8 + u, last_pair=u // 2 == SLOTN - 1)
            pe.wait_ge(once("experts_out"), 2 * HALVES)
            for k in range(4):
                for i in range(2):
                    for m in range(DC):
                        last = pe.transpose(bank[4 + k][:, i * D + m * P:i * D + (m + 1) * P],
                                            yT[:, m, (2 * k + i) * P:(2 * k + i + 1) * P], ident[:, :])
                last.then_inc(once("y_rows"), 1)

            pe.wait_ge(once("xs_updated"), 4)
            pe.wait_ge(once("abs_sums"), 2)
            mm(bank[4][:, 0:2], ones[:, :], st[:, 0:2], start=True, stop=True).then_inc(once("abs_total"), 1)
            pe.wait_ge(once("mu_steps"), 1)
            for e in range(SE):
                for cc in range(DC):
                    last = mm(bank[5][:, e:e + 1], mu2[:, cc, e * SS:(e + 1) * SS], ones[:, 0:1], start=cc == 0, stop=cc == 1)
            last.then_inc(once("mu_products"), 1)
            pe.wait_ge(once("mu_steps"), 3)
            pe.transpose(bankb[6][0:96, 0:P], mst[:, 0, :, :], identb[:, :]).then_inc(once("mu_products"), 1)
            pe.wait_ge(once("mu_partsT"), 1)
            for e in range(SE):
                last = mm(bank[4 + e // 4][:, e % 4 * SS:(e % 4 + 1) * SS], sel[:, e, :], cmT[:, :], start=True, stop=True)
            last.then_inc(once("mu_products"), 1)
            pe.wait_ge(once("stage_loaded"), 5 * 16)
            for g, (srcs, dst) in enumerate(PREP + PREPB):
                if g >= 4:
                    pe.wait_ge(once("prep_done"), g - 3)
                if g == FIRST_STAGES:
                    pe.wait_ge(once("stage_rest_loaded"), 3 * 16)
                if g == len(PREP):
                    pe.wait_ge(once("ternary"), 2)
                for j, src in enumerate(srcs):
                    if g < len(PREP):
                        last = pe.transpose(bank[g % 4][:, j * P:(j + 1) * P], src, ident[:, :])
                    else:
                        last = pe.transpose(bankb[g % 4][:, j * P:(j + 1) * P], src, identb[:, :])
                last.then_inc(once("prep_made"), 1)
            g = len(PREP + PREPB)
            pe.wait_ge(once("prep_done"), g - 3)
            for m in range(DC):
                for cc in range(DC):
                    last = mm(bank[g % 4][:, m * R:(m + 1) * R], wo[:, cc, m * P:(m + 1) * P], am[:, cc, :],
                              start=cc == 0, stop=cc == DC - 1)
            last.then_inc(once("wa_made"), 1)
            pe.wait_ge(once("prepared"), 1)

            def attention(L):
                H, G, HD, causal = ATTENTIONS[L]
                KV, K6, GR = H // G, 6 * HD, H // 8
                first = lambda g: KV // 4 + 11 * g

                def free(r):
                    if r >= 2:
                        pe.wait_ge(S(f"att_left{r % 2}"), before(L, f"left{r % 2}") + r // 2)

                def has_left(r):
                    pe.wait_ge(S(f"att_left{r % 2}"), before(L, f"left{r % 2}") + r // 2 + 1)

                def turn(r, src, h4):
                    free(r)
                    for j in range(4):
                        h = 4 * h4 + j
                        for i in range(NT):
                            last = pe.transpose(bankb[r % 2][0:K6, j * N + i * P:j * N + (i + 1) * P],
                                                src[:, i, h * K6:(h + 1) * K6], identb[:, :])
                    last.then_inc(S("att_partsT"), 1)

                def by_query(g, j):
                    r, i, u = first(g) + 2 + j, j // 4, 4 * g + j % 4
                    if j == 0:
                        for k in range(0 if g == 0 else first(g), first(g) + 2):
                            has_left(k)
                    free(r)
                    if causal:
                        mm(bank[r % 2][:, :], identb[:, :], mask_q[:, i:i + 1, :].broadcast_to([P, 2, N]),
                           start=True, stop=False, skip_group_check=True)
                    for e in range(2):
                        h = 2 * u + e
                        last = mm(bank[r % 2][:, e * N:(e + 1) * N], qT[0:K6, h, i * P:(i + 1) * P], kT[0:K6, h // G, :],
                                  start=not causal, stop=True, skip_group_check=True)
                    last.then_inc(S("att_q_scores"), 1)

                def turn_maxima(g):
                    r = first(g) + 10
                    pe.wait_ge(S("att_max_parts"), before(L, "max_parts") + g + 1)
                    free(r)
                    for i in range(NT):
                        last = pe.transpose(bankb[r % 2][0:96, i * P:(i + 1) * P], mst[:, i, :, :], identb[:, :])
                    last.then_inc(S("att_mT_ps"), 1)

                def by_key(n):
                    u, ti, b_ = n // 2, n % 2, 2 + n % 2
                    if n % 8 == 0:
                        has_left(first(n // 8) + 10)
                    if n >= 2:
                        pe.wait_ge(S("att_probs"), before(L, "probs") + n - 1)
                    if causal:
                        mm(bank[b_][:, :], identb[:, :], mask_t[:, ti:ti + 1, :].broadcast_to([P, 2, N]),
                           start=True, stop=False, skip_group_check=True)
                    for e in range(2):
                        h = 2 * u + e
                        mm(bank[b_][:, e * N:(e + 1) * N], sel[:, h, :], mT[:, :], start=not causal, stop=False,
                           skip_group_check=True)
                        last = mm(bank[b_][:, e * N:(e + 1) * N], kT[0:K6, h // G, ti * P:(ti + 1) * P], qT[0:K6, h, :],
                                  start=False, stop=True, skip_group_check=True)
                    last.then_inc(S("att_scores"), 1)

                def weighted(n):
                    u, ti = n // 2, n % 2
                    pe.wait_ge(S("att_probs"), before(L, "probs") + n + 1)
                    strip = slice(32 * (u % 4), 32 * (u % 4) + 32)
                    if G > 1:
                        last = mm(bank[4 + u // 4][strip, :], vst[:, ti, 2 * u // G, :], prob[n % 4][:, :],
                                  start=ti == 0, stop=ti == 1, skip_group_check=True)
                    else:
                        for e in range(2):
                            last = mm(bank[4 + u // 4][strip, e * N:(e + 1) * N], vst[:, ti, 2 * u + e, :],
                                      prob[n % 4][:, e * N:(e + 1) * N], start=ti == 0 and e == 0, stop=ti == 1,
                                      skip_group_check=True)
                    last.then_inc(S("att_pv"), 1)

                def rows_again(g):
                    pe.wait_ge(S("att_oT"), before(L, "oT") + g + 1)
                    for e in range(2):
                        for i in range(NT):
                            last = pe.transpose(bank[4 + g][:, (2 * e + i) * P:(2 * e + i + 1) * P],
                                                otr[:, g, e * N + i * P:e * N + (i + 1) * P], ident[:, :])
                    last.then_inc(S("att_o"), 1)

                pe.wait_ge(S("att_parts"), before(L, "parts") + 1)
                for r in range(KV // 4):
                    turn(r, kst, r)
                pe.wait_ge(S("att_parts"), before(L, "parts") + 2)
                for k in range(2):
                    turn(first(0) + k, qst, k)
                for j in range(8):
                    by_query(0, j)
                turn_maxima(0)
                pe.wait_ge(S("att_v"), before(L, "v") + ATT_COUNTS["v"][L])
                for g in range(GR):
                    for k in range(8):
                        n = 8 * g + k
                        by_key(n)
                        if g + 1 < GR:
                            if k == 0:
                                for m in range(2):
                                    turn(first(g + 1) + m, qst, 2 * (g + 1) + m)
                            for j in ((), (0, 1), (2,), (3, 4), (5,), (6, 7), (), ())[k]:
                                by_query(g + 1, j)
                        if n >= 2:
                            weighted(n - 2)
                        if k == 3 and g > 0:
                            rows_again(g - 1)
                    if g + 1 < GR:
                        turn_maxima(g + 1)
                weighted(H - 2)
                weighted(H - 1)
                rows_again(GR - 1)

            with pe.Fori(0, B) as b:
                attention("l1x")

                pe.wait_ge(S("l1f_in"), 1)
                four_transposes(pe, bank[0], tmp, ident[:, :]).then_inc(S("l1f_in_ps"), 1)
                pe.wait_ge(S("l1f_in"), 2)
                four_transposes(pe, bank[1], qr, ident[:, :]).then_inc(S("l1f_in_ps"), 1)
                pe.wait_ge(S("l1f_inT"), 1)
                for i in range(NT):
                    for cc in range(DC):
                        mm(bank[2 + i][:, :], xT[:, cc, i * P:(i + 1) * P], wqkvT[:, cc, 0:512], start=cc == 0, stop=cc == 1)
                    for cc in range(DC):
                        last = mm(bank[4][:, i * D:(i + 1) * D], xT[:, cc, i * P:(i + 1) * P], wqkvT[:, cc, 512:768],
                                  start=cc == 0, stop=cc == 1)
                    last.then_inc(S("qkv_ps"), 1)
                attention("l1f")
                pe.wait_ge(S("att_attn"), before("l1f", "attn") + NT)
                four_transposes(pe, bank[4], at, ident[:, :]).then_inc(S("l1f_atT_ps"), 1)
                pe.wait_ge(S("l1f_inT"), 2)
                for cc in range(DC):
                    mm(bank[5][0:R, N:2 * N], am[:, cc, :], hT[:, cc, :], start=cc == 0, stop=cc == 1)
                pe.wait_ge(S("l1f_atT"), 1)
                for cc in range(DC):
                    last = mm(bank[5][0:R, 0:N], wa[:, cc, :], atT[:, cc, :], start=cc == 0, stop=cc == 1)
                last.then_inc(S("mod_ps"), 1)
                pe.wait_ge(S("mh"), 1)
                for f in range(F1 // P):
                    if f >= 4:
                        pe.wait_ge(S("l1f_gu"), f - 3)
                    fs = slice(f * P, (f + 1) * P)
                    mm(bank[f % 4][:, 0:N], winT[:, 0, fs], hT[:, 0, :], start=True, stop=False)
                    mm(bank[f % 4][:, 0:N], winT[:, 1, fs], hT[:, 1, :], start=False, stop=False)
                    mm(bank[f % 4][:, 0:N], bm[:, fs], mh[:, :], start=False, stop=True)
                    mm(bank[f % 4][:, N:2 * N], wupT[:, 0, fs], hT[:, 0, :], start=True, stop=False)
                    mm(bank[f % 4][:, N:2 * N], wupT[:, 1, fs], hT[:, 1, :], start=False, stop=True)\
                        .then_inc(S("l1f_up"), 1)
                for i in range(NT):
                    for f in range(F1 // P):
                        pe.wait_ge(S("l1f_gu"), f + 1)
                        last = mm(bank[6 + i][:, 0:D], gu[:, f, i * P:(i + 1) * P], wdT[:, f, :],
                                  start=f == 0, stop=f == F1 // P - 1)
                    last.then_inc(S("l1f_down"), 1)

                pe.wait_ge(S("c_ready"), 1)
                for i in range(NT):
                    last = pe.transpose(bank[0][0:CD, i * P:(i + 1) * P], c[:, i, :], ident[:, :])
                last.then_inc(S("cT_ps"), 1)
                pe.wait_ge(S("cT"), 1)
                mm(bank[1][:, 0:N], l2wj[:, :], cT[:, :], start=True, stop=True).then_inc(S("sj_ps"), 1)

                pe.wait_ge(S("l2f_q1"), NT)
                for i in range(NT):
                    for cc in range(DC):
                        last = pe.transpose(bankb[0][:, cc * N + i * P:cc * N + i * P + P], q1[:, i, cc * P:(cc + 1) * P], identb[:, :])
                last.then_inc(S("q1T_ps"), 1)
                pe.wait_ge(S("q1T"), 1)
                for i in range(NT):
                    for hf in range(2):
                        for cc in range(DC):
                            last = mm(bank[1 + 2 * i + hf][:, :], q1T[:, cc, i * P:(i + 1) * P],
                                      w1qT[:, cc, hf * 512:(hf + 1) * 512], start=cc == 0, stop=cc == 1)
                    last.then_inc(S("l2f_up"), 1)
                for i in range(NT):
                    pe.wait_ge(S("l2f_q2"), i + 1)
                    for f in range(F1 // P):
                        last = pe.transpose(bankb[5 + i][:, f * P:(f + 1) * P], q2[:, i, f * P:(f + 1) * P], identb[:, :])
                    last.then_inc(S("q2T_ps"), 1)
                for i in range(NT):
                    pe.wait_ge(S("q2T"), i + 1)
                    for f in range(F1 // P):
                        last = mm(bank[7 * i][:, 0:D], q2T[:, f, i * P:(i + 1) * P], w2qT[:, f, :],
                                  start=f == 0, stop=f == F1 // P - 1)
                    last.then_inc(S("l2f_down"), 1)

                attention("l3x")
                pe.wait_ge(S("att_attn"), before("l3x", "attn") + NT)
                four_transposes(pe, bank[4], at, ident[:, :]).then_inc(S("l3x_atT_ps"), 1)
                pe.wait_ge(S("l3x_atT"), 1)
                for i in range(NT):
                    for cc in range(DC):
                        last = mm(bank[5][:, i * D:(i + 1) * D], atT[:, cc, i * P:(i + 1) * P], wcT[:, cc, :],
                                  start=cc == 0, stop=cc == 1)
                    last.then_inc(S("l3x_proj"), 1)

                pe.wait_ge(S("l3f_xl"), NT)
                four_transposes(pe, bank[0], xl, ident[:, :]).then_inc(S("l3f_xT_ps"), 1)
                pe.wait_ge(S("l3f_xT"), 1)
                for ch in range(4):
                    for i in range(NT):
                        for cc in range(DC):
                            last = mm(bank[2 * ch + i][:, :], xT[:, cc, i * P:(i + 1) * P], mun[:, cc, ch * 512:(ch + 1) * 512],
                                      start=cc == 0, stop=cc == 1)
                        last.then_inc(S("logits_ps"), 1)

                def by_slot(g):
                    pe.wait_ge(S("logits_out"), 2 * (g // 2) + 2)
                    for j in range(2):
                        for i in range(NT):
                            last = pe.transpose(bank[g][:, j * N + i * P:j * N + (i + 1) * P],
                                                lg[:, i, (2 * g + j) * P:(2 * g + j + 1) * P], ident[:, :])
                    last.then_inc(S("logitsT_ps"), 1)

                def project(n):
                    i, hf = n // 2, n % 2
                    if n >= 2:
                        pe.wait_ge(S("proj_out"), n - 1)
                    for cc in range(DC):
                        last = mm(bank[hf][:, :], xT[:, cc, i * P:(i + 1) * P], w1s[:, cc, 8 * hf:8 * hf + 8, :],
                                  start=cc == 0, stop=cc == 1)
                    last.then_inc(S("proj_ps"), 1)

                for g in range(6):
                    by_slot(g)
                pe.wait_ge(S("row_parts"), 1)
                pe.wait_ge(S("logits_out"), 8)
                for i in range(NT):
                    last = pe.transpose(bankb[6][0:96, i * P:(i + 1) * P], mst[:, i, :, :], identb[:, :])
                last.then_inc(S("row_partsT_ps"), 1)
                pe.wait_ge(S("row_partsT"), 1)
                mm(bank[7][:, 0:N], sel[:, 0, :], mT3[:, :], start=True, stop=True).then_inc(S("row_max_all"), 1)
                by_slot(6)
                pe.wait_ge(S("row_max_read"), 1)
                by_slot(7)
                pe.wait_ge(S("lT_less_max"), 2)
                project(0)
                project(1)
                pe.wait_ge(S("slot_parts"), 1)
                pe.wait_ge(S("lT_less_max"), 3)
                pe.transpose(bankb[2][0:96, 0:P], mst[:, 0, :, :], identb[:, :]).then_inc(S("slot_partsT_ps"), 1)
                pe.wait_ge(S("slot_partsT"), 1)
                pe.wait_ge(S("lT_less_max"), 8)
                for e in range(SE):
                    last = mm(bank[4 + e // 4][:, e % 4 * SS:(e % 4 + 1) * SS], sel[:, e, :], cmT[:, :], start=True, stop=True)
                    if e % 4 == 3:
                        last.then_inc(S("slot_max_all"), 1)
                project(2)
                project(3)
                pe.wait_ge(S("proj_out"), 4)
                pe.wait_ge(S("ones_columns"), 2)
                for ch in range(4):
                    pe.wait_ge(S("dispatch"), ch + 1)
                    for k in range(4):
                        for i in range(NT):
                            e = 4 * ch + k
                            last = mm(bank[ch][:, k * (SH + 1):(k + 1) * (SH + 1)], lg[:, i, e * SS:(e + 1) * SS],
                                      xw[:, i, e, :], start=i == 0, stop=i == 1)
                    last.then_inc(S("soft_up"), 1)

                def gather(g):
                    pe.wait_ge(S("soft_hidden"), g // 2 + 1)
                    pe.wait_ge(S("combine"), g + 1)
                    if g >= 4:
                        pe.wait_ge(S(f"gathered{g % 2}"), (g - 4) // 2 + 1)
                    for j in range(2):
                        last = mm(bank[4 + g % 4][0:SH + 1, j * N:(j + 1) * N], hs[:, 2 * g + j, :], lT[:, 2 * g + j, :],
                                  start=True, stop=True)
                    last.then_inc(S("gathered_ps"), 1)

                def back(g):
                    pe.wait_ge(S(f"gathered{g % 2}"), g // 2 + 1)
                    for e in (2 * g, 2 * g + 1):
                        for i in range(NT):
                            last = mm(bank[i][:, 0:D + 1], aT[:, e, i * P:(i + 1) * P], w2a[:, e, :],
                                      start=e == 0, stop=e == SE - 1)
                    return last

                pe.wait_ge(S("logits_less_max"), 4)
                for g in range(8):
                    gather(g)
                    if g >= 2:
                        back(g - 2)
                back(6)
                back(7).then_inc(S("soft_out"), 1)
                end_of_batch(pe)
                pe.wait_ge(once("batch_cleared"), b + (B + 1))

        @block.scalar
        def _(act):
            def copy(dst, src, scale=1.0):
                return act.activation(dst, src, ACT.Copy, scale=scale)

            act.wait_ge(once("first_loads"), 9 * 16)
            act.activation(gates[:, :], gates[:, :], ACT.Tanh).then_inc(once("gates_ready"), 1)
            act.wait_ge(once("wk_turned"), 1)
            copy(wkT[:, :], bank[0][0:CD, 0:CD]).then_inc(once("wkT_ready"), 1)
            act.wait_ge(once("x_loaded"), 32)
            with act.Fori(0, B) as b:
                copy(c[:, :, :], ctxs[:, bass.ts(b, NT), :]).then_inc(S("c_ready"), 1)
                act.wait_ge(S("p0"), 1)
                copy(cT[:, :], bank[0][0:CD, 0:N]).then_inc(S("cT"), 1)
                act.wait_ge(S("kvT_ps"), 1)
                act.activation(kvT[:, :], bank[1][0:CD, 0:N], ACT.Identity, bias=bk_col[:, 0:1]).then_inc(S("kvT"), 1)
                act.wait_ge(S("xT_ps"), 1)
                copy(xT[:, :, :], bank[3][:, :]).then_inc(S("xT"), 1)
                act.wait_ge(S("oT_ps"), 1)
                copy(oT[:, :], bank[4][0:CD, 0:N], scale=float(D) ** -0.5).then_inc(S("oT"), 1)
                for i in range(NT):
                    act.wait_ge(S("l0_ln_done"), i + 1)
                    act.activation(tmp[:, i, :], tmp[:, i, :], ACT.Exp, bias=nw[:, i:i + 1],
                                   accum_out=st[:, i:i + 1]).then_inc(S("l0_exp"), 1)
                act.wait_ge(S("xT_ps"), 2)
                copy(xT[:, :, :], bank[6][:, :]).then_inc(S("xT"), 1)
                for i in range(NT):
                    act.wait_ge(S("router_max"), i + 1)
                    act.activation(cb0[:, i, :], lg0[:, i, :], ACT.Exp, bias=nw[:, 2 + i:3 + i]).then_inc(S("router_exp"), 1)
                act.wait_ge(S("comb_ps"), 1)
                copy(comb_hm[:, bass.ts(b, N)], bankb[0][:, 0:N]).then_inc(S("act_last"), 1)
                copy(comb_l[0:E, bass.ts(b, N)], bankb[1][0:E, 0:N]).then_inc(S("act_last"), 1)
                act.wait_ge(S("act_last"), 2)
                end_of_batch(act)
                act.wait_ge(once("batch_cleared"), b + 1)

            def gate(k, u):
                n = 3 * k
                act.wait_ge(once("gate_made"), u + 1)
                act.wait_ge(once("up_used"), u + 1)
                act.activation(sg[k % 2][:, :], bank[4 + n % 4][:, :], ACT.Silu).then_inc(once("gate_used"), 1)
                act.wait_ge(once("hidden_full"), u + 1)
                copy(hhi[k % 2][:, :], hh[k % 2][:, :]).then_inc(once("hidden_high"), 1)

            act.wait_ge(once("picks"), 2)
            with act.Fori(0, PAIRS // SLOTN) as t:
                for k in range(2 * SLOTN):
                    gate(k, t * 8 + k)
            act.wait_ge(once("hidden_used"), 2 * PAIRS + 4)
            for h in range(HALVES):
                for m in range(DC):
                    copy(yT[:, m, h * 512:(h + 1) * 512], bank[2 * m + h][:, :]).then_inc(once("experts_out"), 1)
            act.wait_ge(once("l2_loaded"), 2 * 16)
            for k, scratch in enumerate((w1qT, w2qT)):
                act.activation(scratch[:, :, :].rearrange("p c f -> p (c f)"), l2_raw[k][:, :], ACT.Abs, accum_out=st[:, k:k + 1]).then_inc(once("abs_sums"), 1)
            act.wait_ge(once("mu_products"), 2)
            copy(cmT[:, :], bankb[6][0:96, 0:P]).then_inc(once("mu_partsT"), 1)
            for g, (srcs, dst) in enumerate(PREP + PREPB):
                if g == 0:
                    act.wait_ge(once("ternary"), 2)
                act.wait_ge(once("prep_made"), g + 1)
                src = (bank if g < len(PREP) else bankb)[g % 4]
                copy(dst, src[:, 0:len(srcs) * P]).then_inc(once("prep_done"), 1)

            def attention(L):
                H, G, HD, causal = ATTENTIONS[L]
                KV, K6, GR = H // G, 6 * HD, H // 8
                first = lambda g: KV // 4 + 11 * g

                def turned(r, dst, t):
                    if r % 2 == 0:
                        act.wait_ge(S("att_partsT"), before(L, "partsT") + t + 1)
                        copy(dst, bankb[0][0:K6, :]).then_inc(S("att_left0"), 1)

                def queries(g):
                    for k in range(2):
                        h = 8 * g + 4 * k
                        turned(first(g) + k, qT[0:K6, h:h + 4, :], KV // 4 + 2 * g + k)

                def maxima(g):
                    r = first(g) + 10
                    act.wait_ge(S("att_mT_ps"), before(L, "mT_ps") + g + 1)
                    copy(mT[:, :], bankb[r % 2][0:96, 0:N]).then_inc(S(f"att_left{r % 2}"), 1)

                def results(g):
                    act.wait_ge(S("att_pv"), before(L, "pv") + 8 * g + 8)
                    copy(otr[:, g, :], bank[4 + g][:, :]).then_inc(S("att_oT"), 1)

                for r in range(KV // 4):
                    turned(r, kT[0:K6, 4 * r:4 * r + 4, :], r)
                queries(0)
                maxima(0)
                for g in range(GR):
                    for k in range(8):
                        n = 8 * g + k
                        act.wait_ge(S("att_scores"), before(L, "scores") + n + 1)
                        if n >= 4:
                            act.wait_ge(S("att_pv"), before(L, "pv") + n - 3)
                        act.activation(prob[n % 4][:, :], bank[2 + n % 2][:, :], ACT.Exp).then_inc(S("att_probs"), 1)
                        if k == 0 and g + 1 < GR:
                            queries(g + 1)
                        if k == 2 and g > 0:
                            results(g - 1)
                    if g + 1 < GR:
                        maxima(g + 1)
                results(GR - 1)

            act.wait_ge(once("prepared"), 1)
            with act.Fori(0, B) as b:
                copy(c[:, :, :], ctxs[:, bass.ts(b, NT), :]).then_inc(S("c_ready"), 1)
                attention("l1x")
                act.wait_ge(S("l1f_in_ps"), 1)
                copy(xT[:, :, :], bank[0][:, :]).then_inc(S("l1f_inT"), 1)
                act.wait_ge(S("l1f_in_ps"), 2)
                copy(hT[:, :, :], bank[1][:, :]).then_inc(S("l1f_inT"), 1)
                for i in range(NT):
                    act.wait_ge(S("qkv_ps"), i + 1)
                    copy(qf[:, i, :], bank[2 + i][:, 0:D], scale=0.25).then_inc(S("qk"), 1)
                    copy(kf[:, i, :], bank[2 + i][:, D:2 * D]).then_inc(S("qk"), 1)
                attention("l1f")
                act.wait_ge(S("l1f_atT_ps"), 1)
                copy(atT[:, :, :], bank[4][:, :]).then_inc(S("l1f_atT"), 1)
                act.wait_ge(S("mod_ps"), 1)
                act.activation(modT[:, :], bank[5][0:R, 0:N], ACT.Tanh).then_inc(S("modT"), 1)
                for f in range(F1 // P):
                    act.wait_ge(S("l1f_up"), f + 1)
                    if f >= 2:
                        act.wait_ge(S("l1f_gu"), f - 1)
                    act.activation(sgf[f % 2][:, :], bank[f % 4][:, 0:N], ACT.Silu).then_inc(S("l1f_silu"), 1)
                act.wait_ge(S("cT_ps"), 1)
                copy(cT[:, :], bank[0][0:CD, 0:N]).then_inc(S("cT"), 1)
                act.wait_ge(S("sj_ps"), 1)
                act.wait_ge(S("si"), 1)
                for i in range(NT):
                    act.activation(tmp[:, i, :], bank[1][:, 0:N], ACT.Sigmoid, bias=st[:, 8 + i:9 + i]).then_inc(S("l2x_sig"), 1)
                act.wait_ge(S("q1T_ps"), 1)
                copy(q1T[:, :, :], bankb[0][:, 0:512]).then_inc(S("q1T"), 1)
                for i in range(NT):
                    act.wait_ge(S("l2f_pre"), i + 1)
                    act.activation(h2[:, i, :], h2[:, i, :], ACT.Silu).then_inc(S("l2f_silu"), 1)
                for i in range(NT):
                    act.wait_ge(S("l2f_silu"), i + 1)
                    act.activation(h2[:, i, :], h2[:, i, :], ACT.Gelu).then_inc(S("l2f_gelu"), 1)
                for i in range(NT):
                    act.wait_ge(S("l2f_ln"), i + 1)
                    act.activation(h2s[:, i, :], h2[:, i, :], ACT.Square, accum_out=st[:, 4 + i:5 + i]).then_inc(S("l2f_sq"), 1)
                for i in range(NT):
                    act.wait_ge(S("q2T_ps"), i + 1)
                    copy(q2T[:, :, i * P:(i + 1) * P], bankb[5 + i][:, :].rearrange("p (f t) -> p f t", t=P)).then_inc(S("q2T"), 1)
                attention("l3x")
                act.wait_ge(S("l3x_atT_ps"), 1)
                copy(atT[:, :, :], bank[4][:, :]).then_inc(S("l3x_atT"), 1)
                act.wait_ge(S("l3f_xT_ps"), 1)
                copy(xT[:, :, :], bank[0][:, :]).then_inc(S("l3f_xT"), 1)
                act.wait_ge(S("l3f_rs"), 1)
                for n in range(8):
                    ch, i = n // 2, n % 2
                    act.wait_ge(S("logits_ps"), n + 1)
                    copy(lg[:, i, ch * 512:(ch + 1) * 512], bank[n][:, :], scale=rs[:, i:i + 1]).then_inc(S("logits_out"), 1)
                act.wait_ge(S("row_partsT_ps"), 1)
                copy(mT3[:, :], bankb[6][0:96, 0:N]).then_inc(S("row_partsT"), 1)
                for g in range(8):
                    act.wait_ge(S("lT_less_max"), g + 1)
                    act.activation(lT[:, 2 * g:2 * g + 2, :], lT[:, 2 * g:2 * g + 2, :], ACT.Exp).then_inc(S("combine"), 1)

                def projected(n):
                    i, hf = n // 2, n % 2
                    act.wait_ge(S("proj_ps"), n + 1)
                    copy(xw[:, i, 8 * hf:8 * hf + 8, 0:SH], bank[hf][:, :].rearrange("p (e h) -> p e h", h=SH))\
                        .then_inc(S("proj_out"), 1)

                projected(0)
                projected(1)
                act.wait_ge(S("slot_partsT_ps"), 1)
                copy(cmT[:, :], bankb[2][0:96, 0:P]).then_inc(S("slot_partsT"), 1)
                projected(2)
                projected(3)
                for ch in range(4):
                    lc = lg[:, :, ch * 512:(ch + 1) * 512]
                    act.wait_ge(S("logits_less_max"), ch + 1)
                    act.activation(lc, lc, ACT.Exp).then_inc(S("dispatch"), 1)
                for ch in range(4):
                    h = hs[:, 4 * ch:4 * ch + 4, 0:SH]
                    act.wait_ge(S("soft_pre"), ch + 1)
                    act.activation(h, h, ACT.Gelu).then_inc(S("soft_hidden"), 1)
                for g in range(0, 8, 2):
                    act.wait_ge(S("gathered_ps"), g + 1)
                    copy(aT[:, 2 * g:2 * g + 2, :], bank[4 + g % 4][0:SH + 1, :].rearrange("p (e t) -> p e t", e=2))\
                        .then_inc(S("gathered0"), 1)
                act.wait_ge(S("gathered0"), 4)
                end_of_batch(act)
                act.wait_ge(once("batch_cleared"), b + (B + 1))

        @block.vector
        def _(dve):
            V = nc.vector
            ts, tt, stt = V.tensor_scalar, V.tensor_tensor, V.scalar_tensor_tensor

            def rsqrt(step, out_, v):
                k = v.shape[1]
                w = nw[:, 0:k] if k <= 4 else cmr[:, 0:k]
                step(ts(w.bitcast(I32), v.bitcast(I32), 1, None, ALU.arith_shift_right))
                step(ts(out_.bitcast(I32), w.bitcast(I32), -1, 0x5F3759DF, ALU.mult, ALU.add))
                for _ in range(3):
                    step(tt(w, out_, v, ALU.mult))
                    step(stt(out=w, in0=w, scalar=-0.5, in1=out_, op0=ALU.mult, op1=ALU.mult))
                    step(stt(out=out_, in0=w, scalar=1.5, in1=out_, op0=ALU.add, op1=ALU.mult))

            def stats(step, src, eps):
                step(*[V.bn_stats(bn[:, i, :], src(i)) for i in range(NT)])
                step(*[V.bn_aggr(mv[:, i, :], bn[:, i, :]) for i in range(NT)])
                step(ts(ve[:, 0:NT], mv[:, :, 1], eps, None, ALU.add))
                rsqrt(step, rs[:, 0:NT], ve[:, 0:NT])

            def layernorm(step, out_, scale=1.0):
                stats(step, lambda i: x[:, i, :], 1e-5)
                if scale != 1.0:
                    step(ts(rs[:, 0:NT], rs[:, 0:NT], scale, None, ALU.mult))
                step(*[ts(out_[:, i, :], x[:, i, :], mv[:, i, 0:1], rs[:, i:i + 1], ALU.subtract, ALU.mult) for i in range(NT)])

            def three_parts(step, parts, v, left):
                step(V.tensor_copy(parts[0], v))
                step(tt(left, v, parts[0], ALU.subtract))
                step(V.tensor_copy(parts[1], left))
                step(tt(parts[2], left, parts[1], ALU.subtract))

            dve.wait_ge(once("x_loaded"), 32)
            dve.wait_ge(once("first_loads"), 9 * 16)
            dve.wait_ge(once("gates_ready"), 1)
            with dve.Fori(0, B) as b:
                step = Steps(dve, S("dve_step"))
                step(V.tensor_copy(x[:, :, :], xs[:, bass.ts(b, NT), :]))
                layernorm(step, xn)
                dve.sem_inc(S("xn"), NT)
                dve.wait_ge(S("kv_ps"), 1)
                tt(kv[:, :, :], bank[2][:, 0:P].rearrange("p (i d) -> p i d", i=NT),
                   bk_row[:, :].unsqueeze(1).broadcast_to([P, NT, CD]), ALU.add).then_inc(S("kv"), 1)
                dve.wait_ge(S("sim_ps"), 2)
                stats(step, lambda i: bank[5][:, i * N:(i + 1) * N], 1e-6)
                for i in range(NT):
                    step(ts(tmp[:, i, :], bank[5][:, i * N:(i + 1) * N], mv[:, i, 0:1], rs[:, i:i + 1], ALU.subtract, ALU.mult))
                    step(tt(tmp[:, i, :], tmp[:, i, :], rowsD["L0_xattn_ln_gamma"][:, :], ALU.mult))
                    step(tt(tmp[:, i, :], tmp[:, i, :], rowsD["L0_xattn_ln_beta"][:, :], ALU.add))
                    step(V.reduce_max(ve[:, i:i + 1], tmp[:, i, :], AX))
                    ts(nw[:, i:i + 1], ve[:, i:i + 1], -1.0, None, ALU.mult).then_inc(S("l0_ln_done"), 1)
                dve.wait_ge(S("l0_exp"), 2)
                step(V.reciprocal(st[:, 2:4], st[:, 0:2]))
                step(ts(st[:, 2:4], st[:, 2:4], gates[:, 0:1], None, ALU.mult))
                for i in range(NT):
                    step(stt(out=x[:, i, :], in0=tmp[:, i, :], scalar=st[:, 2 + i:3 + i], in1=x[:, i, :], op0=ALU.mult, op1=ALU.add))
                dve.sem_inc(S("x_done"), 1)
                layernorm(step, xn)
                dve.sem_inc(S("xn"), NT)
                dve.wait_ge(S("router_ps"), 1)
                step(V.tensor_copy(lg0[:, :, :], bank[7][:, 0:NT * E].rearrange("p (i e) -> p i e", i=NT)))
                step(V.memset(lb0[:, :, E:E + TOPK], -BIG))
                step(tt(lb0[:, :, 0:E], lg0[:, :, :], rb[:, :].unsqueeze(1).broadcast_to([P, NT, E]), ALU.add))
                for i in range(NT):
                    step(V.reduce_max(ve[:, i:i + 1], lg0[:, i, :], AX))
                    ts(nw[:, 2 + i:3 + i], ve[:, i:i + 1], -1.0, None, ALU.mult).then_inc(S("router_max"), 1)
                    step(V.max(m8[:, i, :], lb0[:, i, 0:E]))
                    step(V.memset(m8[:, i, TOPK:8], -BIG))
                    step(V.match_replace(lr0[:, i, :], m8[:, i, :], lb0[:, i, :], BIG))
                dve.wait_ge(S("router_exp"), 2)
                step(tt(ct0[:, :, :], lr0[:, :, 0:E], lb0[:, :, 0:E], ALU.not_equal))
                step(tt(ct0[:, :, :], ct0[:, :, :], cb0[:, :, :], ALU.mult))
                step(V.reduce_sum(st[:, 4:6], ct0[:, :, :], AX))
                step(V.reciprocal(st[:, 6:8], st[:, 4:6]))
                for i in range(NT):
                    step(ts(ct0[:, i, :], ct0[:, i, :], st[:, 6 + i:7 + i], None, ALU.mult))
                three_parts(step, [cst[:, :, k, :] for k in range(3)], ct0[:, :, :], cb0[:, :, :])
                dve.sem_inc(S("comb"), 1)
                end_of_batch(dve)
                dve.wait_ge(once("batch_cleared"), b + 1)

            step = Steps(dve, once("dve_step_prep"))
            dve.wait_ge(once("picks"), 2)
            dve.sem_inc(once("hidden_made"), 1)
            dve.sem_inc(once("up_used"), 2)
            with dve.Fori(0, PAIRS // SLOTN) as t:
                for k in range(2 * SLOTN):
                    n, u = 3 * k, t * 8 + k
                    dve.wait_ge(once("gate_used"), u + 1)
                    dve.wait_ge(once("up_made"), u + 1)
                    tt(hu[k % 2][:, :], bank[4 + (n + 1) % 4][:, :], sg[k % 2][:, :], ALU.mult).then_inc(once("up_used"), 1)
                    dve.wait_ge(once("up_used"), u + 3)
                    dve.wait_ge(once("weight_made"), u + 1)
                    dve.wait_ge(once("hidden_used"), u + 3)
                    tt(hh[k % 2][:, :], bank[4 + (n + 2) % 4][:, :], hu[k % 2][:, :], ALU.mult).then_inc(once("hidden_full"), 1)
                    dve.wait_ge(once("hidden_high"), u + 1)
                    tt(hlo[k % 2][:, :], hh[k % 2][:, :], hhi[k % 2][:, :].bitcast(F32), ALU.subtract)\
                        .then_inc(once("hidden_made"), 1)
            for k in range(4):
                dve.wait_ge(once("y_rows"), k + 1)
                rows = xs[:, 2 * k:2 * k + 2, :]
                stt(out=rows, in0=bank[4 + k][:, :].rearrange("p (i d) -> p i d", i=2), scalar=gates[:, 4:5], in1=rows,
                    op0=ALU.mult, op1=ALU.add).then_inc(once("xs_updated"), 1)
            dve.wait_ge(once("rest_loads"), REST * 16)
            dve.wait_ge(once("prep_waits_experts"), 1)
            step(tt(mu2[:, :, :], mun[:, :, :], mun[:, :, :], ALU.mult))
            dve.sem_inc(once("mu_steps"), 1)
            dve.wait_ge(once("abs_total"), 1)
            step(ts(wdq[:, :], bank[4][:, 0:2], 1.0 / (F1 * D), 1e-5, ALU.mult, ALU.max))
            dve.sem_inc(once("mu_steps"), 1)
            step(V.reciprocal(st[:, 2:4], wdq[:, :]))
            for k in range(2):
                w = l2_raw[k][:, :]
                step(ts(w, w, st[:, 2 + k:3 + k], -1.0, ALU.mult, ALU.max))
                step(ts(w, w, 1.0, ROUND, ALU.min, ALU.add))
                ts(tern[k][:, :], w, ROUND, None, ALU.subtract).then_inc(once("ternary"), 1)
            dve.wait_ge(once("mu_products"), 1)
            step(V.tensor_copy(cmx[:, :], bank[5][:, 0:SE]))
            rsqrt(step, rbc[:, 0:SE], cmx[:, :])
            step(tt(cmx[:, :], cmx[:, :], rbc[:, 0:SE], ALU.mult))
            step(ts(cmx[:, :], cmx[:, :], 1e-12, None, ALU.max))
            step(V.reciprocal(rbc[:, 0:SE], cmx[:, :]))
            three_parts(step, [mst[:, 0, k, 0:SE] for k in range(3)], rbc[:, 0:SE], cmr[:, 0:SE])
            dve.sem_inc(once("mu_steps"), 1)
            dve.wait_ge(once("mu_products"), 3)
            for ch in range(4):
                m = mun[:, :, ch * 512:(ch + 1) * 512]
                step(tt(m, m, bank[4 + ch][:, :].unsqueeze(1).broadcast_to([P, DC, 512]), ALU.mult))
            step(V.tensor_copy(l2wj[:, 1:P], l2wj[:, 0:1].broadcast_to([CD, P - 1])))
            dve.wait_ge(once("wa_made"), 1)
            step(V.tensor_copy(wa[:, :, :], bank[len(PREP + PREPB) % 4][:, 0:DC * R].rearrange("p (m r) -> p m r", m=DC)))
            dve.sem_inc(once("prepared"), 1)
            dve.wait_ge(once("xs_updated"), 4)

            def attention(step, L, q, k):
                H, G, HD, causal = ATTENTIONS[L]
                KV, K6 = H // G, 6 * HD

                GR = H // 8
                first = lambda g: KV // 4 + 11 * g

                def slot(t, heads, s):
                    v = t[:, :, 0:heads * K6].rearrange("p i (h s d) -> p s i h d", h=heads, s=6)
                    return v[:, s]
                for t, heads, src, (h, m, l), copies in ((kst, KV, k, (0, 1, 4), ((2, 0), (5, 0), (3, 1))),
                                                         (qst, H, q, (0, 2, 5), ((1, 0), (4, 0), (3, 2)))):
                    src = src.rearrange("p i (h d) -> p i h d", h=heads)
                    left = qr[:, :, 0:heads * HD].rearrange("p i (h d) -> p i h d", h=heads)
                    step(V.tensor_copy(slot(t, heads, h), src))
                    step(tt(left, src, slot(t, heads, h), ALU.subtract))
                    step(V.tensor_copy(slot(t, heads, m), left))
                    step(tt(slot(t, heads, l), left, slot(t, heads, m), ALU.subtract),
                         *[V.tensor_copy(slot(t, heads, to), slot(t, heads, fro)) for to, fro in copies])
                    dve.sem_inc(S("att_parts"), 1)

                def turned(r, dst, t_):
                    if r % 2 == 1:
                        dve.wait_ge(S("att_partsT"), before(L, "partsT") + t_ + 1)
                        V.tensor_copy(dst, bankb[1][0:K6, :].rearrange("p (h n) -> p h n", h=4)).then_inc(S("att_left1"), 1)

                def maxima(g):
                    for k_ in range(2):
                        h = 8 * g + 4 * k_
                        turned(first(g) + k_, qT[0:K6, h:h + 4, :], KV // 4 + 2 * g + k_)
                    for j in range(8):
                        r, i, u = first(g) + 2 + j, j // 4, 4 * g + j % 4
                        dve.wait_ge(S("att_q_scores"), before(L, "q_scores") + 8 * g + j + 1)
                        V.reduce_max(mx[:, i, 2 * u:2 * u + 2], bank[r % 2][:, :].rearrange("p (e t) -> p e t", e=2), AX,
                                     negate=True).then_inc(S(f"att_left{r % 2}"), 1)
                    for r in (first(g) + 8, first(g) + 9):
                        dve.wait_ge(S(f"att_left{r % 2}"), before(L, f"left{r % 2}") + r // 2 + 1)
                    hs = slice(8 * g, 8 * g + 8)
                    three_parts(step, [mst[:, :, s, hs] for s in range(3)], mx[:, :, hs], mr[:, :, hs])
                    dve.sem_inc(S("att_max_parts"), 1)

                def results(g):
                    dve.wait_ge(S("att_o"), before(L, "o") + g + 1)
                    o = bank[4 + g][:, :].rearrange("p (e i j d) -> p e i j d", e=2, i=NT, j=4)
                    step(V.reciprocal(rc[:, g, :], bank[4 + g][:, :].rearrange("p (k d) -> p k d", d=32)[:, :, HD]))
                    r = rc[:, g, :].rearrange("p (e i j) -> p e i j", e=2, i=NT)
                    step(*[tt(at[:, i, g * 8 * HD:(g + 1) * 8 * HD].rearrange("p (j e d) -> p e j d", e=2, d=HD)[:, e],
                              o[:, e, i, :, 0:HD], r[:, e, i, :].unsqueeze(2).broadcast_to([P, 4, HD]), ALU.mult)
                           for i in range(NT) for e in range(2)])

                for r in range(KV // 4):
                    turned(r, kT[0:K6, 4 * r:4 * r + 4, :], r)
                maxima(0)
                for g in range(GR):
                    if g + 1 < GR:
                        maxima(g + 1)
                    if g > 0:
                        results(g - 1)
                results(GR - 1)
                dve.sem_inc(S("att_attn"), NT)

            def residual(step, y, g, done=None):
                step(*[stt(out=x[:, i, :], in0=y(i), scalar=gates[:, g:g + 1], in1=x[:, i, :], op0=ALU.mult, op1=ALU.add)
                       for i in range(NT)])

            with dve.Fori(0, B) as b:
                step = Steps(dve, S("dve_step"))
                step(V.tensor_copy(x[:, :, :], xs[:, bass.ts(b, NT), :]))
                layernorm(step, xn, 8 ** -0.5)
                dve.wait_ge(S("c_ready"), 1)
                dve.sem_inc(S("l1x_begun"), 1)
                attention(step, "l1x", xn[:, :, :], c[:, :, :])
                residual(step, lambda i: at[:, i, :], 1)

                layernorm(step, xn)
                for i in range(NT):
                    step(V.tensor_tensor_reduce(out=tmp[:, i, :], in0=xn[:, i, :], in1=xn[:, i, :], scale=1.0, scalar=0.0,
                                                op0=ALU.mult, op1=ALU.add, accum_out=st[:, i:i + 1]))
                step(ts(ve[:, 0:NT], st[:, 0:NT], 1.0 / D, 1e-6, ALU.mult, ALU.add))
                rsqrt(step, rs[:, 0:NT], ve[:, 0:NT])
                for w, dst in (("L1_ffn_ln1_w", tmp), ("L1_ffn_ln2_w", qr)):
                    for i in range(NT):
                        step(stt(out=dst[:, i, :], in0=xn[:, i, :], scalar=rs[:, i:i + 1], in1=rowsD[w][:, :],
                                 op0=ALU.mult, op1=ALU.mult))
                    dve.sem_inc(S("l1f_in"), 1)
                dve.wait_ge(S("l1f_in_ps"), 2)
                dve.wait_ge(S("qkv_ps"), 2)
                V.tensor_copy(vst[:, :, :, 0:16], bank[4][:, :].rearrange("p (i h d) -> p i h d", i=NT, d=16)).then_inc(S("att_v"), 1)
                dve.wait_ge(S("qk"), 4)
                attention(step, "l1f", qf[:, :, :], kf[:, :, :])
                dve.wait_ge(S("modT"), 1)
                stt(out=mh[:, :], in0=modT[:, :], scalar=0.1, in1=bank[5][0:R, N:2 * N], op0=ALU.mult, op1=ALU.mult)\
                    .then_inc(S("mh"), 1)
                for f in range(F1 // P):
                    dve.wait_ge(S("l1f_silu"), f + 1)
                    tt(gu[:, f, :], bank[f % 4][:, N:2 * N], sgf[f % 2][:, :], ALU.mult).then_inc(S("l1f_gu"), 1)
                dve.wait_ge(S("l1f_down"), 2)
                for i in range(NT):
                    step(tt(xn[:, i, :], xn[:, i, :], bank[6 + i][:, 0:D], ALU.add))
                residual(step, lambda i: xn[:, i, :], 5)

                for i in range(NT):
                    step(V.tensor_tensor_reduce(out=qr[:, i, 0:CD], in0=c[:, i, :], in1=l2wi[:, :], scale=1.0, scalar=0.0,
                                                op0=ALU.mult, op1=ALU.add, accum_out=st[:, 8 + i:9 + i]))
                step(ts(st[:, 8:10], st[:, 8:10], l2b[:, 0:1], None, ALU.add))
                dve.sem_inc(S("si"), 1)
                layernorm(step, xn)
                dve.wait_ge(S("l2x_sig"), 2)
                for i in range(NT):
                    step(ts(tmp[:, i, :], tmp[:, i, :], 0.6, None, ALU.mult))
                    step(stt(out=tmp[:, i, :], in0=xn[:, i, :], scalar=1.0 - 0.6, in1=tmp[:, i, :], op0=ALU.mult, op1=ALU.add))
                residual(step, lambda i: tmp[:, i, :], 2)

                layernorm(step, xn)
                for i in range(NT):
                    step(V.tensor_tensor_reduce(out=tmp[:, i, :], in0=xn[:, i, :], in1=xn[:, i, :], scale=1.0, scalar=0.0,
                                                op0=ALU.mult, op1=ALU.add, accum_out=st[:, 4 + i:5 + i]))

                def quantise(src, n, k, dst, work, name):
                    step(ts(ve[:, 0:NT], st[:, 4:6], 1.0 / n, 1e-5, ALU.mult, ALU.add))
                    rsqrt(step, rs[:, 0:NT], ve[:, 0:NT])
                    for i in range(NT):
                        step(V.reduce_max(st[:, 6 + i:7 + i], src(i), AX, apply_absolute_value=True))
                    step(tt(st[:, 6:8], st[:, 6:8], rs[:, 0:NT], ALU.mult))
                    step(ts(st[:, 6:8], st[:, 6:8], 1e-5, None, ALU.max))
                    step(ts(st[:, 10:12], st[:, 6:8], 1.0 / 127.0, wdq[:, k:k + 1], ALU.mult, ALU.mult))
                    step(V.reciprocal(st[:, 6:8], st[:, 6:8]))
                    step(stt(out=rs[:, 0:NT], in0=st[:, 6:8], scalar=127.0, in1=rs[:, 0:NT], op0=ALU.mult, op1=ALU.mult))
                    for i in range(NT):
                        step(ts(work(i), src(i), rs[:, i:i + 1], -128.0, ALU.mult, ALU.max))
                        step(ts(work(i), work(i), 127.0, ROUND, ALU.min, ALU.add))
                        ts(dst(i), work(i), ROUND, None, ALU.subtract).then_inc(S(name), 1)

                quantise(lambda i: xn[:, i, :], D, 0, lambda i: q1[:, i, :], lambda i: tmp[:, i, :], "l2f_q1")
                for i in range(NT):
                    dve.wait_ge(S("l2f_up"), i + 1)
                    for hf in range(2):
                        cs = slice(hf * 512, (hf + 1) * 512)
                        step(stt(out=h2[:, i, cs], in0=bank[1 + 2 * i + hf][:, :], scalar=st[:, 10 + i:11 + i],
                                 in1=rowsF["L2_ffn_b1"][:, cs], op0=ALU.mult, op1=ALU.add))
                    dve.sem_inc(S("l2f_pre"), 1)
                for i in range(NT):
                    dve.wait_ge(S("l2f_gelu"), i + 1)
                    for hf in range(2):
                        step(V.bn_stats(bn[:, 2 * i + hf, :], h2[:, i, hf * 512:(hf + 1) * 512]))
                    step(V.bn_aggr(mv[:, i, :], bn[:, 2 * i:2 * i + 2, :].rearrange("p a s -> p (a s)")))
                step(ts(ve[:, 0:NT], mv[:, :, 1], 1e-5, None, ALU.add))
                rsqrt(step, rs[:, 0:NT], ve[:, 0:NT])
                for i in range(NT):
                    step(ts(h2[:, i, :], h2[:, i, :], mv[:, i, 0:1], rs[:, i:i + 1], ALU.subtract, ALU.mult))
                    step(tt(h2[:, i, :], h2[:, i, :], rowsF["L2_ffn_ln_g"][:, :], ALU.mult))
                    step(tt(h2[:, i, :], h2[:, i, :], rowsF["L2_ffn_ln_b"][:, :], ALU.add))
                    dve.sem_inc(S("l2f_ln"), 1)
                dve.wait_ge(S("l2f_sq"), 2)
                quantise(lambda i: h2[:, i, :], F1, 1, lambda i: q2[:, i, :], lambda i: h2s[:, i, :], "l2f_q2")
                for i in range(NT):
                    dve.wait_ge(S("l2f_down"), i + 1)
                    step(stt(out=tmp[:, i, :], in0=bank[7 * i][:, 0:D], scalar=st[:, 10 + i:11 + i],
                             in1=rowsD["L2_ffn_b2"][:, :], op0=ALU.mult, op1=ALU.add))
                residual(step, lambda i: tmp[:, i, :], 6)

                layernorm(step, xn, 0.25)
                dve.sem_inc(S("l3x_begun"), 1)
                attention(step, "l3x", xn[:, :, :], c[:, :, :])
                dve.wait_ge(S("l3x_proj"), 2)
                for i in range(NT):
                    step(tt(tmp[:, i, :], bank[5][:, i * D:(i + 1) * D], rowsD["L3_xattn_bc"][:, :], ALU.add))
                residual(step, lambda i: tmp[:, i, :], 3)

                layernorm(step, xn)
                dve.sem_inc(S("l3f_begun"), 1)
                step(*[tt(xl[:, i, :], xn[:, i, :], rowsD["L3_ffn_gamma"][:, :], ALU.mult) for i in range(NT)])
                step(*[tt(xl[:, i, :], xl[:, i, :], rowsD["L3_ffn_beta"][:, :], ALU.add) for i in range(NT)])
                dve.sem_inc(S("l3f_xl"), NT)
                step(*[V.tensor_tensor_reduce(out=tmp[:, i, :], in0=xl[:, i, :], in1=xl[:, i, :], scale=1.0, scalar=0.0,
                                              op0=ALU.mult, op1=ALU.add, accum_out=st[:, i:i + 1]) for i in range(NT)])
                rsqrt(step, rs[:, 0:NT], st[:, 0:NT])
                step(tt(st[:, 0:NT], st[:, 0:NT], rs[:, 0:NT], ALU.mult))
                step(ts(st[:, 0:NT], st[:, 0:NT], 1e-12, None, ALU.max))
                step(V.reciprocal(rs[:, 0:NT], st[:, 0:NT]))
                step(ts(rs[:, 0:NT], rs[:, 0:NT], sc_scale[:, 0:1], None, ALU.mult))
                dve.sem_inc(S("l3f_rs"), 1)
                for n in range(8):
                    ch, i = n // 2, n % 2
                    dve.wait_ge(S("logits_out"), n + 1)
                    V.reduce_max(rmx[:, i, ch:ch + 1], lg[:, i, ch * 512:(ch + 1) * 512], AX).then_inc(S("logits_max"), 1)
                dve.wait_ge(S("logits_max"), 8)
                step(V.tensor_reduce(ve[:, 0:NT], rmx[:, :, :], AX, ALU.max, negate=True))
                three_parts(step, [mst[:, :, s, 0] for s in range(3)], ve[:, 0:NT], nw[:, 0:NT])
                dve.sem_inc(S("row_parts"), 1)

                def slot_max(g):
                    dve.wait_ge(S("logitsT_ps"), g + 1)
                    V.reduce_max(cmx[:, 2 * g:2 * g + 2], bank[g][:, :].rearrange("p (e t) -> p e t", e=2), AX, negate=True)\
                        .then_inc(S("slots_max"), 1)

                def less_row_max(g):
                    tt(lT[:, 2 * g:2 * g + 2, :], bank[g][:, :].rearrange("p (e t) -> p e t", e=2),
                       rbc[:, :].unsqueeze(1).broadcast_to([P, 2, N]), ALU.add).then_inc(S("lT_less_max"), 1)

                for g in range(6):
                    slot_max(g)
                dve.wait_ge(S("row_max_all"), 1)
                step(V.tensor_copy(rbc[:, :], bank[7][:, 0:N]))
                dve.sem_inc(S("row_max_read"), 1)
                for g in range(4):
                    less_row_max(g)
                slot_max(6)
                slot_max(7)
                dve.wait_ge(S("slots_max"), 8)
                three_parts(step, [mst[:, 0, s, 0:SE] for s in range(3)], cmx[:, :], cmr[:, :])
                dve.sem_inc(S("slot_parts"), 1)
                for g in range(4, 8):
                    less_row_max(g)
                for ch in range(4):
                    dve.wait_ge(S("slot_max_all"), ch + 1)
                    lc = lg[:, :, ch * 512:(ch + 1) * 512]
                    tt(lc, lc, bank[4 + ch][:, :].unsqueeze(1).broadcast_to([P, NT, 512]), ALU.add).then_inc(S("logits_less_max"), 1)
                for ch in range(4):
                    dve.wait_ge(S("soft_up"), ch + 1)
                    up = bank[ch][:, 0:4 * (SH + 1)].rearrange("p (e h) -> p e h", e=4)
                    h, es = hs[:, 4 * ch:4 * ch + 4, 0:SH], slice(4 * ch, 4 * ch + 4)
                    step(V.reciprocal(cmr[:, es], up[:, :, SH]))
                    step(tt(h, up[:, :, 0:SH], cmr[:, es].unsqueeze(2).broadcast_to([P, 4, SH]), ALU.mult))
                    tt(h, h, b1[:, es, :], ALU.add).then_inc(S("soft_pre"), 1)
                for g in range(1, 8, 2):
                    dve.wait_ge(S("gathered_ps"), g + 1)
                    V.tensor_copy(aT[:, 2 * g:2 * g + 2, :], bank[4 + g % 4][0:SH + 1, :].rearrange("p (e t) -> p e t", e=2))\
                        .then_inc(S("gathered1"), 1)
                dve.wait_ge(S("soft_out"), 1)
                for i in range(NT):
                    step(V.reciprocal(st[:, i:i + 1], bank[i][:, D:D + 1]))
                    step(ts(st[:, i:i + 1], st[:, i:i + 1], gates[:, 7:8], None, ALU.mult))
                    stt(out=xs[:, bass.ts(b, NT), :][:, i, :], in0=bank[i][:, 0:D], scalar=st[:, i:i + 1], in1=x[:, i, :],
                        op0=ALU.mult, op1=ALU.add).then_inc(once("x_final"), 1)
                dve.wait_ge(once("x_final"), b * NT + NT)
                end_of_batch(dve)
                dve.wait_ge(once("batch_cleared"), b + (B + 1))

        @block.gpsimd
        def _(pool):
            G = nc.gpsimd
            step = Steps(pool, once("pool_step"))

            def select(t, compare, fill, base, pattern, m=1):
                step(G.affine_select(out=t, in_=t, compare_op=compare, fill=fill, base=base, pattern=pattern, channel_multiplier=m))

            step(G.memset(ident[:, :], 0.0))
            select(ident[:, :], ALU.not_equal, 1.0, 0, [[-1, P]])
            pool.sem_inc(once("consts"), 1)
            step(G.tensor_copy(identb[:, :], ident[:, :]))
            pool.sem_inc(once("consts"), 1)
            step(G.memset(ones[:, :], 1.0))
            pool.sem_inc(once("consts"), 1)
            step(G.memset(sel[:, :, :], 0.0))
            for k in range(3):
                select(sel[:, :, :], ALU.not_equal, 1.0, -32 * k, [[-1, 32], [0, P]])
            pool.sem_inc(once("consts"), 1)
            step(G.memset(mask_q[:, :, :], 0.0))
            select(mask_q[:, :, :], ALU.is_ge, MASKED, 0, [[P, NT], [-1, N]])
            step(G.memset(mask_t[:, :, :], 0.0))
            select(mask_t[:, :, :], ALU.is_ge, MASKED, 0, [[-P, NT], [1, N]], -1)
            step(G.memset(mst[:, :, :, :], 0.0))
            step(G.memset(vst[:, :, :, :], 0.0))
            pool.sem_inc(once("consts"), 1)
            step(G.memset(w2a[:, :, D:D + 1], 0.0))
            step(G.memset(w2a[SH:SH + 1, :, D:D + 1], 1.0))
            step(G.memset(zero_w[:, :], 0.0))
            step(G.memset(pick_hm[:, :, :], 0.0))
            step(G.memset(pick_l[:, :, :], 0.0))
            for k in range(2):
                t = pick_hm[:, 0:E // 2, :].rearrange("p q (e f) -> p q e f", e=2)
                select(t, ALU.not_equal, 1.0, -E * k, [[-2, E // 2], [-1, 2], [0, F]])
            t = pick_l[:, 0:E // 2, :].rearrange("p q (e f) -> p q e f", e=2)
            select(t, ALU.not_equal, 1.0, 0, [[-2, E // 2], [-1, 2], [0, F]])
            step(G.memset(pick_l[E:E + 1, E // 2:PAIRS, :], 1.0))
            step(G.memset(comb_l[E:E + 1, :], 1.0))
            with pool.Fori(0, B) as b:
                step = Steps(pool, S("pool_step_b"))
                pool.wait_ge(S("x_done"), 1)
                step(G.tensor_copy(xs[:, bass.ts(b, NT), :], x[:, :, :]))
                pool.wait_ge(S("xT"), 2)
                high = xh[:, :, bass.ts(b, N)]
                step(G.tensor_copy(high, xT[:, :, :]))
                step(G.tensor_tensor(xlo[:, :, bass.ts(b, N)], xT[:, :, :], high.bitcast(F32), ALU.subtract))
                pool.wait_ge(once("batch_arrived"), b * 3 + 3)
                pool.sem_inc(once("all_arrived"), 1)
                clear(pool)
                pool.sem_inc(once("batch_cleared"), 1)
            pool.sem_inc(once("picks"), 2)
            pool.sem_inc(once("hidden_used"), 4)
            with pool.Fori(0, PAIRS // SLOTN) as t:
                for k in range(SLOTN):
                    pool.wait_ge(once(f"experts_loaded{k}"), t * (5 * 16) + 5 * 16)
                    pool.wait_ge(once("hidden_used"), t * (2 * SLOTN) + (2 * k + 2))
                    pool.sem_inc(once("split_begins"), 1)
                    G.tensor_copy(wh[k % 2][:, :, :], wraw[k][:, :, :]).then_inc(once("weights_high"), 1)
                    pool.wait_ge(once("weights_high"), t * SLOTN + (k + 1))
                    pool.sem_inc(once("split_begins"), 1)
                    G.tensor_tensor(wl[k % 2][:, :, :], wraw[k][:, :, :], wh[k % 2][:, :, :].bitcast(F32), ALU.subtract)\
                        .then_inc(once("weights_split"), 1)
            pool.wait_ge(once("hidden_used"), 2 * PAIRS + 4)
            pool.sem_inc(once("prep_waits_experts"), 1)
            pool.wait_ge(once("prepared"), 1)
            pool.wait_ge(once("xs_updated"), 4)

            def attention(step, L, v):
                H, GG, HD, causal = ATTENTIONS[L]
                KV, K6 = H // GG, 6 * HD

                G.memset(vst[:, :, 0:KV, HD:HD + 1], 1.0).then_inc(S("att_v"), 1)
                if v is not None:
                    G.tensor_copy(vst[:, :, 0:KV, 0:HD], v.rearrange("p i (h d) -> p i h d", h=KV)).then_inc(S("att_v"), 1)
                else:
                    pool.sem_inc(S("att_v"), 1)

            with pool.Fori(0, B) as b:
                step = Steps(pool, S("pool_step_b"))
                pool.wait_ge(S("c_ready"), 1)
                pool.wait_ge(S("l1x_begun"), 1)
                attention(step, "l1x", c[:, :, :])
                pool.wait_ge(S("l1f_in"), 2)
                attention(step, "l1f", None)
                pool.wait_ge(S("l3x_begun"), 1)
                attention(step, "l3x", c[:, :, :])
                pool.wait_ge(S("l3f_begun"), 1)
                G.memset(xw[:, :, :, SH:SH + 1], 1.0).then_inc(S("ones_columns"), 1)
                G.memset(hs[:, :, SH:SH + 1], 1.0).then_inc(S("ones_columns"), 1)
                pool.wait_ge(once("batch_arrived"), b * 3 + (3 * B + 3))
                pool.sem_inc(once("all_arrived"), 1)
                clear(pool)
                pool.sem_inc(once("batch_cleared"), 1)


_INS = ['x', 'ctx_512', 'g_xattn', 'g_ffn', 'L0_xattn_W_k', 'L0_xattn_b_k', 'L0_xattn_ln_gamma', 'L0_xattn_ln_beta',
        'L0_ffn_router_w', 'L0_ffn_router_bias', 'L0_ffn_wg', 'L0_ffn_wu', 'L0_ffn_wd', 'L0_ffn_swg', 'L0_ffn_swu',
        'L0_ffn_swd', 'L1_ffn_ln1_w', 'L1_ffn_ln2_w', 'L1_ffn_Wq', 'L1_ffn_Wk', 'L1_ffn_Wv', 'L1_ffn_Wo', 'L1_ffn_A',
        'L1_ffn_B', 'L1_ffn_W_in_base', 'L1_ffn_W_up_base', 'L1_ffn_W_down', 'L2_xattn_W', 'L2_xattn_b', 'L2_ffn_w1',
        'L2_ffn_b1', 'L2_ffn_ln_g', 'L2_ffn_ln_b', 'L2_ffn_w2', 'L2_ffn_b2', 'L3_xattn_Wc', 'L3_xattn_bc',
        'L3_ffn_gamma', 'L3_ffn_beta', 'L3_ffn_mu', 'L3_ffn_scale', 'L3_ffn_W1', 'L3_ffn_b1', 'L3_ffn_W2', 'L3_ffn_b2']


def kernel(**inputs):
    import numpy as _np
    import concourse.bacc as _bacc
    from concourse import mybir as _mybir
    from concourse.bass_utils import run_bass_kernel_spmd as _run

    nc = _bacc.Bacc("TRN2", target_bir_lowering=False, num_devices=1)
    arrays, args = {}, {}
    for name in _INS:
        a = _np.ascontiguousarray(inputs[name])
        arrays[f"in_{name}_dram"] = a
        args[name] = nc.dram_tensor(f"in_{name}_dram", a.shape, _mybir.dt.from_np(a.dtype), kind="ExternalInput").ap()
    out = nc.dram_tensor("out_0_dram", (B, N, D), _mybir.dt.float32, kind="ExternalOutput").ap()
    flamingo(nc, args, out)
    r = _run(nc, [arrays], core_ids=[0])
    return r.results[0]["out_0_dram"]
```

```python
from contextlib import ExitStack

import numpy as np

import concourse.bass as bass
from concourse import mybir

P = 128
ALU = mybir.AluOpType
ACT = mybir.ActivationFunctionType
F32 = mybir.dt.float32
FR = mybir.dt.float32r
BF16 = mybir.dt.bfloat16
I32 = mybir.dt.int32
AX = mybir.AxisListType.X

B, N, D = 4, 256, 256
NT = N // P
DC = D // P
CD = 64
E, F = 64, 64
TOPK = 4
PAIRS = E // 2 + 4
F1 = 1024
R = 16
SE, SS, SH = 16, 128, 64
SLOTS = SE * SS
MASKED = -1e30
BIG = 3e38
ROUND = 1.5 * 2.0 ** 23
TOKENS = B * N
T0 = 2 * NT
HALVES = TOKENS // 512
ATTENTIONS = {"l1x": (32, 4, 8, False), "l1f": (16, 1, 16, True), "l3x": (16, 4, 16, False)}


K_SLOTS = ((0, 1, 4), ((2, 0), (5, 0), (3, 1)))
Q_SLOTS = ((0, 2, 5), ((1, 0), (4, 0), (3, 2)))

ATT_COUNTS = {}
for _L, (_H, _G, _HD, _) in ATTENTIONS.items():
    _K, _GR = _H // _G // 4, _H // 8
    for _name, _n in (("parts", 2), ("partsT", _K + 2 * _GR), ("left0", (_K + 11 * _GR + 1) // 2),
                      ("left1", (_K + 11 * _GR) // 2), ("q_scores", _H), ("max_parts", _GR), ("mT_ps", _GR),
                      ("v", 2 if _G > 1 else 3), ("probs", _H), ("scores", _H), ("pv", _H),
                      ("oT", _GR), ("o", _GR), ("attn", NT)):
        ATT_COUNTS.setdefault(_name, {})[_L] = _n


def turns(L, g):
    H, G = ATTENTIONS[L][:2]
    return 2 if G == 1 else (H // G // 4 if g == 0 else 0)


def first(L, g):
    return sum(turns(L, k) + 11 for k in range(g))


def queries_at(L, g):
    return first(L, g) + turns(L, g)


def turned_before(L, g):
    return sum(turns(L, k) + 2 for k in range(g))


def before(L, name):
    return ATT_COUNTS[name]["l1x"] if L == "l1f" else 0


class Steps:

    def __init__(self, eng, sem):
        self.eng, self.sem, self.n = eng, sem, 0

    def __call__(self, *instructions):
        for ins in instructions:
            ins.then_inc(self.sem, 1)
        self.n += len(instructions)
        self.eng.wait_ge(self.sem, self.n)


def flamingo(nc, I, out):
    with ExitStack() as ctx:
        sems, batch_sems = {}, []

        def once(name):
            if name not in sems:
                sems[name] = ctx.enter_context(nc.semaphore(name))
            return sems[name]

        def S(name):
            if name not in sems:
                sems[name] = ctx.enter_context(nc.semaphore(name))
                batch_sems.append(sems[name])
            return sems[name]

        top = [(nc.sbuf_base + 63) // 64 * 64]
        high = [0]

        def sb(name, shape, dt=F32):
            size = int(np.prod(shape[1:])) * (2 if dt == BF16 else 4)
            t = nc.alloc_sbuf_tensor_at(name, list(shape), dt, offset=top[0])
            top[0] += (size + 31) // 32 * 32
            high[0] = max(high[0], top[0])
            return t

        bank = [ctx.enter_context(nc.psum_tensor(f"bank{k}", [P, 512], F32)) for k in range(8)]
        bankb = [k[:, :].bitcast(BF16) for k in bank]

        xs = sb("xs", [P, B * NT, D])
        ctxs = sb("ctxs", [P, B * NT, CD])
        ident = sb("ident", [P, P])
        identb = sb("identb", [P, P], BF16)
        ones = sb("ones", [P, P])
        sel = sb("sel", [96, 16, P], BF16)
        sel2 = sb("sel2", [96, 16, P], BF16)
        parity = sb("parity", [P, 2])
        mask_q = sb("mask_q", [P, NT, N], BF16)
        mask_t = sb("mask_t", [P, NT, N], BF16)
        gates = sb("gates", [P, 8])
        mst = sb("mst", [P, NT, 3, 32], BF16)
        vst = sb("vst", [P, NT, 16, 32])
        wkT = sb("wkT", [CD, CD])
        bk_col = sb("bk_col", [CD, 1])
        bk_row = sb("bk_row", [P, CD])
        sc_scale = sb("sc_scale", [P, 1])
        l2b = sb("l2b", [P, 1])
        l2wi = sb("l2wi", [P, CD])
        l2wj = sb("l2wj", [CD, P])
        at_wqkvT = top[0]
        wqkvT = sb("wqkvT", [P, DC, 3 * D])
        wcT = sb("wcT", [P, DC, D])
        early = top[0]
        winT = sb("winT", [P, DC, F1])
        wupT = sb("wupT", [P, DC, F1])
        wdT = sb("wdT", [P, F1 // P, D])
        w1qT = sb("w1qT", [P, DC, F1], BF16)
        w2qT = sb("w2qT", [P, F1 // P, D], BF16)
        mun = sb("mun", [P, DC, SLOTS])
        w1s = sb("w1s", [P, DC, SE, SH])
        w2a = sb("w2a", [SH + 1, SE, D + 1])
        rowsD = {n: sb("row_" + n, [P, D]) for n in
                 ("L0_xattn_ln_gamma", "L0_xattn_ln_beta", "L1_ffn_ln1_w", "L1_ffn_ln2_w", "L2_ffn_b2",
                  "L3_xattn_bc", "L3_ffn_gamma", "L3_ffn_beta")}
        rowsF = {n: sb("row_" + n, [P, F1]) for n in ("L2_ffn_b1", "L2_ffn_ln_g", "L2_ffn_ln_b")}
        wa = sb("wa", [P, DC, R])
        am = sb("am", [P, DC, R])
        bm = sb("bm", [R, F1])
        b1 = sb("b1", [P, SE, SH])
        wdq = sb("wdq", [P, 2])
        at_x = top[0]
        x = sb("x", [P, NT, D])
        c = sb("c", [P, NT, CD])
        xn = sb("xn", [P, NT, D])
        xT = sb("xT", [P, DC, N])
        at_cT = top[0]
        cT = sb("cT", [CD, N])
        tmp = sb("tmp", [P, NT, D])
        bn = sb("bn", [P, T0, 6])
        mv = sb("mv", [P, T0, 2])
        ve = sb("ve", [P, 4])
        rs = sb("rs", [P, 4])
        nw = sb("nw", [P, 4])
        st = sb("st", [P, 16])
        rbc = sb("rbc", [P, N])
        cmx = sb("cmx", [P, SE])
        cmr = sb("cmr", [P, SE])
        cmT = sb("cmT", [96, P], BF16)
        region = top[0]

        xh = sb("xh", [P, DC, TOKENS], FR)
        mu2 = sb("mu2", [P, DC, SLOTS])
        comb = sb("comb", [P, TOKENS], FR)
        picks = sb("picks", [P, E // 2, P], BF16)
        pick = [sb(f"pick{k}", [P, P], FR) for k in range(2)]
        SLOTN = 4
        wraw = [sb(f"wraw{k}", [P, 3, D]) for k in range(SLOTN)]
        wg = [w[:, 0, :].rearrange("p (c f) -> p c f", c=DC) for w in wraw]
        wu = [w[:, 1, :].rearrange("p (c f) -> p c f", c=DC) for w in wraw]
        wd = [w[:, 2, :] for w in wraw]
        zero_w = sb("zero_w", [P, P], BF16)
        hidden_at = top[0]
        sg = [sb(f"sg{k}", [P, 512]) for k in range(2)]
        hu = [sb(f"hu{k}", [P, 512]) for k in range(2)]
        hh = [sb(f"hh{k}", [P, 512]) for k in range(2)]
        after_hidden = top[0]
        top[0] = hidden_at
        c0 = sb("c0", [P, T0, CD])
        kv = sb("kv", [P, T0, CD])
        oT = sb("oT", [CD, T0 * P])
        rw = sb("rw", [P, DC, E])
        rb = sb("rb", [P, E])
        lg0 = sb("lg0", [P, T0, E])
        lb0 = sb("lb0", [P, T0, E + TOPK])
        lr0 = sb("lr0", [P, T0, E + TOPK])
        cb0 = sb("cb0", [P, T0, E])
        ct0 = sb("ct0", [P, T0, E])
        ct2 = sb("ct2", [P, T0, 2, E])
        m8 = sb("m8", [P, T0, 8])
        after_experts = max(top[0], after_hidden)
        top[0] = region
        yT = sb("yT", [P, DC, TOKENS])
        top[0] = early
        xlo = sb("xlo", [P, DC, TOKENS], FR)
        wh = [sb(f"wh{k}", [P, 3, D], FR) for k in range(2)]
        wl = [sb(f"wl{k}", [P, 3, D], FR) for k in range(2)]
        hhi = [sb(f"hhi{k}", [P, 512], FR) for k in range(2)]
        hlo = [sb(f"hlo{k}", [P, 512], FR) for k in range(2)]
        assert top[0] <= early + 32 * 1024
        top[0] = early + DC * TOKENS * 4
        xn0 = sb("xn0", [P, T0, D])
        tmp0 = sb("tmp0", [P, T0, D])
        xT0 = sb("xT0", [P, DC, T0 * P])
        cT0 = sb("cT0", [CD, T0 * P])
        kvT = sb("kvT", [CD, T0 * P])
        l2_raw = []
        for k, place in enumerate((at_wqkvT, at_x)):
            top[0] = place
            l2_raw.append(sb(f"l2_raw{k}", [P, 2048]))
        top[0] = after_experts

        top[0] = region
        top[0] += DC * TOKENS * 4 + DC * SLOTS * 4
        stage = [sb(f"stage{k}", [P, 2048]) for k in range(4)]
        wo = sb("wo", [P, DC, D])
        top[0] = region
        tern = [sb(f"tern{k}", [P, 2048], BF16) for k in range(2)]
        top[0] = region
        qst = sb("qst", [P, NT, 6 * D], BF16)
        kst = sb("kst", [P, NT, 6 * D], BF16)
        qT = sb("qT", [96, 32, N], BF16)
        kT = sb("kT", [96, 16, N], BF16)
        prob = [sb(f"prob{k}", [P, 512]) for k in range(4)]
        mx = sb("mx", [P, NT, 32])
        mr = sb("mr", [P, NT, 32])
        qr = sb("qr", [P, NT, D])
        after_otr = top[0]
        top[0] = at_cT
        mT = sb("mT", [96, 2, N], BF16)
        top[0] = after_otr
        otr = sb("otr", [P, 4, 512])
        after_otr = top[0]
        top[0] -= 4 * 512 * 4
        qf = sb("qf", [P, NT, D])
        kf = sb("kf", [P, NT, D])
        top[0] = after_otr
        rc = sb("rc", [P, 4, 16])
        at = sb("at", [P, NT, D])
        atT = sb("atT", [P, DC, N])
        hT = sb("hT", [P, DC, N])
        modT, mh = rbc[0:R, :], cT[0:R, :]
        top[0] = region
        sgf = [sb(f"sgf{k}", [P, N]) for k in range(2)]
        gu = sb("gu", [P, F1 // P, N])
        top[0] = region
        h2 = sb("h2", [P, T0, F1])
        q2 = sb("q2", [P, T0, F1], BF16)
        q2T = sb("q2T", [P, F1 // P, T0 * P], BF16)
        q1 = sb("q1", [P, T0, D], BF16)
        q1T = sb("q1T", [P, DC, T0 * P], BF16)
        xn2 = sb("xn2", [P, T0, D])
        tmp2 = sb("tmp2", [P, T0, D])
        bn2 = sb("bn2", [P, T0, 2, 6])
        c2 = sb("c2", [P, T0, CD])
        cT2 = sb("cT2", [CD, T0 * P])
        top[0] = region
        aT = sb("aT", [SH + 1, SE, N])
        top[0] = region
        lg = sb("lg", [P, NT, SLOTS])
        lT = sb("lT", [P, SE, N])
        xw = sb("xw", [P, NT, SE, SH + 1])
        hs = sb("hs", [P, SE, SH + 1])
        xl = sb("xl", [P, NT, D])
        rmx = sb("rmx", [P, NT, 4])
        mT3 = sb("mT3", [96, N], BF16)
        assert high[0] <= nc.sbuf_usable_end

        block = ctx.enter_context(nc.Block())

        def blocks_of(w, rows, cols, dst):
            groups = []
            for ic in range(cols // P):
                for oc0 in range(0, rows // P, 4):
                    n = min(4, rows // P - oc0)
                    groups.append(([w[:, (oc0 + j) * cols + ic * P:(oc0 + j) * cols + ic * P + P] for j in range(n)],
                                   dst(ic, oc0 * P, n * P)))
            return groups

        PREP = []
        for k in range(3):
            PREP += blocks_of(stage[0][:, k * 512:(k + 1) * 512], D, D,
                              lambda ic, o, n, k=k: wqkvT[:, ic, k * D + o:k * D + o + n])
        PREP += blocks_of(stage[0][:, 1536:2048], D, D, lambda ic, o, n: wcT[:, ic, o:o + n])
        PREP += blocks_of(stage[1], F1, D, lambda ic, o, n: winT[:, ic, o:o + n])
        FIRST_STAGES = len(PREP)
        PREP += blocks_of(stage[2], F1, D, lambda ic, o, n: wupT[:, ic, o:o + n])
        PREP += blocks_of(stage[3], D, F1, lambda ic, o, n: wdT[:, ic, o:o + n])
        PREPB = blocks_of(tern[0], F1, D, lambda ic, o, n: w1qT[:, ic, o:o + n])
        PREPB += blocks_of(tern[1], D, F1, lambda ic, o, n: w2qT[:, ic, o:o + n])

        REST = len(rowsD) - 2 + len(rowsF) + 12

        def clear(eng):
            nums = sorted(s.num for s in batch_sems)
            first = nums[0]
            for a, b in zip(nums, nums[1:] + [None]):
                if b != a + 1:
                    eng.sem_clear(range(first, a + 1))
                    first = b

        def end_of_batch(eng):
            eng.sem_inc(once("batch_arrived"), 1)

        @block.sync
        def _(sp):
            W = sp.dma_start
            ld = once("first_loads")
            W(xs[:, :, :], I["x"].rearrange("b (i p) d -> p (b i) d", p=P)).then_inc(once("x_loaded"), 16)
            W(ctxs[:, :, :], I["ctx_512"].rearrange("b (i p) d -> p (b i) d", p=P)).then_inc(once("x_loaded"), 16)
            W(wkT[:, :], I["L0_xattn_W_k"]).then_inc(ld, 16)
            W(bk_col[:, :], I["L0_xattn_b_k"].rearrange("(p a) -> p a", a=1)).then_inc(ld, 16)
            W(bk_row[:, :], I["L0_xattn_b_k"].partition_broadcast(P)).then_inc(ld, 16)
            for n in ("L0_xattn_ln_gamma", "L0_xattn_ln_beta"):
                W(rowsD[n][:, :], I[n].partition_broadcast(P)).then_inc(ld, 16)
            W(gates[:, 0:4], I["g_xattn"].partition_broadcast(P)).then_inc(ld, 16)
            W(gates[:, 4:8], I["g_ffn"].partition_broadcast(P)).then_inc(ld, 16)
            W(rw[:, :, :], I["L0_ffn_router_w"].rearrange("(p c) e -> p c e", c=DC)).then_inc(ld, 16)
            W(rb[:, :], I["L0_ffn_router_bias"].partition_broadcast(P)).then_inc(ld, 16)

            def load_experts(k, pair, shared):
                sem = once(f"experts_loaded{k}")
                for w, name in ((wg[k], "g"), (wu[k], "u")):
                    for e in range(2):
                        if shared is None:
                            src = I["L0_ffn_w" + name].rearrange("(q e) (p c) f -> e q p c f", e=2, c=DC)[e, pair]
                        else:
                            src = I["L0_ffn_sw" + name].rearrange("s (p c) (q e f) -> s q e p c f", c=DC, e=2, f=F)[
                                shared // 2, shared % 2, e]
                        W(w[:, :, e * F:(e + 1) * F], src).then_inc(sem, 16)
                if shared is None:
                    W(wd[k][:, :], I["L0_ffn_wd"].rearrange("(q e) f d -> q (e f) d", e=2)[pair]).then_inc(sem, 16)
                else:
                    W(wd[k][:, :], I["L0_ffn_swd"].rearrange("s (q p) d -> (s q) p d", p=P)[shared]).then_inc(sem, 16)

            for k in range(SLOTN):
                load_experts(k, k, None)
            rest = once("rest_loads")
            for n in list(rowsD)[2:]:
                W(rowsD[n][:, :], I[n].partition_broadcast(P)).then_inc(rest, 16)
            for n in rowsF:
                W(rowsF[n][:, :], I[n].partition_broadcast(P)).then_inc(rest, 16)
            W(sc_scale[:, :], I["L3_ffn_scale"].partition_broadcast(P)).then_inc(rest, 16)
            W(l2b[:, :], I["L2_xattn_b"].partition_broadcast(P)).then_inc(rest, 16)
            W(l2wi[:, :], I["L2_xattn_W"][0, 0:CD].partition_broadcast(P)).then_inc(rest, 16)
            W(l2wj[:, 0:1], I["L2_xattn_W"].rearrange("a (t p) -> t p a", p=CD)[1]).then_inc(rest, 16)
            W(mun[:, :, :], I["L3_ffn_mu"].rearrange("(c p) e s -> p c (e s)", p=P)).then_inc(rest, 16)
            for cc in range(DC):
                W(w1s[:, cc, :, :], I["L3_ffn_W1"].rearrange("e (c p) h -> c p e h", p=P)[cc]).then_inc(rest, 16)
            W(w2a[0:SH, :, 0:D], I["L3_ffn_W2"].rearrange("e h d -> h e d")).then_inc(rest, 16)
            W(w2a[SH:SH + 1, :, 0:D], I["L3_ffn_b2"].rearrange("(a e) d -> a e d", a=1)).then_inc(rest, 16)
            W(am[:, :, :], I["L1_ffn_A"].rearrange("(c p) r -> p c r", p=P)).then_inc(rest, 16)
            W(bm[:, :], I["L1_ffn_B"]).then_inc(rest, 16)
            W(b1[:, :, :], I["L3_ffn_b1"].partition_broadcast(P)).then_inc(rest, 16)
            def stage_load(to, n, cols, sem):
                W(to[:, :].rearrange("p (o i) -> p o i", i=cols),
                  I[n].rearrange("(o p) i -> p o i", p=P)).then_inc(sem, 16)

            with sp.Fori(0, E // 2 // SLOTN - 1) as t:
                for k in range(SLOTN):
                    sp.wait_ge(once("downs_split"), t * SLOTN + (k + 1))
                    sp.sem_inc(once("went_on"), 1)
                    load_experts(k, t * SLOTN + (SLOTN + k), None)
            sp.wait_ge(once("picks"), 2)
            stage_load(l2_raw[0], "L2_ffn_w1", D, once("l2_loaded"))
            stage_load(l2_raw[1], "L2_ffn_w2", F1, once("l2_loaded"))
            for k in range(SLOTN):
                sp.wait_ge(once("downs_split"), E // 2 - SLOTN + k + 1)
                load_experts(k, None, k)
            sp.wait_ge(once("hidden_used"), 2 * PAIRS + 4)
            sp.wait_ge(once("experts_out"), 2 * HALVES)
            stg = once("stage_loaded")
            for k, n in enumerate(("Wq", "Wk", "Wv")):
                W(stage[0][:, k * 512:(k + 1) * 512].rearrange("p (o i) -> p o i", i=D),
                  I["L1_ffn_" + n].rearrange("(o p) i -> p o i", p=P)).then_inc(stg, 16)
            W(stage[0][:, 1536:2048].rearrange("p (o i) -> p o i", i=D),
              I["L3_xattn_Wc"].rearrange("(o p) i -> p o i", p=P)).then_inc(stg, 16)
            stage_load(stage[1], "L1_ffn_W_in_base", D, stg)
            stg = once("stage_rest_loaded")
            stage_load(stage[2], "L1_ffn_W_up_base", D, stg)
            stage_load(stage[3], "L1_ffn_W_down", F1, stg)
            W(wo[:, :, :], I["L1_ffn_Wo"].rearrange("(o p) i -> p o i", p=P)).then_inc(stg, 16)
            with sp.Fori(0, B) as b:
                sp.wait_ge(once("x_final"), b * NT + NT)
                sp.sem_inc(once("went_on"), 1)
                W(out.rearrange("b (i p) d -> b p i d", p=P)[b], xs[:, bass.ts(b, NT), :]).then_inc(once("x_out"), 16)
            sp.wait_ge(once("x_out"), B * 16)

        def four_transposes(pe, dst, src, ident_, strided=False):
            for cc in range(DC):
                for i in range(NT):
                    s = src[:, i, cc:D:DC] if strided else src[:, i, cc * P:(cc + 1) * P]
                    last = pe.transpose(dst[:, cc * N + i * P:cc * N + i * P + P], s, ident_)
            return last

        @block.tensor
        def _(pe):
            mm = pe.matmul
            pe.wait_ge(once("first_loads"), 9 * 16)
            pe.wait_ge(once("consts"), 2)
            pe.transpose(bank[0][0:CD, 0:CD], wkT[:, :], ident[0:CD, 0:CD]).then_inc(once("wk_turned"), 1)
            pe.wait_ge(once("wkT_ready"), 1)

            def keep_clock(k, n):
                for _ in range(n):
                    mm(bank[k][:, :], identb[:, :], mask_q[:, :, :], start=True, stop=True, skip_group_check=True)

            def transposes0(first_bank, strided=False):
                for cc in range(DC):
                    for i in range(T0):
                        src = xn0[:, i, cc:D:DC] if strided else xn0[:, i, cc * P:(cc + 1) * P]
                        last = pe.transpose(bank[first_bank + cc][:, i * P:(i + 1) * P], src, ident[:, :])
                    last.then_inc(S("xT_ps"), 1)

            with pe.Fori(0, B // 2) as b:
                pe.wait_ge(S("c_ready"), 1)
                for i in range(T0):
                    last = pe.transpose(bank[0][0:CD, i * P:(i + 1) * P], c0[:, i, :], ident[:, :])
                last.then_inc(S("p0"), 1)
                pe.wait_ge(S("cT"), 1)
                mm(bank[1][0:CD, :], wkT[:, :], cT0[:, :], start=True, stop=True).then_inc(S("kvT_ps"), 1)
                for i in range(T0):
                    last = mm(bank[2][:, i * CD:(i + 1) * CD], cT0[:, i * P:(i + 1) * P], wkT[:, :], start=True, stop=True)
                last.then_inc(S("kv_ps"), 1)
                pe.wait_ge(S("xn"), 1)
                transposes0(3)
                pe.wait_ge(S("kv"), 1)
                pe.wait_ge(S("xT"), 2)
                for bb in range(2):
                    for j in range(DC):
                        last = mm(bank[5][0:CD, bb * N:(bb + 1) * N], kv[:, 2 * bb + j, :], xT0[:, j, bb * N:(bb + 1) * N],
                                  start=j == 0, stop=j == DC - 1)
                last.then_inc(S("oT_ps"), 1)
                pe.wait_ge(S("oT"), 1)
                pe.wait_ge(S("kvT"), 1)
                for i in range(T0):
                    mm(bank[6 + i // 2][:, i % 2 * N:(i % 2 + 1) * N], oT[:, i * P:(i + 1) * P],
                       kvT[:, i // 2 * N:(i // 2 + 1) * N], start=True, stop=True).then_inc(S("sim_ps"), 1)
                pe.wait_ge(S("xn"), 2)
                transposes0(0, True)
                pe.wait_ge(S("xT"), 4)
                for i in range(T0):
                    for cc in range(DC):
                        last = mm(bank[2][:, i * E:(i + 1) * E], xT0[:, cc, i * P:(i + 1) * P], rw[:, cc, :],
                                  start=cc == 0, stop=cc == DC - 1)
                last.then_inc(S("router_ps"), 1)
                pe.wait_ge(S("comb"), 1)
                for i in range(T0):
                    last = pe.transpose(bank[3][:, i * P:(i + 1) * P], ct2[:, i, :, :], ident[:, :])
                last.then_inc(S("comb_ps"), 1)
                end_of_batch(pe)
                pe.wait_ge(once("batch_cleared"), b + 1)

            def up(k, h, u, pair, shared=False):
                n = 3 * (2 * k + h)
                tok = slice(h * 512, (h + 1) * 512)
                if h == 0:
                    pe.wait_ge(once("weights_split"), pair + 1)
                if not (isinstance(u, int) and u == 0):
                    pe.wait_ge(once("gate_used"), u)
                    pe.wait_ge(once("hidden_made"), u)
                for m, made in ((0, "gate_made"), (1, "up_made")):
                    for j, (w, v) in enumerate(((wh, xh), (wh, xlo), (wl, xh))):
                        for cc in range(DC):
                            last = mm(bank[4 + (n + m) % 4][:, :], w[k % 2][:, m, cc * P:(cc + 1) * P], v[:, cc, tok],
                                      start=j == 0 and cc == 0, stop=j == 2 and cc == 1)
                    last.then_inc(once(made), 1)
                pe.wait_ge(once("up_used"), u + 2)
                if not shared:
                    if h == 0:
                        pe.wait_ge(once("pick_ready"), pair + 1)
                    mm(bank[4 + (n + 2) % 4][:, :], pick[k % 2][:, :], comb[:, tok], start=True, stop=True)\
                        .then_inc(once("weight_made"), 1)

            def down(k, h, u, pair, last_pair=False):
                pe.wait_ge(once("hidden_made"), u + 2)
                if h == 0:
                    pe.wait_ge(once("downs_split"), pair + 1)
                for m in range(DC):
                    for j, (w, v) in enumerate(((wh, hhi), (wl, hhi), (wh, hlo))):
                        last = mm(bank[2 * m + h][:, :], w[k % 2][:, 2, m * P:(m + 1) * P], v[h][:, :],
                                  start=False, stop=last_pair and j == 2, skip_group_check=True)
                last.then_inc(once("hidden_used"), 1)

            pe.wait_ge(once("consts"), 4)
            pe.wait_ge(once("sel_ready"), 1)
            pe.wait_ge(once("picks"), 2)
            for h in range(HALVES):
                for m in range(DC):
                    mm(bank[2 * m + h][:, :], zero_w[:, :], mask_q[:, :, :], start=True, stop=False,
                       skip_group_check=True)
            up(0, 0, 0, 0)
            with pe.Fori(0, E // 2 // SLOTN) as t:
                for k in range(SLOTN):
                    for h in range(HALVES):
                        u = 2 * k + h
                        if u + 1 < 2 * SLOTN:
                            up((u + 1) // 2, (u + 1) % 2, t * 8 + (u + 1), t * SLOTN + (u + 1) // 2)
                        else:
                            up(0, 0, t * 8 + 8, t * SLOTN + SLOTN)
                        down(k, h, t * 8 + u, t * SLOTN + k)
            T = E // 2 // SLOTN
            for u in range(2 * SLOTN):
                if u + 1 < 2 * SLOTN:
                    up((u + 1) // 2, (u + 1) % 2, T * 8 + u + 1, T * SLOTN + (u + 1) // 2, shared=True)
                down(u // 2, u % 2, T * 8 + u, T * SLOTN + u // 2, last_pair=u // 2 == SLOTN - 1)
            pe.wait_ge(once("experts_out"), 2 * HALVES)
            for k in range(4):
                for i in range(2):
                    for m in range(DC):
                        last = pe.transpose(bank[4 + k][:, i * D + m * P:i * D + (m + 1) * P],
                                            yT[:, m, (2 * k + i) * P:(2 * k + i + 1) * P], ident[:, :])
                last.then_inc(once("y_rows"), 1)

            pe.wait_ge(once("xs_updated"), 4)
            pe.wait_ge(once("abs_sums"), 2)
            mm(bank[4][:, 0:2], ones[:, :], st[:, 0:2], start=True, stop=True).then_inc(once("abs_total"), 1)
            pe.wait_ge(once("mu_steps"), 1)
            for e in range(SE):
                for cc in range(DC):
                    last = mm(bank[5][:, e:e + 1], mu2[:, cc, e * SS:(e + 1) * SS], ones[:, 0:1], start=cc == 0, stop=cc == 1)
            last.then_inc(once("mu_products"), 1)
            pe.wait_ge(once("mu_steps"), 3)
            pe.transpose(bankb[6][0:96, 0:P], mst[:, 0, :, :], identb[:, :]).then_inc(once("mu_products"), 1)
            pe.wait_ge(once("mu_partsT"), 1)
            for e in range(SE):
                last = mm(bank[4 + e // 4][:, e % 4 * SS:(e % 4 + 1) * SS], sel[:, e, :], cmT[:, :], start=True, stop=True)
            last.then_inc(once("mu_products"), 1)
            pe.wait_ge(once("stage_loaded"), 5 * 16)
            for g, (srcs, dst) in enumerate(PREP + PREPB):
                if g >= 4:
                    pe.wait_ge(once("prep_done"), g - 3)
                if g == FIRST_STAGES:
                    pe.wait_ge(once("stage_rest_loaded"), 3 * 16)
                if g == len(PREP):
                    pe.wait_ge(once("ternary"), 2)
                for j, src in enumerate(srcs):
                    if g < len(PREP):
                        last = pe.transpose(bank[g % 4][:, j * P:(j + 1) * P], src, ident[:, :])
                    else:
                        last = pe.transpose(bankb[g % 4][:, j * P:(j + 1) * P], src, identb[:, :])
                last.then_inc(once("prep_made"), 1)
            g = len(PREP + PREPB)
            pe.wait_ge(once("prep_done"), g - 3)
            for m in range(DC):
                for cc in range(DC):
                    last = mm(bank[g % 4][:, m * R:(m + 1) * R], wo[:, cc, m * P:(m + 1) * P], am[:, cc, :],
                              start=cc == 0, stop=cc == DC - 1)
            last.then_inc(once("wa_made"), 1)
            pe.wait_ge(once("prepared"), 1)
            pe.wait_ge(once("prep_done"), len(PREP + PREPB))

            def attention(L):
                H, G, HD, causal = ATTENTIONS[L]
                KV, K6, GR = H // G, 6 * HD, H // 8
                q_at = lambda g: queries_at(L, g)

                def free(r):
                    if r >= 2:
                        pe.wait_ge(S(f"att_left{r % 2}"), before(L, f"left{r % 2}") + r // 2)

                def has_left(r):
                    pe.wait_ge(S(f"att_left{r % 2}"), before(L, f"left{r % 2}") + r // 2 + 1)

                def turn(r, src, h4):
                    free(r)
                    for j in range(4):
                        h = 4 * h4 + j
                        for i in range(NT):
                            last = pe.transpose(bankb[r % 2][0:K6, j * N + i * P:j * N + (i + 1) * P],
                                                src[:, i, h * K6:(h + 1) * K6], identb[:, :])
                    last.then_inc(S("att_partsT"), 1)

                def turn_group(g):
                    for m in range(turns(L, g)):
                        turn(first(L, g) + m, kst, 2 * g + m)
                    for m in range(2):
                        turn(q_at(g) + m, qst, 2 * g + m)

                def by_query(g, j):
                    r, i, u = q_at(g) + 2 + j, j // 4, 4 * g + j % 4
                    if j == 0:
                        for k in range(first(L, g), q_at(g) + 2):
                            has_left(k)
                    free(r)
                    if causal:
                        mm(bank[r % 2][:, :], identb[:, :], mask_q[:, i:i + 1, :].broadcast_to([P, 2, N]),
                           start=True, stop=False, skip_group_check=True)
                    for e in range(2):
                        h = 2 * u + e
                        last = mm(bank[r % 2][:, e * N:(e + 1) * N], qT[0:K6, h, i * P:(i + 1) * P], kT[0:K6, h // G, :],
                                  start=not causal, stop=True, skip_group_check=True)
                    last.then_inc(S("att_q_scores"), 1)

                def turn_maxima(g):
                    r = q_at(g) + 10
                    pe.wait_ge(S("att_max_parts"), before(L, "max_parts") + g + 1)
                    free(r)
                    for i in range(NT):
                        last = pe.transpose(bankb[r % 2][0:96, i * P:(i + 1) * P], mst[:, i, :, :], identb[:, :])
                    last.then_inc(S("att_mT_ps"), 1)

                def by_key(n):
                    u, ti, b_ = n // 2, n % 2, 2 + n % 2
                    if n % 8 == 0:
                        has_left(q_at(n // 8) + 10)
                    if n >= 2:
                        pe.wait_ge(S("att_probs"), before(L, "probs") + n - 1)
                    if causal:
                        mm(bank[b_][:, :], identb[:, :], mask_t[:, ti:ti + 1, :].broadcast_to([P, 2, N]),
                           start=True, stop=False, skip_group_check=True)
                    mm(bank[b_][:, :], sel2[:, u, :], mT[:, :, :], start=not causal, stop=False, skip_group_check=True)
                    if G > 1:
                        last = mm(bank[b_][:, :], kT[0:K6, 2 * u // G, ti * P:(ti + 1) * P], qT[0:K6, 2 * u:2 * u + 2, :],
                                  start=False, stop=True, skip_group_check=True)
                    else:
                        for e in range(2):
                            h = 2 * u + e
                            last = mm(bank[b_][:, e * N:(e + 1) * N], kT[0:K6, h, ti * P:(ti + 1) * P], qT[0:K6, h, :],
                                      start=False, stop=True, skip_group_check=True)
                    last.then_inc(S("att_scores"), 1)

                def weighted(n):
                    u, ti = n // 2, n % 2
                    pe.wait_ge(S("att_probs"), before(L, "probs") + n + 1)
                    strip = slice(32 * (u % 4), 32 * (u % 4) + 32)
                    if G > 1:
                        last = mm(bank[4 + u // 4][strip, :], vst[:, ti, 2 * u // G, :], prob[n % 4][:, :],
                                  start=ti == 0, stop=ti == 1, skip_group_check=True)
                    else:
                        for e in range(2):
                            last = mm(bank[4 + u // 4][strip, e * N:(e + 1) * N], vst[:, ti, 2 * u + e, :],
                                      prob[n % 4][:, e * N:(e + 1) * N], start=ti == 0 and e == 0, stop=ti == 1,
                                      skip_group_check=True)
                    last.then_inc(S("att_pv"), 1)

                def rows_again(g):
                    pe.wait_ge(S("att_oT"), before(L, "oT") + g + 1)
                    for e in range(2):
                        for i in range(NT):
                            last = pe.transpose(bank[4 + g][:, (2 * e + i) * P:(2 * e + i + 1) * P],
                                                otr[:, g, e * N + i * P:e * N + (i + 1) * P], ident[:, :])
                    last.then_inc(S("att_o"), 1)

                if G > 1:
                    pe.wait_ge(S("att_k_parts"), 1)
                    for m in range(turns(L, 0)):
                        turn(m, kst, m)
                if G > 1:
                    keep_clock(3, 6)
                pe.wait_ge(S("att_parts"), before(L, "parts") + 1)
                if G == 1:
                    turn_group(0)
                else:
                    for m in range(2):
                        turn(q_at(0) + m, qst, m)
                for j in range(8):
                    keep_clock(3, 2)
                    by_query(0, j)
                keep_clock(3, 6)
                turn_maxima(0)
                pe.wait_ge(S("att_v"), before(L, "v") + ATT_COUNTS["v"][L])
                for g in range(GR):
                    turn_at, queries = ((2, ((), (), (), (0, 1), (2, 3), (4, 5), (6, 7), ())) if g == 0 else
                                        (0, ((), (0, 1), (2,), (3, 4), (5,), (6, 7), (), ())))
                    for k in range(8):
                        n = 8 * g + k
                        by_key(n)
                        if g + 1 < GR:
                            if k == turn_at:
                                pe.wait_ge(S("att_parts"), before(L, "parts") + 2)
                                turn_group(g + 1)
                            for j in queries[k]:
                                by_query(g + 1, j)
                        if n >= 2:
                            weighted(n - 2)
                        if k == 3 and g > 0:
                            rows_again(g - 1)
                    if g + 1 < GR:
                        keep_clock(5 + g, 4)
                        turn_maxima(g + 1)
                        keep_clock(5 + g, 4)
                weighted(H - 2)
                weighted(H - 1)
                rows_again(GR - 1)

            with pe.Fori(0, B) as b:
                keep_clock(3, 8)
                attention("l1x")

                keep_clock(3, 24)
                pe.wait_ge(S("l1f_in"), 1)
                four_transposes(pe, bank[0], tmp, ident[:, :]).then_inc(S("l1f_in_ps"), 1)
                pe.wait_ge(S("l1f_in"), 2)
                four_transposes(pe, bank[1], qr, ident[:, :]).then_inc(S("l1f_in_ps"), 1)
                pe.wait_ge(S("l1f_inT"), 1)
                for i in range(NT):
                    for cc in range(DC):
                        mm(bank[2 + i][:, :], xT[:, cc, i * P:(i + 1) * P], wqkvT[:, cc, 0:512], start=cc == 0, stop=cc == 1)
                    for cc in range(DC):
                        last = mm(bank[4][:, i * D:(i + 1) * D], xT[:, cc, i * P:(i + 1) * P], wqkvT[:, cc, 512:768],
                                  start=cc == 0, stop=cc == 1)
                    last.then_inc(S("qkv_ps"), 1)
                attention("l1f")
                pe.wait_ge(S("att_attn"), before("l1f", "attn") + NT)
                four_transposes(pe, bank[4], at, ident[:, :]).then_inc(S("l1f_atT_ps"), 1)
                pe.wait_ge(S("l1f_inT"), 2)
                for cc in range(DC):
                    mm(bank[5][0:R, N:2 * N], am[:, cc, :], hT[:, cc, :], start=cc == 0, stop=cc == 1)
                pe.wait_ge(S("l1f_atT"), 1)
                for cc in range(DC):
                    last = mm(bank[5][0:R, 0:N], wa[:, cc, :], atT[:, cc, :], start=cc == 0, stop=cc == 1)
                last.then_inc(S("mod_ps"), 1)
                pe.wait_ge(S("mh"), 1)
                for f in range(F1 // P):
                    if f >= 4:
                        pe.wait_ge(S("l1f_gu"), f - 3)
                    fs = slice(f * P, (f + 1) * P)
                    mm(bank[f % 4][:, 0:N], winT[:, 0, fs], hT[:, 0, :], start=True, stop=False)
                    mm(bank[f % 4][:, 0:N], winT[:, 1, fs], hT[:, 1, :], start=False, stop=False)
                    mm(bank[f % 4][:, 0:N], bm[:, fs], mh[:, :], start=False, stop=True)
                    mm(bank[f % 4][:, N:2 * N], wupT[:, 0, fs], hT[:, 0, :], start=True, stop=False)
                    mm(bank[f % 4][:, N:2 * N], wupT[:, 1, fs], hT[:, 1, :], start=False, stop=True)\
                        .then_inc(S("l1f_up"), 1)
                for i in range(NT):
                    for f in range(F1 // P):
                        pe.wait_ge(S("l1f_gu"), f + 1)
                        last = mm(bank[6 + i][:, 0:D], gu[:, f, i * P:(i + 1) * P], wdT[:, f, :],
                                  start=f == 0, stop=f == F1 // P - 1)
                    last.then_inc(S("l1f_down"), 1)

                end_of_batch(pe)
                pe.wait_ge(once("batch_cleared"), b + (B // 2 + 1))

            with pe.Fori(0, B // 2) as b:
                pe.wait_ge(S("c_ready"), 1)
                for i in range(T0):
                    last = pe.transpose(bank[7][0:CD, i * P:(i + 1) * P], c2[:, i, :], ident[:, :])
                last.then_inc(S("cT_ps"), 1)
                pe.wait_ge(S("cT"), 1)
                mm(bank[6][:, :], l2wj[:, :], cT2[:, :], start=True, stop=True).then_inc(S("sj_ps"), 1)

                pe.wait_ge(S("l2x_done"), 1)
                keep_clock(3, 50)
                pe.wait_ge(S("l2f_q1"), T0)
                for i in range(T0):
                    for cc in range(DC):
                        last = pe.transpose(bankb[0][:, cc * 512 + i * P:cc * 512 + i * P + P], q1[:, i, cc * P:(cc + 1) * P],
                                            identb[:, :])
                last.then_inc(S("q1T_ps"), 1)
                pe.wait_ge(S("q1T"), 1)
                for i in range(T0):
                    if i == 3:
                        pe.wait_ge(S("l2f_pre"), 1)
                    for hf in range(2):
                        for cc in range(DC):
                            last = mm(bank[1 + 2 * (i % 3) + hf][:, :], q1T[:, cc, i * P:(i + 1) * P],
                                      w1qT[:, cc, hf * 512:(hf + 1) * 512], start=cc == 0, stop=cc == 1)
                    last.then_inc(S("l2f_up"), 1)
                pe.wait_ge(S("l2f_ln"), T0)
                keep_clock(0, 40)
                for i in range(T0):
                    pe.wait_ge(S("l2f_q2"), i + 1)
                    for f in range(F1 // P):
                        last = pe.transpose(bankb[3 + i][:, f * P:(f + 1) * P], q2[:, i, f * P:(f + 1) * P], identb[:, :])
                    last.then_inc(S("q2T_ps"), 1)
                for i in range(T0):
                    pe.wait_ge(S("q2T"), i + 1)
                    for f in range(F1 // P):
                        last = mm(bank[(7 + i) % 8][:, 0:D], q2T[:, f, i * P:(i + 1) * P], w2qT[:, f, :],
                                  start=f == 0, stop=f == F1 // P - 1)
                    last.then_inc(S("l2f_down"), 1)
                end_of_batch(pe)
                pe.wait_ge(once("batch_cleared"), b + (B // 2 + B + 1))

            with pe.Fori(0, B) as b:
                keep_clock(3, 10)
                attention("l3x")
                pe.wait_ge(S("att_attn"), before("l3x", "attn") + NT)
                four_transposes(pe, bank[4], at, ident[:, :]).then_inc(S("l3x_atT_ps"), 1)
                pe.wait_ge(S("l3x_atT"), 1)
                for i in range(NT):
                    for cc in range(DC):
                        last = mm(bank[5][:, i * D:(i + 1) * D], atT[:, cc, i * P:(i + 1) * P], wcT[:, cc, :],
                                  start=cc == 0, stop=cc == 1)
                    last.then_inc(S("l3x_proj"), 1)

                keep_clock(3, 25)
                pe.wait_ge(S("l3f_xl"), NT)
                four_transposes(pe, bank[0], xl, ident[:, :]).then_inc(S("l3f_xT_ps"), 1)
                pe.wait_ge(S("l3f_xT"), 1)
                for ch in range(4):
                    for i in range(NT):
                        for cc in range(DC):
                            last = mm(bank[2 * ch + i][:, :], xT[:, cc, i * P:(i + 1) * P], mun[:, cc, ch * 512:(ch + 1) * 512],
                                      start=cc == 0, stop=cc == 1)
                        last.then_inc(S("logits_ps"), 1)

                def by_slot(g):
                    pe.wait_ge(S("logits_out"), 2 * (g // 2) + 2)
                    for j in range(2):
                        for i in range(NT):
                            last = pe.transpose(bank[g][:, j * N + i * P:j * N + (i + 1) * P],
                                                lg[:, i, (2 * g + j) * P:(2 * g + j + 1) * P], ident[:, :])
                    last.then_inc(S("logitsT_ps"), 1)

                def project(n):
                    i, hf = n // 2, n % 2
                    if n >= 2:
                        pe.wait_ge(S("proj_out"), n - 1)
                    for cc in range(DC):
                        last = mm(bank[hf][:, :], xT[:, cc, i * P:(i + 1) * P], w1s[:, cc, 8 * hf:8 * hf + 8, :],
                                  start=cc == 0, stop=cc == 1)
                    last.then_inc(S("proj_ps"), 1)

                for g in range(6):
                    by_slot(g)
                pe.wait_ge(S("row_parts"), 1)
                pe.wait_ge(S("logits_out"), 8)
                for i in range(NT):
                    last = pe.transpose(bankb[6][0:96, i * P:(i + 1) * P], mst[:, i, :, :], identb[:, :])
                last.then_inc(S("row_partsT_ps"), 1)
                pe.wait_ge(S("row_partsT"), 1)
                mm(bank[7][:, 0:N], sel[:, 0, :], mT3[:, :], start=True, stop=True).then_inc(S("row_max_all"), 1)
                by_slot(6)
                pe.wait_ge(S("row_max_read"), 1)
                by_slot(7)
                pe.wait_ge(S("lT_less_max"), 2)
                project(0)
                project(1)
                pe.wait_ge(S("slot_parts"), 1)
                pe.wait_ge(S("lT_less_max"), 3)
                pe.transpose(bankb[2][0:96, 0:P], mst[:, 0, :, :], identb[:, :]).then_inc(S("slot_partsT_ps"), 1)
                pe.wait_ge(S("slot_partsT"), 1)
                pe.wait_ge(S("lT_less_max"), 8)
                for e in range(SE):
                    last = mm(bank[4 + e // 4][:, e % 4 * SS:(e % 4 + 1) * SS], sel[:, e, :], cmT[:, :], start=True, stop=True)
                    if e % 4 == 3:
                        last.then_inc(S("slot_max_all"), 1)
                project(2)
                project(3)
                keep_clock(3, 12)
                pe.wait_ge(S("proj_out"), 4)
                pe.wait_ge(S("ones_columns"), 2)
                for ch in range(4):
                    pe.wait_ge(S("dispatch"), ch + 1)
                    for k in range(4):
                        for i in range(NT):
                            e = 4 * ch + k
                            last = mm(bank[ch][:, k * (SH + 1):(k + 1) * (SH + 1)], lg[:, i, e * SS:(e + 1) * SS],
                                      xw[:, i, e, :], start=i == 0, stop=i == 1)
                    last.then_inc(S("soft_up"), 1)

                def gather(g):
                    pe.wait_ge(S("soft_hidden"), g // 2 + 1)
                    pe.wait_ge(S("combine"), g + 1)
                    if g >= 4:
                        pe.wait_ge(S(f"gathered{g % 2}"), (g - 4) // 2 + 1)
                    for j in range(2):
                        last = mm(bank[4 + g % 4][0:SH + 1, j * N:(j + 1) * N], hs[:, 2 * g + j, :], lT[:, 2 * g + j, :],
                                  start=True, stop=True)
                    last.then_inc(S("gathered_ps"), 1)

                def back(g):
                    pe.wait_ge(S(f"gathered{g % 2}"), g // 2 + 1)
                    for e in (2 * g, 2 * g + 1):
                        for i in range(NT):
                            last = mm(bank[i][:, 0:D + 1], aT[:, e, i * P:(i + 1) * P], w2a[:, e, :],
                                      start=e == 0, stop=e == SE - 1)
                    return last

                pe.wait_ge(S("logits_less_max"), 4)
                for g in range(8):
                    gather(g)
                    if g >= 2:
                        back(g - 2)
                back(6)
                back(7).then_inc(S("soft_out"), 1)
                end_of_batch(pe)
                pe.wait_ge(once("batch_cleared"), b + (B + B + 1))

        @block.scalar
        def _(act):
            def copy(dst, src, scale=1.0):
                return act.activation(dst, src, ACT.Copy, scale=scale)

            act.wait_ge(once("first_loads"), 9 * 16)
            act.activation(gates[:, :], gates[:, :], ACT.Tanh).then_inc(once("gates_ready"), 1)
            act.wait_ge(once("wk_turned"), 1)
            copy(wkT[:, :], bank[0][0:CD, 0:CD]).then_inc(once("wkT_ready"), 1)
            act.wait_ge(once("x_loaded"), 32)
            with act.Fori(0, B // 2) as b:
                copy(c0[:, :, :], ctxs[:, bass.ts(b, T0), :]).then_inc(S("c_ready"), 1)
                act.wait_ge(S("p0"), 1)
                copy(cT0[:, :], bank[0][0:CD, :]).then_inc(S("cT"), 1)
                act.wait_ge(S("kvT_ps"), 1)
                act.activation(kvT[:, :], bank[1][0:CD, :], ACT.Identity, bias=bk_col[:, 0:1]).then_inc(S("kvT"), 1)
                for cc in range(DC):
                    act.wait_ge(S("xT_ps"), cc + 1)
                    copy(xT0[:, cc, :], bank[3 + cc][:, :]).then_inc(S("xT"), 1)
                act.wait_ge(S("oT_ps"), 1)
                copy(oT[:, :], bank[5][0:CD, :], scale=float(D) ** -0.5).then_inc(S("oT"), 1)
                act.wait_ge(S("l0_ln_done"), 1)
                for i in range(T0):
                    act.activation(tmp0[:, i, :], tmp0[:, i, :], ACT.Exp, bias=nw[:, i:i + 1],
                                   accum_out=st[:, i:i + 1]).then_inc(S("l0_exp"), 1)
                for cc in range(DC):
                    act.wait_ge(S("xT_ps"), DC + cc + 1)
                    copy(xT0[:, cc, :], bank[cc][:, :]).then_inc(S("xT"), 1)
                act.wait_ge(S("router_max"), 1)
                for i in range(T0):
                    act.activation(cb0[:, i, :], lg0[:, i, :], ACT.Exp, bias=st[:, 12 + i:13 + i]).then_inc(S("router_exp"), 1)
                act.wait_ge(S("comb_ps"), 1)
                copy(comb[:, bass.ts(b, T0 * P)], bank[3][:, :]).then_inc(S("comb_high"), 1)
                act.wait_ge(S("comb_high"), 1)
                end_of_batch(act)
                act.wait_ge(once("batch_cleared"), b + 1)

            def gate(k, u):
                n = 3 * k
                act.wait_ge(once("gate_made"), u + 1)
                act.wait_ge(once("up_used"), u + 1)
                act.activation(sg[k % 2][:, :], bank[4 + n % 4][:, :], ACT.Silu).then_inc(once("gate_used"), 1)
                act.wait_ge(once("hidden_full"), u + 1)
                copy(hhi[k % 2][:, :], hh[k % 2][:, :]).then_inc(once("hidden_high"), 1)

            act.wait_ge(once("picks"), 2)
            with act.Fori(0, PAIRS // SLOTN) as t:
                for k in range(2 * SLOTN):
                    gate(k, t * 8 + k)
            act.wait_ge(once("hidden_used"), 2 * PAIRS + 4)
            for h in range(HALVES):
                for m in range(DC):
                    copy(yT[:, m, h * 512:(h + 1) * 512], bank[2 * m + h][:, :]).then_inc(once("experts_out"), 1)
            act.wait_ge(once("l2_loaded"), 2 * 16)
            for k, scratch in enumerate((w1qT, w2qT)):
                act.activation(scratch[:, :, :].rearrange("p c f -> p (c f)"), l2_raw[k][:, :], ACT.Abs, accum_out=st[:, k:k + 1]).then_inc(once("abs_sums"), 1)
            act.wait_ge(once("mu_products"), 2)
            copy(cmT[:, :], bankb[6][0:96, 0:P]).then_inc(once("mu_partsT"), 1)
            for g, (srcs, dst) in enumerate(PREP + PREPB):
                if g == 0:
                    act.wait_ge(once("ternary"), 2)
                act.wait_ge(once("prep_made"), g + 1)
                src = (bank if g < len(PREP) else bankb)[g % 4]
                copy(dst, src[:, 0:len(srcs) * P]).then_inc(once("prep_done"), 1)

            def attention(L):
                H, G, HD, causal = ATTENTIONS[L]
                K6, GR = 6 * HD, H // 8

                def turned(r, dst, t):
                    if r % 2 == 0:
                        act.wait_ge(S("att_partsT"), before(L, "partsT") + t + 1)
                        copy(dst, bankb[0][0:K6, :]).then_inc(S("att_left0"), 1)

                def operands(g):
                    t, n = turned_before(L, g), turns(L, g)
                    for m in range(n):
                        turned(first(L, g) + m, kT[0:K6, 8 * g + 4 * m:8 * g + 4 * m + 4, :], t + m)
                    for m in range(2):
                        h = 8 * g + 4 * m
                        turned(queries_at(L, g) + m, qT[0:K6, h:h + 4, :], t + n + m)

                def maxima(g):
                    r = queries_at(L, g) + 10
                    act.wait_ge(S("att_mT_ps"), before(L, "mT_ps") + g + 1)
                    copy(mT[:, 0, :], bankb[r % 2][0:96, 0:N], scale=parity[0:96, 0:1])
                    copy(mT[:, 1, :], bankb[r % 2][0:96, 0:N], scale=parity[0:96, 1:2]).then_inc(S(f"att_left{r % 2}"), 1)

                def results(g):
                    act.wait_ge(S("att_pv"), before(L, "pv") + 8 * g + 8)
                    copy(otr[:, g, :], bank[4 + g][:, :]).then_inc(S("att_oT"), 1)

                operands(0)
                maxima(0)
                for g in range(GR):
                    for k in range(8):
                        n = 8 * g + k
                        act.wait_ge(S("att_scores"), before(L, "scores") + n + 1)
                        if n >= 4:
                            act.wait_ge(S("att_pv"), before(L, "pv") + n - 3)
                        act.activation(prob[n % 4][:, :], bank[2 + n % 2][:, :], ACT.Exp).then_inc(S("att_probs"), 1)
                        if k == (2 if g == 0 else 0) and g + 1 < GR:
                            operands(g + 1)
                        if k == 2 and g > 0:
                            results(g - 1)
                    if g + 1 < GR:
                        maxima(g + 1)
                results(GR - 1)

            act.wait_ge(once("prepared"), 1)
            with act.Fori(0, B) as b:
                attention("l1x")
                act.wait_ge(S("l1f_in_ps"), 1)
                copy(xT[:, :, :], bank[0][:, :]).then_inc(S("l1f_inT"), 1)
                act.wait_ge(S("l1f_in_ps"), 2)
                copy(hT[:, :, :], bank[1][:, :]).then_inc(S("l1f_inT"), 1)
                for i in range(NT):
                    act.wait_ge(S("qkv_ps"), i + 1)
                    copy(qf[:, i, :], bank[2 + i][:, 0:D], scale=0.25).then_inc(S("qk"), 1)
                    copy(kf[:, i, :], bank[2 + i][:, D:2 * D]).then_inc(S("qk"), 1)
                attention("l1f")
                act.wait_ge(S("l1f_atT_ps"), 1)
                copy(atT[:, :, :], bank[4][:, :]).then_inc(S("l1f_atT"), 1)
                act.wait_ge(S("mod_ps"), 1)
                act.activation(modT[:, :], bank[5][0:R, 0:N], ACT.Tanh).then_inc(S("modT"), 1)
                for f in range(F1 // P):
                    act.wait_ge(S("l1f_up"), f + 1)
                    if f >= 2:
                        act.wait_ge(S("l1f_gu"), f - 1)
                    act.activation(sgf[f % 2][:, :], bank[f % 4][:, 0:N], ACT.Silu).then_inc(S("l1f_silu"), 1)
                end_of_batch(act)
                act.wait_ge(once("batch_cleared"), b + (B // 2 + 1))

            with act.Fori(0, B // 2) as b:
                copy(c2[:, :, :], ctxs[:, bass.ts(b, T0), :]).then_inc(S("c_ready"), 1)
                act.wait_ge(S("cT_ps"), 1)
                copy(cT2[:, :], bank[7][0:CD, :]).then_inc(S("cT"), 1)
                act.wait_ge(S("sj_ps"), 1)
                act.wait_ge(S("si"), 1)
                for i in range(T0):
                    act.activation(tmp2[:, i, :], bank[6][:, i // NT * N:(i // NT + 1) * N], ACT.Sigmoid, bias=st[:, 8 + i:9 + i])\
                        .then_inc(S("l2x_sig"), 1)
                act.wait_ge(S("q1T_ps"), 1)
                copy(q1T[:, :, :], bankb[0][:, :].rearrange("p (c t) -> p c t", c=DC)).then_inc(S("q1T"), 1)
                for i in range(T0):
                    act.wait_ge(S("l2f_pre"), i + 1)
                    act.activation(h2[:, i, :], h2[:, i, :], ACT.Silu).then_inc(S("l2f_silu"), 1)
                for i in range(T0):
                    act.wait_ge(S("l2f_silu"), i + 1)
                    act.activation(h2[:, i, :], h2[:, i, :], ACT.Gelu).then_inc(S("l2f_gelu"), 1)
                for i in range(T0):
                    act.wait_ge(S("l2f_ln"), i + 1)
                    act.activation(q2[:, i, :], h2[:, i, :], ACT.Square, accum_out=st[:, i:i + 1]).then_inc(S("l2f_sq"), 1)
                for i in range(T0):
                    act.wait_ge(S("q2T_ps"), i + 1)
                    copy(q2T[:, :, i * P:(i + 1) * P], bankb[3 + i][:, :].rearrange("p (f t) -> p f t", t=P)).then_inc(S("q2T"), 1)
                end_of_batch(act)
                act.wait_ge(once("batch_cleared"), b + (B // 2 + B + 1))

            with act.Fori(0, B) as b:
                attention("l3x")
                act.wait_ge(S("l3x_atT_ps"), 1)
                copy(atT[:, :, :], bank[4][:, :]).then_inc(S("l3x_atT"), 1)
                act.wait_ge(S("l3f_xT_ps"), 1)
                copy(xT[:, :, :], bank[0][:, :]).then_inc(S("l3f_xT"), 1)
                act.wait_ge(S("l3f_rs"), 1)
                for n in range(8):
                    ch, i = n // 2, n % 2
                    act.wait_ge(S("logits_ps"), n + 1)
                    copy(lg[:, i, ch * 512:(ch + 1) * 512], bank[n][:, :], scale=rs[:, i:i + 1]).then_inc(S("logits_out"), 1)
                act.wait_ge(S("row_partsT_ps"), 1)
                copy(mT3[:, :], bankb[6][0:96, 0:N]).then_inc(S("row_partsT"), 1)
                for g in range(8):
                    act.wait_ge(S("lT_less_max"), g + 1)
                    act.activation(lT[:, 2 * g:2 * g + 2, :], lT[:, 2 * g:2 * g + 2, :], ACT.Exp).then_inc(S("combine"), 1)

                def projected(n):
                    i, hf = n // 2, n % 2
                    act.wait_ge(S("proj_ps"), n + 1)
                    copy(xw[:, i, 8 * hf:8 * hf + 8, 0:SH], bank[hf][:, :].rearrange("p (e h) -> p e h", h=SH))\
                        .then_inc(S("proj_out"), 1)

                projected(0)
                projected(1)
                act.wait_ge(S("slot_partsT_ps"), 1)
                copy(cmT[:, :], bankb[2][0:96, 0:P]).then_inc(S("slot_partsT"), 1)
                projected(2)
                projected(3)
                for ch in range(4):
                    lc = lg[:, :, ch * 512:(ch + 1) * 512]
                    act.wait_ge(S("logits_less_max"), ch + 1)
                    act.activation(lc, lc, ACT.Exp).then_inc(S("dispatch"), 1)
                for ch in range(4):
                    h = hs[:, 4 * ch:4 * ch + 4, 0:SH]
                    act.wait_ge(S("soft_pre"), ch + 1)
                    act.activation(h, h, ACT.Gelu).then_inc(S("soft_hidden"), 1)
                for g in range(0, 8, 2):
                    act.wait_ge(S("gathered_ps"), g + 1)
                    copy(aT[:, 2 * g:2 * g + 2, :], bank[4 + g % 4][0:SH + 1, :].rearrange("p (e t) -> p e t", e=2))\
                        .then_inc(S("gathered0"), 1)
                act.wait_ge(S("gathered0"), 4)
                end_of_batch(act)
                act.wait_ge(once("batch_cleared"), b + (B + B + 1))

        @block.vector
        def _(dve):
            V = nc.vector
            ts, tt, stt = V.tensor_scalar, V.tensor_tensor, V.scalar_tensor_tensor

            def rsqrt(step, out_, v):
                k = v.shape[1]
                w = nw[:, 0:k] if k <= 4 else cmr[:, 0:k]
                step(ts(w.bitcast(I32), v.bitcast(I32), 1, None, ALU.arith_shift_right))
                step(ts(out_.bitcast(I32), w.bitcast(I32), -1, 0x5F3759DF, ALU.mult, ALU.add))
                for _ in range(3):
                    step(tt(w, out_, v, ALU.mult))
                    step(stt(out=w, in0=w, scalar=-0.5, in1=out_, op0=ALU.mult, op1=ALU.mult))
                    step(stt(out=out_, in0=w, scalar=1.5, in1=out_, op0=ALU.add, op1=ALU.mult))

            def stats(step, src, *scales, between=None, tiles=NT):
                step(*[V.bn_stats(bn[:, i, :], src(i)) for i in range(tiles)])
                step(*[V.bn_aggr(mv[:, i, :], bn[:, i, :]) for i in range(tiles)])
                step(*[ts(ve[:, tiles * k:tiles * k + tiles], mv[:, 0:tiles, 1], m, a, ALU.mult, ALU.add)
                       for k, (m, a) in enumerate(scales)], *(between() if between else []))
                rsqrt(step, rs[:, 0:tiles * len(scales)], ve[:, 0:tiles * len(scales)])

            def x_rows(i):
                return x[:, i, :]

            def normed(step, out_, k=0):
                step(*[ts(out_[:, i, :], x[:, i, :], mv[:, i, 0:1], rs[:, NT * k + i:NT * k + i + 1], ALU.subtract, ALU.mult)
                       for i in range(NT)])

            def less_mean_times(out_, src, w, tiles=NT):
                return [stt(out=out_(i), in0=src(i), scalar=mv[:, i, 0:1], in1=w, op0=ALU.subtract, op1=ALU.mult)
                        for i in range(tiles)]

            def layernorm(step, out_, scale=1.0):
                stats(step, x_rows, (scale ** -2, 1e-5 * scale ** -2))
                normed(step, out_)

            def three_parts(step, parts, v, left):
                step(V.tensor_copy(parts[0], v))
                step(tt(left, v, parts[0], ALU.subtract))
                step(V.tensor_copy(parts[1], left))
                step(tt(parts[2], left, parts[1], ALU.subtract))

            step = step_once = Steps(dve, once("dve_step_prep"))
            dve.wait_ge(once("consts"), 1)
            heads = st[0:96, 0:16]
            step(V.reduce_sum(heads, ident[0:96, 0:96].rearrange("p (s h) -> p h s", h=32)[:, 0:16, :], AX))
            step(V.tensor_copy(sel[:, :, :], heads.unsqueeze(2).broadcast_to([96, 16, P])))
            step(V.reduce_sum(heads, ident[0:96, 0:96].rearrange("p (s u e) -> p u s e", u=16, e=2), mybir.AxisListType.XY))
            step(V.tensor_copy(sel2[:, :, :], heads.unsqueeze(2).broadcast_to([96, 16, P])))
            step(*[V.reduce_sum(parity[:, e:e + 1], ident[:, e:P:2], AX) for e in range(2)])
            dve.sem_inc(once("sel_ready"), 1)
            dve.wait_ge(once("x_loaded"), 32)
            dve.wait_ge(once("first_loads"), 9 * 16)
            dve.wait_ge(once("gates_ready"), 1)
            with dve.Fori(0, B // 2) as b:
                step = Steps(dve, S("dve_step"))
                rows = xs[:, bass.ts(b, T0), :]

                def norm0():
                    stats(step, lambda i: rows[:, i, :], (1.0, 1e-5), tiles=T0)
                    step(*[ts(xn0[:, i, :], rows[:, i, :], mv[:, i, 0:1], rs[:, i:i + 1], ALU.subtract, ALU.mult)
                           for i in range(T0)])
                    dve.sem_inc(S("xn"), 1)

                norm0()
                dve.wait_ge(S("kv_ps"), 1)
                tt(kv[:, :, :], bank[2][:, 0:T0 * CD].rearrange("p (i d) -> p i d", i=T0),
                   bk_row[:, :].unsqueeze(1).broadcast_to([P, T0, CD]), ALU.add).then_inc(S("kv"), 1)
                dve.wait_ge(S("sim_ps"), T0)
                sims = lambda i: bank[6 + i // 2][:, i % 2 * N:(i % 2 + 1) * N]
                stats(step, sims, (1.0, 1e-6), tiles=T0,
                      between=lambda: less_mean_times(lambda i: tmp0[:, i, :], sims, rowsD["L0_xattn_ln_gamma"][:, :], T0))
                step(*[stt(out=tmp0[:, i, :], in0=tmp0[:, i, :], scalar=rs[:, i:i + 1], in1=rowsD["L0_xattn_ln_beta"][:, :],
                           op0=ALU.mult, op1=ALU.add) for i in range(T0)])
                step(V.tensor_reduce(nw[:, 0:T0], tmp0[:, :, :], AX, ALU.max, negate=True))
                dve.sem_inc(S("l0_ln_done"), 1)
                dve.wait_ge(S("l0_exp"), T0)
                step(V.reciprocal(st[:, 4:8], st[:, 0:4]))
                step(ts(st[:, 4:8], st[:, 4:8], gates[:, 0:1], None, ALU.mult))
                step(*[stt(out=rows[:, i, :], in0=tmp0[:, i, :], scalar=st[:, 4 + i:5 + i], in1=rows[:, i, :],
                           op0=ALU.mult, op1=ALU.add) for i in range(T0)])
                norm0()
                dve.wait_ge(S("router_ps"), 1)
                step(V.tensor_copy(lg0[:, :, :], bank[2][:, 0:T0 * E].rearrange("p (i e) -> p i e", i=T0)),
                     V.memset(lb0[:, :, E:E + TOPK], -BIG))
                step(tt(lb0[:, :, 0:E], lg0[:, :, :], rb[:, :].unsqueeze(1).broadcast_to([P, T0, E]), ALU.add),
                     V.tensor_reduce(st[:, 12:16], lg0[:, :, :], AX, ALU.max, negate=True))
                dve.sem_inc(S("router_max"), 1)
                step(*[V.max(m8[:, i, :], lb0[:, i, 0:E]) for i in range(T0)])
                step(V.memset(m8[:, :, TOPK:8], -BIG))
                step(*[V.match_replace(lr0[:, i, :], m8[:, i, :], lb0[:, i, :], BIG) for i in range(T0)])
                step(tt(ct0[:, :, :], lr0[:, :, 0:E], lb0[:, :, 0:E], ALU.not_equal))
                dve.wait_ge(S("router_exp"), T0)
                step(tt(ct0[:, :, :], ct0[:, :, :], cb0[:, :, :], ALU.mult))
                step(V.reduce_sum(st[:, 0:4], ct0[:, :, :], AX))
                step(V.reciprocal(st[:, 4:8], st[:, 0:4]))
                step(*[tt(ct2[:, :, k, :], ct0[:, :, :], st[:, 4:8].unsqueeze(2).broadcast_to([P, T0, E]), ALU.mult)
                       for k in range(2)])
                dve.sem_inc(S("comb"), 1)
                dve.wait_ge(S("comb_high"), 1)
                low = comb[E:2 * E, bass.ts(b, T0 * P)]
                step(tt(low, bank[3][E:2 * E, :], low.bitcast(F32), ALU.subtract))
                end_of_batch(dve)
                dve.wait_ge(once("batch_cleared"), b + 1)

            step = step_once
            dve.wait_ge(once("picks"), 2)
            dve.sem_inc(once("hidden_made"), 1)
            dve.sem_inc(once("up_used"), 2)
            dve.wait_ge(once("rest_loads"), REST * 16)
            step(tt(mu2[:, :, :], mun[:, :, :], mun[:, :, :], ALU.mult))
            dve.sem_inc(once("mu_steps"), 1)

            def rest_of_hidden(k, u):
                dve.wait_ge(once("hidden_high"), u + 1)
                tt(hlo[k % 2][:, :], hh[k % 2][:, :], hhi[k % 2][:, :].bitcast(F32), ALU.subtract)\
                    .then_inc(once("hidden_made"), 1)

            with dve.Fori(0, E // 2 // SLOTN) as t:
                for k in range(2 * SLOTN):
                    n, u = 3 * k, t * 8 + k
                    dve.wait_ge(once("gate_used"), u + 1)
                    dve.wait_ge(once("up_made"), u + 5)
                    tt(hu[k % 2][:, :], bank[4 + (n + 1) % 4][:, :], sg[k % 2][:, :], ALU.mult).then_inc(once("up_used"), 1)
                    dve.wait_ge(once("up_used"), u + 3)
                    dve.wait_ge(once("weight_made"), u + 1)
                    dve.wait_ge(once("hidden_used"), u + 3)
                    tt(hh[k % 2][:, :], bank[4 + (n + 2) % 4][:, :], hu[k % 2][:, :], ALU.mult).then_inc(once("hidden_full"), 1)
                    rest_of_hidden(k, u)
            for k in range(2 * SLOTN):
                n, u = 3 * k, E + k
                dve.wait_ge(once("gate_used"), u + 1)
                dve.wait_ge(once("up_made"), u + 5)
                dve.wait_ge(once("hidden_used"), u + 3)
                tt(hh[k % 2][:, :], bank[4 + (n + 1) % 4][:, :], sg[k % 2][:, :], ALU.mult).then_inc(once("up_used"), 1)
                dve.wait_ge(once("up_used"), u + 3)
                dve.sem_inc(once("hidden_full"), 1)
                rest_of_hidden(k, u)
            for k in range(4):
                dve.wait_ge(once("y_rows"), k + 1)
                rows = xs[:, 2 * k:2 * k + 2, :]
                stt(out=rows, in0=bank[4 + k][:, :].rearrange("p (i d) -> p i d", i=2), scalar=gates[:, 4:5], in1=rows,
                    op0=ALU.mult, op1=ALU.add).then_inc(once("xs_updated"), 1)
            dve.wait_ge(once("abs_total"), 1)
            step(ts(wdq[:, :], bank[4][:, 0:2], 1.0 / (F1 * D), 1e-5, ALU.mult, ALU.max))
            dve.sem_inc(once("mu_steps"), 1)
            step(V.reciprocal(st[:, 2:4], wdq[:, :]))
            for k in range(2):
                w = l2_raw[k][:, :]
                step(ts(w, w, st[:, 2 + k:3 + k], -1.0, ALU.mult, ALU.max))
                step(ts(w, w, 1.0, ROUND, ALU.min, ALU.add))
                ts(tern[k][:, :], w, ROUND, None, ALU.subtract).then_inc(once("ternary"), 1)
            dve.wait_ge(once("mu_products"), 1)
            step(V.tensor_copy(cmx[:, :], bank[5][:, 0:SE]))
            rsqrt(step, rbc[:, 0:SE], cmx[:, :])
            step(tt(cmx[:, :], cmx[:, :], rbc[:, 0:SE], ALU.mult))
            step(ts(cmx[:, :], cmx[:, :], 1e-12, None, ALU.max))
            step(V.reciprocal(rbc[:, 0:SE], cmx[:, :]))
            three_parts(step, [mst[:, 0, k, 0:SE] for k in range(3)], rbc[:, 0:SE], cmr[:, 0:SE])
            dve.sem_inc(once("mu_steps"), 1)
            dve.wait_ge(once("mu_products"), 3)
            for ch in range(4):
                m = mun[:, :, ch * 512:(ch + 1) * 512]
                step(tt(m, m, bank[4 + ch][:, :].unsqueeze(1).broadcast_to([P, DC, 512]), ALU.mult))
            step(V.tensor_copy(l2wj[:, 1:P], l2wj[:, 0:1].broadcast_to([CD, P - 1])))
            dve.wait_ge(once("wa_made"), 1)
            step(V.tensor_copy(wa[:, :, :], bank[len(PREP + PREPB) % 4][:, 0:DC * R].rearrange("p (m r) -> p m r", m=DC)))
            dve.sem_inc(once("prepared"), 1)
            dve.wait_ge(once("xs_updated"), 4)

            def attention(step, L, q, k):
                H, G, HD, causal = ATTENTIONS[L]
                K6, GR = 6 * HD, H // 8

                def parts(t, src, slots, copies, g0, g1):
                    heads = slice(8 * g0, 8 * g1)

                    def slot(k_):
                        return t[:, :, 0:H * K6].rearrange("p i (h s d) -> p s i h d", h=H, s=6)[:, k_, :, heads]
                    v = src.rearrange("p i (h d) -> p i h d", h=H)[:, :, heads]
                    left = qr.rearrange("p i (h d) -> p i h d", h=H)[:, :, heads]
                    h, m, l = slots
                    step(V.tensor_copy(slot(h), v))
                    step(tt(left, v, slot(h), ALU.subtract))
                    step(V.tensor_copy(slot(m), left))
                    step(tt(slot(l), left, slot(m), ALU.subtract), *[V.tensor_copy(slot(to), slot(fro)) for to, fro in copies])

                def operands(g0, g1):
                    if G == 1:
                        parts(kst, k, *K_SLOTS, g0, g1)
                    parts(qst, q, *Q_SLOTS, g0, g1)
                    dve.sem_inc(S("att_parts"), 1)

                def turned(r, dst, t_):
                    if r % 2 == 1:
                        dve.wait_ge(S("att_partsT"), before(L, "partsT") + t_ + 1)
                        V.tensor_copy(dst, bankb[1][0:K6, :].rearrange("p (h n) -> p h n", h=4)).then_inc(S("att_left1"), 1)

                def maxima(g):
                    t, n = turned_before(L, g), turns(L, g)
                    for m in range(n):
                        turned(first(L, g) + m, kT[0:K6, 8 * g + 4 * m:8 * g + 4 * m + 4, :], t + m)
                    for m in range(2):
                        h = 8 * g + 4 * m
                        turned(queries_at(L, g) + m, qT[0:K6, h:h + 4, :], t + n + m)
                    for j in range(8):
                        r, i, u = queries_at(L, g) + 2 + j, j // 4, 4 * g + j % 4
                        dve.wait_ge(S("att_q_scores"), before(L, "q_scores") + 8 * g + j + 1)
                        V.reduce_max(mx[:, i, 2 * u:2 * u + 2], bank[r % 2][:, :].rearrange("p (e t) -> p e t", e=2), AX,
                                     negate=True).then_inc(S(f"att_left{r % 2}"), 1)
                    for r in (queries_at(L, g) + 8, queries_at(L, g) + 9):
                        dve.wait_ge(S(f"att_left{r % 2}"), before(L, f"left{r % 2}") + r // 2 + 1)
                    hs = slice(8 * g, 8 * g + 8)
                    three_parts(step, [mst[:, :, s, hs] for s in range(3)], mx[:, :, hs], mr[:, :, hs])
                    dve.sem_inc(S("att_max_parts"), 1)

                def results(g):
                    dve.wait_ge(S("att_o"), before(L, "o") + g + 1)
                    o = bank[4 + g][:, :].rearrange("p (e i j d) -> p e i j d", e=2, i=NT, j=4)
                    step(V.reciprocal(rc[:, g, :], bank[4 + g][:, :].rearrange("p (k d) -> p k d", d=32)[:, :, HD]))
                    r = rc[:, g, :].rearrange("p (e i j) -> p e i j", e=2, i=NT)
                    step(*[tt(at[:, i, g * 8 * HD:(g + 1) * 8 * HD].rearrange("p (j e d) -> p e j d", e=2, d=HD)[:, e],
                              o[:, e, i, :, 0:HD], r[:, e, i, :].unsqueeze(2).broadcast_to([P, 4, HD]), ALU.mult)
                           for i in range(NT) for e in range(2)])

                operands(0, 1)
                maxima(0)
                operands(1, GR)
                for g in range(GR):
                    if g + 1 < GR:
                        maxima(g + 1)
                    if g > 0:
                        results(g - 1)
                results(GR - 1)
                dve.sem_inc(S("att_attn"), NT)

            def residual(step, y, g, done=None):
                step(*[stt(out=x[:, i, :], in0=y(i), scalar=gates[:, g:g + 1], in1=x[:, i, :], op0=ALU.mult, op1=ALU.add)
                       for i in range(NT)])

            with dve.Fori(0, B) as b:
                step = Steps(dve, S("dve_step"))
                step(V.tensor_copy(x[:, :, :], xs[:, bass.ts(b, NT), :]))
                layernorm(step, xn, 8 ** -0.5)
                attention(step, "l1x", xn, None)
                residual(step, lambda i: at[:, i, :], 1)

                stats(step, x_rows, (1.0, 1e-5), (1.0 + 1e-6, 1e-6 * 1e-5))
                normed(step, xn, 1)
                for w, dst in (("L1_ffn_ln1_w", tmp), ("L1_ffn_ln2_w", qr)):
                    step(*[tt(dst[:, i, :], xn[:, i, :], rowsD[w][:, :], ALU.mult) for i in range(NT)])
                    dve.sem_inc(S("l1f_in"), 1)
                normed(step, xn)
                residual(step, lambda i: xn[:, i, :], 5)
                dve.wait_ge(S("l1f_in_ps"), 2)
                dve.wait_ge(S("qkv_ps"), 2)
                V.tensor_copy(vst[:, :, :, 0:16], bank[4][:, :].rearrange("p (i h d) -> p i h d", i=NT, d=16)).then_inc(S("att_v"), 1)
                dve.wait_ge(S("qk"), 4)
                attention(step, "l1f", qf, kf)
                dve.wait_ge(S("modT"), 1)
                stt(out=mh[:, :], in0=modT[:, :], scalar=0.1, in1=bank[5][0:R, N:2 * N], op0=ALU.mult, op1=ALU.mult)\
                    .then_inc(S("mh"), 1)
                for f in range(F1 // P):
                    dve.wait_ge(S("l1f_silu"), f + 1)
                    tt(gu[:, f, :], bank[f % 4][:, N:2 * N], sgf[f % 2][:, :], ALU.mult).then_inc(S("l1f_gu"), 1)
                dve.wait_ge(S("l1f_down"), 2)
                step(*[stt(out=xs[:, bass.ts(b, NT), :][:, i, :], in0=bank[6 + i][:, 0:D], scalar=gates[:, 5:6], in1=x[:, i, :],
                           op0=ALU.mult, op1=ALU.add) for i in range(NT)])
                end_of_batch(dve)
                dve.wait_ge(once("batch_cleared"), b + (B // 2 + 1))

            with dve.Fori(0, B // 2) as b:
                step = Steps(dve, S("dve_step"))
                rows = xs[:, bass.ts(b, T0), :]
                tiles = range(T0)

                dve.wait_ge(S("c_ready"), 1)
                step(*[V.tensor_tensor_reduce(out=xn2[:, i, 0:CD], in0=c2[:, i, :], in1=l2wi[:, :], scale=1.0, scalar=0.0,
                                              op0=ALU.mult, op1=ALU.add, accum_out=st[:, 8 + i:9 + i]) for i in tiles])
                step(ts(st[:, 8:12], st[:, 8:12], l2b[:, 0:1], None, ALU.add))
                dve.sem_inc(S("si"), 1)
                stats(step, lambda i: rows[:, i, :], (1.0, 1e-5), tiles=T0)
                dve.wait_ge(S("l2x_sig"), T0)
                step(ts(tmp2[:, :, :], tmp2[:, :, :], 0.6, gates[:, 2:3], ALU.mult, ALU.mult),
                     ts(rs[:, :], rs[:, :], 1.0 - 0.6, gates[:, 2:3], ALU.mult, ALU.mult))
                step(tt(tmp2[:, :, :], tmp2[:, :, :], rows, ALU.add),
                     *[ts(xn2[:, i, :], rows[:, i, :], mv[:, i, 0:1], rs[:, i:i + 1], ALU.subtract, ALU.mult) for i in tiles])
                step(tt(rows, xn2[:, :, :], tmp2[:, :, :], ALU.add))

                dve.sem_inc(S("l2x_done"), 1)
                stats(step, lambda i: rows[:, i, :], (1.0 + 1e-5, 1e-5 * 1e-5), tiles=T0)
                step(*[ts(xn2[:, i, :], rows[:, i, :], mv[:, i, 0:1], rs[:, i:i + 1], ALU.subtract, ALU.mult) for i in tiles])

                def quantise(v, k, q, name, root=None):
                    step(V.tensor_reduce(st[:, 4:8], v[:, :, :], AX, ALU.max, apply_absolute_value=True))
                    if root is not None:
                        root(step)
                        step(tt(st[:, 4:8], st[:, 4:8], rs[:, :], ALU.mult))
                    step(ts(st[:, 4:8], st[:, 4:8], 1e-5, None, ALU.max))
                    step(ts(st[:, 8:12], st[:, 4:8], 1.0 / 127.0, wdq[:, k:k + 1], ALU.mult, ALU.mult),
                         V.reciprocal(st[:, 12:16], st[:, 4:8]))
                    if root is not None:
                        step(stt(out=st[:, 12:16], in0=st[:, 12:16], scalar=127.0, in1=rs[:, :], op0=ALU.mult, op1=ALU.mult))
                    else:
                        step(ts(st[:, 12:16], st[:, 12:16], 127.0, None, ALU.mult))
                    step(*[ts(v[:, i, :], v[:, i, :], st[:, 12 + i:13 + i], -128.0, ALU.mult, ALU.max) for i in tiles])
                    for i in tiles:
                        step(ts(v[:, i, :], v[:, i, :], 127.0, ROUND, ALU.min, ALU.add))
                        ts(q[:, i, :], v[:, i, :], ROUND, None, ALU.subtract).then_inc(S(name), 1)

                quantise(xn2, 0, q1, "l2f_q1")
                for i in tiles:
                    dve.wait_ge(S("l2f_up"), i + 1)
                    step(*[stt(out=h2[:, i, hf * 512:(hf + 1) * 512], in0=bank[1 + 2 * (i % 3) + hf][:, :],
                               scalar=st[:, 8 + i:9 + i], in1=rowsF["L2_ffn_b1"][:, hf * 512:(hf + 1) * 512],
                               op0=ALU.mult, op1=ALU.add) for hf in range(2)])
                    dve.sem_inc(S("l2f_pre"), 1)
                step(*[stt(out=rows[:, i, :], in0=rowsD["L2_ffn_b2"][:, :], scalar=gates[:, 6:7], in1=rows[:, i, :],
                           op0=ALU.mult, op1=ALU.add) for i in tiles])
                for i in tiles:
                    dve.wait_ge(S("l2f_gelu"), i + 1)
                    for hf in range(2):
                        V.bn_stats(bn2[:, i, hf, :], h2[:, i, hf * 512:(hf + 1) * 512]).then_inc(S("l2f_stats"), 1)
                dve.wait_ge(S("l2f_stats"), 2 * T0)
                step(*[V.bn_aggr(mv[:, i, :], bn2[:, i, :, :].rearrange("p a s -> p (a s)")) for i in tiles])
                step(ts(ve[:, :], mv[:, :, 1], 1e-5, None, ALU.add),
                     *less_mean_times(lambda i: h2[:, i, :], lambda i: h2[:, i, :], rowsF["L2_ffn_ln_g"][:, :], T0))
                rsqrt(step, rs[:, :], ve[:, :])
                for i in tiles:
                    stt(out=h2[:, i, :], in0=h2[:, i, :], scalar=rs[:, i:i + 1], in1=rowsF["L2_ffn_ln_b"][:, :],
                        op0=ALU.mult, op1=ALU.add).then_inc(S("l2f_ln"), 1)
                dve.wait_ge(S("l2f_ln"), T0)

                def root_mean_square(step):
                    dve.wait_ge(S("l2f_sq"), T0)
                    step(ts(ve[:, :], st[:, 0:4], 1.0 / F1, 1e-5, ALU.mult, ALU.add))
                    rsqrt(step, rs[:, :], ve[:, :])

                quantise(h2, 1, q2, "l2f_q2", root_mean_square)
                step(ts(st[:, 8:12], st[:, 8:12], gates[:, 6:7], None, ALU.mult))
                for i in tiles:
                    dve.wait_ge(S("l2f_down"), i + 1)
                    step(stt(out=rows[:, i, :], in0=bank[(7 + i) % 8][:, 0:D], scalar=st[:, 8 + i:9 + i], in1=rows[:, i, :],
                             op0=ALU.mult, op1=ALU.add))
                end_of_batch(dve)
                dve.wait_ge(once("batch_cleared"), b + (B // 2 + B + 1))

            with dve.Fori(0, B) as b:
                step = Steps(dve, S("dve_step"))
                step(V.tensor_copy(x[:, :, :], xs[:, bass.ts(b, NT), :]))
                layernorm(step, xn, 0.25)
                attention(step, "l3x", xn, None)
                residual(step, lambda i: rowsD["L3_xattn_bc"][:, :], 3)
                dve.wait_ge(S("l3x_proj"), 2)
                residual(step, lambda i: bank[5][:, i * D:(i + 1) * D], 3)

                dve.sem_inc(S("l3f_begun"), 1)
                stats(step, x_rows, (1.0, 1e-5),
                      between=lambda: less_mean_times(lambda i: xl[:, i, :], x_rows, rowsD["L3_ffn_gamma"][:, :]))
                step(*[stt(out=xl[:, i, :], in0=xl[:, i, :], scalar=rs[:, i:i + 1], in1=rowsD["L3_ffn_beta"][:, :],
                           op0=ALU.mult, op1=ALU.add) for i in range(NT)])
                dve.sem_inc(S("l3f_xl"), NT)
                step(*[V.tensor_tensor_reduce(out=tmp[:, i, :], in0=xl[:, i, :], in1=xl[:, i, :], scale=1.0, scalar=0.0,
                                              op0=ALU.mult, op1=ALU.add, accum_out=st[:, i:i + 1]) for i in range(NT)])
                rsqrt(step, rs[:, 0:NT], st[:, 0:NT])
                step(tt(st[:, 0:NT], st[:, 0:NT], rs[:, 0:NT], ALU.mult))
                step(ts(st[:, 0:NT], st[:, 0:NT], 1e-12, None, ALU.max))
                step(V.reciprocal(rs[:, 0:NT], st[:, 0:NT]))
                step(ts(rs[:, 0:NT], rs[:, 0:NT], sc_scale[:, 0:1], None, ALU.mult))
                dve.sem_inc(S("l3f_rs"), 1)
                for n in range(8):
                    ch, i = n // 2, n % 2
                    dve.wait_ge(S("logits_out"), n + 1)
                    V.reduce_max(rmx[:, i, ch:ch + 1], lg[:, i, ch * 512:(ch + 1) * 512], AX).then_inc(S("logits_max"), 1)
                dve.wait_ge(S("logits_max"), 8)
                step(V.tensor_reduce(ve[:, 0:NT], rmx[:, :, :], AX, ALU.max, negate=True))
                three_parts(step, [mst[:, :, s, 0] for s in range(3)], ve[:, 0:NT], nw[:, 0:NT])
                dve.sem_inc(S("row_parts"), 1)

                def slot_max(g):
                    dve.wait_ge(S("logitsT_ps"), g + 1)
                    V.reduce_max(cmx[:, 2 * g:2 * g + 2], bank[g][:, :].rearrange("p (e t) -> p e t", e=2), AX, negate=True)\
                        .then_inc(S("slots_max"), 1)

                def less_row_max(g):
                    tt(lT[:, 2 * g:2 * g + 2, :], bank[g][:, :].rearrange("p (e t) -> p e t", e=2),
                       rbc[:, :].unsqueeze(1).broadcast_to([P, 2, N]), ALU.add).then_inc(S("lT_less_max"), 1)

                for g in range(6):
                    slot_max(g)
                dve.wait_ge(S("row_max_all"), 1)
                step(V.tensor_copy(rbc[:, :], bank[7][:, 0:N]))
                dve.sem_inc(S("row_max_read"), 1)
                for g in range(4):
                    less_row_max(g)
                slot_max(6)
                slot_max(7)
                dve.wait_ge(S("slots_max"), 8)
                three_parts(step, [mst[:, 0, s, 0:SE] for s in range(3)], cmx[:, :], cmr[:, :])
                dve.sem_inc(S("slot_parts"), 1)
                for g in range(4, 8):
                    less_row_max(g)
                for ch in range(4):
                    dve.wait_ge(S("slot_max_all"), ch + 1)
                    lc = lg[:, :, ch * 512:(ch + 1) * 512]
                    tt(lc, lc, bank[4 + ch][:, :].unsqueeze(1).broadcast_to([P, NT, 512]), ALU.add).then_inc(S("logits_less_max"), 1)
                for ch in range(4):
                    dve.wait_ge(S("soft_up"), ch + 1)
                    up = bank[ch][:, 0:4 * (SH + 1)].rearrange("p (e h) -> p e h", e=4)
                    h, es = hs[:, 4 * ch:4 * ch + 4, 0:SH], slice(4 * ch, 4 * ch + 4)
                    step(V.reciprocal(cmr[:, es], up[:, :, SH]))
                    step(tt(h, up[:, :, 0:SH], cmr[:, es].unsqueeze(2).broadcast_to([P, 4, SH]), ALU.mult))
                    tt(h, h, b1[:, es, :], ALU.add).then_inc(S("soft_pre"), 1)
                for g in range(1, 8, 2):
                    dve.wait_ge(S("gathered_ps"), g + 1)
                    V.tensor_copy(aT[:, 2 * g:2 * g + 2, :], bank[4 + g % 4][0:SH + 1, :].rearrange("p (e t) -> p e t", e=2))\
                        .then_inc(S("gathered1"), 1)
                dve.wait_ge(S("soft_out"), 1)
                for i in range(NT):
                    step(V.reciprocal(st[:, i:i + 1], bank[i][:, D:D + 1]))
                    step(ts(st[:, i:i + 1], st[:, i:i + 1], gates[:, 7:8], None, ALU.mult))
                    stt(out=xs[:, bass.ts(b, NT), :][:, i, :], in0=bank[i][:, 0:D], scalar=st[:, i:i + 1], in1=x[:, i, :],
                        op0=ALU.mult, op1=ALU.add).then_inc(once("x_final"), 1)
                dve.wait_ge(once("x_final"), b * NT + NT)
                end_of_batch(dve)
                dve.wait_ge(once("batch_cleared"), b + (B + B + 1))

        @block.gpsimd
        def _(pool):
            G = nc.gpsimd
            step = Steps(pool, once("pool_step"))

            def select(t, compare, fill, base, pattern, m=1):
                step(G.affine_select(out=t, in_=t, compare_op=compare, fill=fill, base=base, pattern=pattern, channel_multiplier=m))

            step(G.memset(ident[:, :], 0.0))
            select(ident[:, :], ALU.not_equal, 1.0, 0, [[-1, P]])
            pool.sem_inc(once("consts"), 1)
            step(G.tensor_copy(identb[:, :], ident[:, :]))
            pool.sem_inc(once("consts"), 1)
            step(G.memset(ones[:, :], 1.0))
            pool.sem_inc(once("consts"), 1)
            step(G.memset(mask_q[:, :, :], 0.0))
            select(mask_q[:, :, :], ALU.is_ge, MASKED, 0, [[P, NT], [-1, N]])
            step(G.memset(mask_t[:, :, :], 0.0))
            select(mask_t[:, :, :], ALU.is_ge, MASKED, 0, [[-P, NT], [1, N]], -1)
            step(G.memset(mst[:, :, :, :], 0.0))
            step(G.memset(vst[:, :, :, :], 0.0))
            pool.sem_inc(once("consts"), 1)
            step(G.memset(w2a[:, :, D:D + 1], 0.0))
            step(G.memset(w2a[SH:SH + 1, :, D:D + 1], 1.0))
            step(G.memset(zero_w[:, :], 0.0))
            step(G.memset(picks[:, :, :], 0.0))
            for k in range(2):
                t = picks[:, 0:E // 2, :].rearrange("p q (e f) -> p q e f", e=2)
                select(t, ALU.not_equal, 1.0, -E * k, [[-2, E // 2], [-1, 2], [0, F]])
            def end_loop(arrived):
                pool.wait_ge(once("batch_arrived"), arrived)
                pool.sem_inc(once("went_on"), 1)
                clear(pool)
                pool.sem_inc(once("batch_cleared"), 1)

            with pool.Fori(0, B // 2) as b:
                step = Steps(pool, S("pool_step_b"))
                pool.wait_ge(S("xT"), 4)
                high = xh[:, :, bass.ts(b, T0 * P)]
                step(G.tensor_copy(high, xT0[:, :, :]))
                step(G.tensor_tensor(xlo[:, :, bass.ts(b, T0 * P)], xT0[:, :, :], high.bitcast(F32), ALU.subtract))
                end_loop(b * 3 + 3)
            pool.sem_inc(once("picks"), 2)
            pool.sem_inc(once("hidden_used"), 4)
            pool.sem_inc(once("up_made"), 4)
            def split(t, k, shared=False):
                pool.wait_ge(once(f"experts_loaded{k}"), t * (5 * 16) + 5 * 16)
                q, high, low = t * SLOTN + k, wh[k % 2], wl[k % 2]
                for m, cols in enumerate((slice(0, 2), slice(2, 3))):
                    if m == 0:
                        pool.wait_ge(once("up_made"), 2 * q + 2)
                    else:
                        pool.wait_ge(once("hidden_used"), 2 * q + 2)
                        if not shared:
                            pool.sem_inc(once("went_on"), 1)
                            G.tensor_copy(pick[k % 2][:, :], picks[:, q, :]).then_inc(once("pick_ready"), 1)
                        else:
                            pool.sem_inc(once("pick_ready"), 1)
                    pool.sem_inc(once("went_on"), 1)
                    G.tensor_copy(high[:, cols, :], wraw[k][:, cols, :]).then_inc(once("weights_high"), 1)
                    pool.wait_ge(once("weights_high"), 2 * q + (m + 1))
                    pool.sem_inc(once("went_on"), 1)
                    G.tensor_tensor(low[:, cols, :], wraw[k][:, cols, :], high[:, cols, :].bitcast(F32), ALU.subtract)\
                        .then_inc(once(("weights_split", "downs_split")[m]), 1)

            with pool.Fori(0, E // 2 // SLOTN) as t:
                for k in range(SLOTN):
                    split(t, k)
            for k in range(SLOTN):
                split(E // 2 // SLOTN, k, shared=True)
            pool.wait_ge(once("hidden_used"), 2 * PAIRS + 4)
            pool.sem_inc(once("prep_waits_experts"), 1)
            pool.wait_ge(once("prepared"), 1)
            pool.wait_ge(once("xs_updated"), 4)

            def values(L, v):
                H, GG, HD, causal = ATTENTIONS[L]
                KV = H // GG
                G.memset(vst[:, :, 0:KV, HD:HD + 1], 1.0).then_inc(S("att_v"), 1)
                if v is not None:
                    G.tensor_copy(vst[:, :, 0:KV, 0:HD], v.rearrange("p i (h d) -> p i h d", h=KV)).then_inc(S("att_v"), 1)
                else:
                    pool.sem_inc(S("att_v"), 1)

            def keys(step, L):
                H, GG, HD, causal = ATTENTIONS[L]
                KV = H // GG
                (h, m, l), copies = K_SLOTS
                slots = kst[:, :, 0:KV * 6 * HD].rearrange("p i (h s d) -> p s i h d", h=KV, s=6)
                v = c.rearrange("p i (h d) -> p i h d", h=KV)
                left = kf[:, :, 0:CD].rearrange("p i (h d) -> p i h d", h=KV)
                step(G.tensor_copy(slots[:, h], v))
                step(G.tensor_tensor(left, v, slots[:, h], ALU.subtract))
                step(G.tensor_copy(slots[:, m], left))
                step(G.tensor_tensor(slots[:, l], left, slots[:, m], ALU.subtract),
                     *[G.tensor_copy(slots[:, to], slots[:, fro]) for to, fro in copies])
                pool.sem_inc(S("att_k_parts"), 1)

            with pool.Fori(0, B) as b:
                step = Steps(pool, S("pool_step_b"))
                G.tensor_copy(c[:, :, :], ctxs[:, bass.ts(b, NT), :]).then_inc(S("c_ready"), 1)
                pool.wait_ge(S("c_ready"), 1)
                keys(step, "l1x")
                values("l1x", c[:, :, :])
                pool.wait_ge(S("l1f_in"), 2)
                values("l1f", None)
                end_loop(b * 3 + (3 * B // 2 + 3))
            with pool.Fori(0, B // 2) as b:
                end_loop(b * 3 + (3 * B // 2 + 3 * B + 3))
            with pool.Fori(0, B) as b:
                step = Steps(pool, S("pool_step_b"))
                G.tensor_copy(c[:, :, :], ctxs[:, bass.ts(b, NT), :]).then_inc(S("c_ready"), 1)
                pool.wait_ge(S("c_ready"), 1)
                keys(step, "l3x")
                values("l3x", c[:, :, :])
                pool.wait_ge(S("l3f_begun"), 1)
                G.memset(xw[:, :, :, SH:SH + 1], 1.0).then_inc(S("ones_columns"), 1)
                G.memset(hs[:, :, SH:SH + 1], 1.0).then_inc(S("ones_columns"), 1)
                end_loop(b * 3 + (3 * B // 2 + 3 * B + 3 * B // 2 + 3))


_INS = ['x', 'ctx_512', 'g_xattn', 'g_ffn', 'L0_xattn_W_k', 'L0_xattn_b_k', 'L0_xattn_ln_gamma', 'L0_xattn_ln_beta',
        'L0_ffn_router_w', 'L0_ffn_router_bias', 'L0_ffn_wg', 'L0_ffn_wu', 'L0_ffn_wd', 'L0_ffn_swg', 'L0_ffn_swu',
        'L0_ffn_swd', 'L1_ffn_ln1_w', 'L1_ffn_ln2_w', 'L1_ffn_Wq', 'L1_ffn_Wk', 'L1_ffn_Wv', 'L1_ffn_Wo', 'L1_ffn_A',
        'L1_ffn_B', 'L1_ffn_W_in_base', 'L1_ffn_W_up_base', 'L1_ffn_W_down', 'L2_xattn_W', 'L2_xattn_b', 'L2_ffn_w1',
        'L2_ffn_b1', 'L2_ffn_ln_g', 'L2_ffn_ln_b', 'L2_ffn_w2', 'L2_ffn_b2', 'L3_xattn_Wc', 'L3_xattn_bc',
        'L3_ffn_gamma', 'L3_ffn_beta', 'L3_ffn_mu', 'L3_ffn_scale', 'L3_ffn_W1', 'L3_ffn_b1', 'L3_ffn_W2', 'L3_ffn_b2']


def kernel(**inputs):
    import numpy as _np
    import concourse.bacc as _bacc
    from concourse import mybir as _mybir
    from concourse.bass_utils import run_bass_kernel_spmd as _run

    nc = _bacc.Bacc("TRN2", target_bir_lowering=False, num_devices=1)
    arrays, args = {}, {}
    for name in _INS:
        a = _np.ascontiguousarray(inputs[name])
        arrays[f"in_{name}_dram"] = a
        args[name] = nc.dram_tensor(f"in_{name}_dram", a.shape, _mybir.dt.from_np(a.dtype), kind="ExternalInput").ap()
    out = nc.dram_tensor("out_0_dram", (B, N, D), _mybir.dt.float32, kind="ExternalOutput").ap()
    flamingo(nc, args, out)
    r = _run(nc, [arrays], core_ids=[0])
    return r.results[0]["out_0_dram"]
```
